# Optimizing a Trainium2 kernel written in Bass

```python
import numpy as np
import jax
import jax.numpy as jnp

def _softmax(x, axis=-1):
    return jax.nn.softmax(x, axis=axis)

def _gelu(x):
    return jax.nn.gelu(x, approximate=True)

def _silu(x):
    return jax.nn.silu(x)

def _sigmoid(x):
    return jax.nn.sigmoid(x)

def _layernorm(x, axis=-1, eps=1e-05):
    m = jnp.mean(x, axis=axis, keepdims=True)
    v = jnp.var(x, axis=axis, keepdims=True)
    return (x - m) / jnp.sqrt(v + eps)

def _scatter_add(tgt, idx, src, axis=0):
    return tgt.at[idx].add(src)

def _segment_sum(src, seg, n):
    return jax.ops.segment_sum(src, seg, n)
kernel_name = 'mk_conv_attn_hybrid_d2_conv_nchw128_r2_43427f'

def setup_inputs(seed: int=0):
    np.random.seed(seed)
    _w = jnp.asarray

    def _rec_inputs():
        import jax
        import jax.numpy as jnp
        _gk = jax.random.key(seed)
        x = -0.0005207 + 1.001 * jax.random.normal(jax.random.fold_in(_gk, 1), (16, 64, 32, 32), jnp.float32)
        return x
    x = _rec_inputs()

    def _L0_conv_setup():
        import jax, jax.numpy as jnp
        import numpy as np
        B, FEAT, H, W = (16, 32, 32, 32)

        def _shift_right_w(a):
            return jnp.pad(a, ((0, 0), (0, 0), (0, 0), (1, 0)))[:, :, :, :-1]

        def _shift_left_w(a):
            return jnp.pad(a, ((0, 0), (0, 0), (0, 0), (0, 1)))[:, :, :, 1:]

        def _shift_down_h(a):
            return jnp.pad(a, ((0, 0), (0, 0), (1, 0), (0, 0)))[:, :, :-1, :]

        def _s2s(hprev, w, b, wshift):
            hw = wshift(hprev)
            hd = _shift_down_h(hw)
            return jnp.einsum('bchw,oc->bohw', hd, w[:, :, 0]) + jnp.einsum('bchw,oc->bohw', hw, w[:, :, 1]) + b[None, :, None, None]

        def _forward(x, w_i2s, w_left, b_left, w_right, b_right, w_skip, b_skip):
            b_, c2, h_, w_ = x.shape
            f = c2 // 2
            hmap = jnp.einsum('bchw,oc->bohw', x, w_i2s)
            left_h = hmap
            right_h = hmap
            zeros = jnp.zeros((b_, f, h_, w_), x.dtype)

            def step(carry, _):
                lc, lh, rc, rh = carry
                pre = jax.nn.sigmoid(_s2s(lh, w_left, b_left, _shift_right_w) + left_h)
                o, fg, ig, g = jnp.split(pre, 4, axis=1)
                lc = fg * lc + ig * g
                lh = o * jnp.tanh(lc)
                pre = jax.nn.sigmoid(_s2s(rh, w_right, b_right, _shift_left_w) + right_h)
                o, fg, ig, g = jnp.split(pre, 4, axis=1)
                rc = fg * rc + ig * g
                rh = o * jnp.tanh(rc)
                return ((lc, lh, rc, rh), None)
            (lc, lh, rc, rh), _ = jax.lax.scan(step, (zeros, zeros, zeros, zeros), None, length=h_)
            rh = _shift_down_h(rh)
            out_h = lh + rh
            skip = jnp.einsum('bchw,oc->bohw', out_h, w_skip) + b_skip[None, :, None, None]
            return x + skip
        key = jax.random.key(seed)
        ks = jax.random.split(key, 8)
        s = 0.05
        return {'x': jax.random.normal(ks[0], (B, 2 * FEAT, H, W), jnp.float32), 'w_i2s': jax.random.normal(ks[1], (4 * FEAT, 2 * FEAT), jnp.float32) * s, 'w_left': jax.random.normal(ks[2], (4 * FEAT, FEAT, 2), jnp.float32) * s, 'b_left': jax.random.normal(ks[3], (4 * FEAT,), jnp.float32) * s, 'w_right': jax.random.normal(ks[4], (4 * FEAT, FEAT, 2), jnp.float32) * s, 'b_right': jax.random.normal(ks[5], (4 * FEAT,), jnp.float32) * s, 'w_skip': jax.random.normal(ks[6], (2 * FEAT, FEAT), jnp.float32) * s, 'b_skip': jax.random.normal(ks[7], (2 * FEAT,), jnp.float32) * s}
    _L0_conv_all = _L0_conv_setup()
    _L0_conv_in = {k: v for k, v in _L0_conv_all.items() if k in ('w_i2s', 'w_left', 'b_left', 'w_right', 'b_right', 'w_skip', 'b_skip')}
    del _L0_conv_all

    def _L1_attn_setup():
        import jax, jax.numpy as jnp
        import numpy as np
        BATCH, LENGTH = (4, 256)
        D_MODEL, D_STATE, EXPAND = (64, 128, 2)
        D_INNER = EXPAND * D_MODEL
        key = jax.random.key(seed)
        ks = jax.random.split(key, 8)
        x = jax.random.normal(ks[0], (BATCH, LENGTH, D_MODEL), jnp.float32)
        W_in = jax.random.normal(ks[1], (D_MODEL, 2 * D_INNER), jnp.float32) / np.float32(np.sqrt(D_MODEL))
        W_delta = jax.random.normal(ks[2], (D_INNER, D_INNER), jnp.float32) * np.float32(0.005)
        W_B = jax.random.normal(ks[3], (D_INNER, D_STATE), jnp.float32) / np.float32(np.sqrt(D_INNER))
        W_C = jax.random.normal(ks[4], (D_INNER, D_INNER), jnp.float32) / np.float32(np.sqrt(D_INNER))
        W_out = jax.random.normal(ks[5], (D_INNER, D_MODEL), jnp.float32) / np.float32(np.sqrt(D_INNER))
        A = jax.random.normal(ks[6], (D_INNER, D_STATE), jnp.float32) * np.float32(0.02)
        D = jnp.ones((D_INNER,), jnp.float32)
        return dict(x=x, W_in=W_in, W_delta=W_delta, W_B=W_B, W_C=W_C, W_out=W_out, A=A, D=D)
    _L1_attn_all = _L1_attn_setup()
    _L1_attn_in = {k: v for k, v in _L1_attn_all.items() if k in ('W_in', 'W_delta', 'W_B', 'W_C', 'W_out', 'A', 'D')}
    del _L1_attn_all

    def _L1_ffn_setup():
        import jax, jax.numpy as jnp
        import numpy as np
        B, S, D, E, H, O, K = (256, 1024, 64, 32, 256, 64, 8)
        key = jax.random.key(seed)
        k0, k1, k2, k3 = jax.random.split(key, 4)
        x = jax.random.normal(k0, (B, S, D), dtype=jnp.float32)
        gate_w = jax.random.normal(k1, (E, D), dtype=jnp.float32) * (1.0 / np.sqrt(D))
        gate_b = jnp.zeros((E,), dtype=jnp.float32)
        weight1 = jax.random.uniform(k2, (E, D + 1, H), dtype=jnp.float32, minval=-1.0, maxval=1.0) * (1.0 / np.sqrt(D + 1))
        weight2 = jax.random.uniform(k3, (E, H + 1, O), dtype=jnp.float32, minval=-1.0, maxval=1.0) * (1.0 / np.sqrt(H + 1))
        return {'x': x, 'gate_w': gate_w, 'gate_b': gate_b, 'weight1': weight1, 'weight2': weight2}
    _L1_ffn_all = _L1_ffn_setup()
    _L1_ffn_in = {k: v for k, v in _L1_ffn_all.items() if k in ('gate_w', 'gate_b', 'weight1', 'weight2')}
    del _L1_ffn_all
    return {'x': x, 'L0_conv_w_i2s': _L0_conv_in['w_i2s'], 'L0_conv_w_left': _L0_conv_in['w_left'], 'L0_conv_b_left': _L0_conv_in['b_left'], 'L0_conv_w_right': _L0_conv_in['w_right'], 'L0_conv_b_right': _L0_conv_in['b_right'], 'L0_conv_w_skip': _L0_conv_in['w_skip'], 'L0_conv_b_skip': _L0_conv_in['b_skip'], 'L1_attn_W_in': _L1_attn_in['W_in'], 'L1_attn_W_delta': _L1_attn_in['W_delta'], 'L1_attn_W_B': _L1_attn_in['W_B'], 'L1_attn_W_C': _L1_attn_in['W_C'], 'L1_attn_W_out': _L1_attn_in['W_out'], 'L1_attn_A': _L1_attn_in['A'], 'L1_attn_D': _L1_attn_in['D'], 'L1_ffn_gate_w': _L1_ffn_in['gate_w'], 'L1_ffn_gate_b': _L1_ffn_in['gate_b'], 'L1_ffn_weight1': _L1_ffn_in['weight1'], 'L1_ffn_weight2': _L1_ffn_in['weight2']}

def reference(x, L0_conv_w_i2s, L0_conv_w_left, L0_conv_b_left, L0_conv_w_right, L0_conv_b_right, L0_conv_w_skip, L0_conv_b_skip, L1_attn_W_in, L1_attn_W_delta, L1_attn_W_B, L1_attn_W_C, L1_attn_W_out, L1_attn_A, L1_attn_D, L1_ffn_gate_w, L1_ffn_gate_b, L1_ffn_weight1, L1_ffn_weight2):
    import jax
    import jax.numpy as jnp

    def _L0_conv_ref(x, w_i2s, w_left, b_left, w_right, b_right, w_skip, b_skip):
        import jax, jax.numpy as jnp
        import numpy as np
        B, FEAT, H, W = (16, 32, 32, 32)

        def _shift_right_w(a):
            return jnp.pad(a, ((0, 0), (0, 0), (0, 0), (1, 0)))[:, :, :, :-1]

        def _shift_left_w(a):
            return jnp.pad(a, ((0, 0), (0, 0), (0, 0), (0, 1)))[:, :, :, 1:]

        def _shift_down_h(a):
            return jnp.pad(a, ((0, 0), (0, 0), (1, 0), (0, 0)))[:, :, :-1, :]

        def _s2s(hprev, w, b, wshift):
            hw = wshift(hprev)
            hd = _shift_down_h(hw)
            return jnp.einsum('bchw,oc->bohw', hd, w[:, :, 0]) + jnp.einsum('bchw,oc->bohw', hw, w[:, :, 1]) + b[None, :, None, None]

        def _forward(x, w_i2s, w_left, b_left, w_right, b_right, w_skip, b_skip):
            b_, c2, h_, w_ = x.shape
            f = c2 // 2
            hmap = jnp.einsum('bchw,oc->bohw', x, w_i2s)
            left_h = hmap
            right_h = hmap
            zeros = jnp.zeros((b_, f, h_, w_), x.dtype)

            def step(carry, _):
                lc, lh, rc, rh = carry
                pre = jax.nn.sigmoid(_s2s(lh, w_left, b_left, _shift_right_w) + left_h)
                o, fg, ig, g = jnp.split(pre, 4, axis=1)
                lc = fg * lc + ig * g
                lh = o * jnp.tanh(lc)
                pre = jax.nn.sigmoid(_s2s(rh, w_right, b_right, _shift_left_w) + right_h)
                o, fg, ig, g = jnp.split(pre, 4, axis=1)
                rc = fg * rc + ig * g
                rh = o * jnp.tanh(rc)
                return ((lc, lh, rc, rh), None)
            (lc, lh, rc, rh), _ = jax.lax.scan(step, (zeros, zeros, zeros, zeros), None, length=h_)
            rh = _shift_down_h(rh)
            out_h = lh + rh
            skip = jnp.einsum('bchw,oc->bohw', out_h, w_skip) + b_skip[None, :, None, None]
            return x + skip
        return _forward(x, w_i2s, w_left, b_left, w_right, b_right, w_skip, b_skip)

    def _L1_attn_ref(x, W_in, W_delta, W_B, W_C, W_out, A, D):
        import jax, jax.numpy as jnp
        import numpy as np
        BATCH, LENGTH = (4, 256)
        D_MODEL, D_STATE, EXPAND = (64, 128, 2)
        D_INNER = EXPAND * D_MODEL
        x_proj = x @ W_in
        xs, z = jnp.split(x_proj, 2, axis=-1)
        delta = xs @ W_delta
        Bv = xs @ W_B
        Cv = xs @ W_C
        deltaA = jnp.exp(jnp.einsum('bld,dn->bldn', delta, A))
        deltaB = jnp.einsum('bld,bln->bldn', delta, Bv)

        def step(state, inp):
            dA_i, dB_i, x_i, C_i = inp
            state = dA_i * state + dB_i * x_i[:, None, :]
            y = jnp.einsum('bdn,bn->bd', state, C_i)
            return (state, y)
        init = jnp.zeros((x.shape[0], D_INNER, D_STATE), xs.dtype)
        inps = (jnp.moveaxis(deltaA, 1, 0), jnp.moveaxis(deltaB, 1, 0), jnp.moveaxis(xs, 1, 0), jnp.moveaxis(Cv, 1, 0))
        _, ys = jax.lax.scan(step, init, inps)
        y = jnp.moveaxis(ys, 0, 1)
        y = y * jax.nn.silu(z)
        return y @ W_out

    def _L1_ffn_ref(x, gate_w, gate_b, weight1, weight2):
        import jax, jax.numpy as jnp
        import numpy as np
        B, S, D, E, H, O, K = (256, 1024, 64, 32, 256, 64, 8)
        Bn, Sn, Dn = x.shape
        logits = jnp.einsum('bsd,ed->bse', x, gate_w) + gate_b
        probs = jax.nn.softmax(logits, axis=1)
        vals, idx = jax.lax.top_k(probs.transpose(0, 2, 1), K)
        topv = vals.transpose(0, 2, 1)
        topi = idx.transpose(0, 2, 1)
        flat_idx = topi.reshape(Bn, K * E)
        gathered = jnp.take_along_axis(x, flat_idx[:, :, None], axis=1)
        gathered = gathered.reshape(Bn, K, E, Dn)
        pooled = jnp.einsum('bked,bke->bed', gathered, topv)
        ones = jnp.ones((E, Bn, 1), dtype=x.dtype)
        h = jnp.concatenate([pooled.transpose(1, 0, 2), ones], axis=-1)
        h = jax.nn.gelu(jnp.einsum('ebd,edh->ebh', h, weight1), approximate=False)
        h = jnp.concatenate([h, ones], axis=-1)
        out = jnp.einsum('ebh,eho->ebo', h, weight2)
        out = out.transpose(1, 0, 2)
        weighted = jnp.einsum('beo,bke->bkeo', out, topv).reshape(Bn, K * E, O)
        outputs = jnp.zeros((Bn, Sn, O), dtype=x.dtype)
        outputs = outputs.at[jnp.arange(Bn)[:, None], flat_idx].add(weighted)
        return outputs

    def _gn(v, G=32, eps=1e-05):
        B_, C_, H_, W_ = v.shape
        g = v.reshape(B_, G, C_ // G, H_, W_)
        m = jnp.mean(g, axis=(2, 3, 4), keepdims=True)
        s = jnp.var(g, axis=(2, 3, 4), keepdims=True)
        return ((g - m) / jnp.sqrt(s + eps)).reshape(v.shape)

    def _ln_c(v, eps=1e-06):
        m = jnp.mean(v, axis=1, keepdims=True)
        s = jnp.var(v, axis=1, keepdims=True)
        return (v - m) / jnp.sqrt(s + eps)

    def _ln_t(v, eps=1e-05):
        m = jnp.mean(v, axis=-1, keepdims=True)
        s = jnp.var(v, axis=-1, keepdims=True)
        return (v - m) / jnp.sqrt(s + eps)

    def _to_tokens(v):
        B_, C_, H_, W_ = v.shape
        return v.reshape(B_, C_, H_ * W_).transpose(0, 2, 1)

    def _from_tokens(t, like):
        B_, C_, H_, W_ = like.shape
        return t.transpose(0, 2, 1).reshape(B_, C_, H_, W_)
    x = _L0_conv_ref(x, L0_conv_w_i2s, L0_conv_w_left, L0_conv_b_left, L0_conv_w_right, L0_conv_b_right, L0_conv_w_skip, L0_conv_b_skip)
    t = _to_tokens(x)
    t = t + _L1_attn_ref(_ln_t(t), L1_attn_W_in, L1_attn_W_delta, L1_attn_W_B, L1_attn_W_C, L1_attn_W_out, L1_attn_A, L1_attn_D)
    t = t + _L1_ffn_ref(_ln_t(t), L1_ffn_gate_w, L1_ffn_gate_b, L1_ffn_weight1, L1_ffn_weight2)
    x = _from_tokens(t, x)
    return x

_drawn_inputs = setup_inputs


def setup_inputs(seed=0):
    import zlib

    import numpy as np

    out = dict(_drawn_inputs(seed))
    spreads = {'L1_attn_D': (1.0, 0.2), 'L1_ffn_gate_b': (0.0, 0.1)}
    factors = {'L0_conv_b_left': 4.25,
     'L0_conv_b_right': 4.522,
     'L1_ffn_gate_w': 8.0,
     'L1_ffn_weight1': 8.0,
     'L1_ffn_weight2': 8.0}
    for name, (base, spread) in spreads.items():
        noise = np.random.default_rng([zlib.crc32(name.encode()), seed]).standard_normal(out[name].shape)
        drawn = base * np.exp(spread * noise) if base else spread * noise
        out[name] = jnp.asarray(drawn.astype(out[name].dtype))
    for name, factor in factors.items():
        out[name] = (out[name] * factor).astype(out[name].dtype)
    return out
```

```python
from contextlib import ExitStack

import concourse.bass as bass
from concourse import mybir

F32 = mybir.dt.float32
BF16 = mybir.dt.bfloat16
ALU = mybir.AluOpType
ACT = mybir.ActivationFunctionType
AX = mybir.AxisListType

BATCH = 16
CH = 64
SIDE = 32
LEN = SIDE * SIDE
FEAT = CH // 2
STEPS = SIDE
INNER = 128
STATE = 128
EXPERTS = 32
TOPK = 8
HIDDEN = 256
BANK = 512
DMA = 16
START = 1

GROUP = 4
PITCH = SIDE + 1
IMG = SIDE * PITCH
MARGIN = 2
RW = MARGIN + IMG + 2
STREAMS = 4
ROUNDS = BATCH // (2 * GROUP)
CHUNKS = LEN // BANK
CROWS = BANK // SIDE
CIMG = CROWS * PITCH


class Semaphores:

    def __init__(self, nc, ctx, phase):
        self.nc, self.ctx, self.phase, self.made = nc, ctx, phase, []

    def __call__(self, name):
        self.made.append(self.ctx.enter_context(self.nc.semaphore(f"{self.phase}_{name}")))
        return self.made[-1]


def conv_phase(nc, x_pad, w_left, w_right, bias_left, bias_right, w_skip_left, w_skip_right, b_skip, x1_dram):
    with ExitStack() as ctx:
        def sb(name, shape, dt=F32):
            return ctx.enter_context(nc.sbuf_tensor(name, shape, dt))

        sem = Semaphores(nc, ctx, "conv")
        rows = [sb(f"rows{s}", [128, GROUP, RW]) for s in range(STREAMS)]
        feat = [sb(f"feat{s}", [128, IMG]) for s in range(STREAMS)]
        cell = [sb(f"cell{s}", [128, LEN]) for s in range(STREAMS)]
        gates = [sb(f"gates{c}", [128, 4, BANK]) for c in range(CHUNKS)]
        forgot = [sb(f"forgot{c}", [128, BANK]) for c in range(CHUNKS)]
        entered = [sb(f"entered{c}", [128, BANK]) for c in range(CHUNKS)]
        squashed = [sb(f"squashed{c}", [128, BANK]) for c in range(CHUNKS)]
        weights = [sb("weights_left", [128, 128]), sb("weights_right", [128, 128])]
        biases = [sb("biases_left", [128, 4]), sb("biases_right", [128, 4])]
        skip_w = [sb("skip_w_left", [128, CH]), sb("skip_w_right", [128, CH])]
        skip_b = sb("skip_b", [128, 1])
        x1 = [sb(f"x1_{i}", [128, BANK]) for i in range(2)]
        pre = [ctx.enter_context(nc.psum_tensor(f"pre{c}", [128, 4, BANK], F32)) for c in range(CHUNKS)]

        weights_in, x_in, zeroed, state_zeroed = sem("weights_in"), sem("x_in"), sem("zeroed"), sem("state_zeroed")
        pre_ready, gates_ready, forgot_ready, entered_ready = (
            sem("pre_ready"), sem("gates_ready"), sem("forgot_ready"), sem("entered_ready"))
        cell_ready, squashed_ready, feat_ready = sem("cell_ready"), sem("squashed_ready"), sem("feat_ready")
        rows_in = [sem(f"rows_in{s}") for s in range(STREAMS)]
        skip_ready, x1_ready = sem("skip_ready"), sem("x1_ready")
        x1_out = [sem(f"x1_out{i}") for i in range(2)]
        passed = sem("passed")
        block = ctx.enter_context(nc.Block())

        def side(s):
            return s // 2

        def half(s):
            return s % 2

        SLOTS = STREAMS * CHUNKS
        SKIPS = 2 * GROUP * CHUNKS

        def image(tile, at):
            return tile[..., at:at + CIMG].rearrange("p (h w) -> p h w", w=PITCH)[:, :, 0:SIDE]

        above = [(PITCH + 1, IMG - PITCH - 1), (PITCH - 1, IMG - PITCH + 1)]
        same = [(1, IMG), (-1, IMG)]
        MOVES = 2 * GROUP

        @block.sync
        def _(sp):
            for s in sem.made:
                sp.sem_inc(s, START)
            for d, s in ((weights[0], w_left), (weights[1], w_right), (biases[0], bias_left),
                         (biases[1], bias_right), (skip_w[0], w_skip_left), (skip_w[1], w_skip_right)):
                sp.dma_start(d[:, :], s).then_inc(weights_in, DMA)
            sp.dma_start(skip_b[CH:128, :], b_skip).then_inc(weights_in, DMA)
            sp.wait_ge(zeroed, START + 1)
            with sp.Fori(0, ROUNDS) as r:
                sp.wait_ge(x1_ready, START + r * SKIPS)
                for s in range(STREAMS):
                    src = x_pad[bass.ds((r * 2 + half(s)) * GROUP, GROUP), :, :].rearrange("q c p -> c q p")
                    sp.dma_start(rows[s][CH:128, :, MARGIN:MARGIN + IMG], src).then_inc(x_in, DMA)
                with sp.Fori(0, STEPS) as t:
                    for s in range(STREAMS):
                        sp.wait_ge(feat_ready, START + (r * STEPS + t) * SLOTS + CHUNKS * (s + 1))
                        for q in range(GROUP):
                            for part, (to, n) in ((0, above[side(s)]), (1, same[side(s)])):
                                sp.dma_start(rows[s][32 * part:32 * part + 32, q, MARGIN + to:MARGIN + to + n],
                                             feat[s][32 * q:32 * q + 32, 0:n]).then_inc(rows_in[s], DMA)
                for k in range(SKIPS):
                    h, q, c = k // (GROUP * CHUNKS), k // CHUNKS % GROUP, k % CHUNKS
                    sp.wait_ge(x1_ready, START + r * SKIPS + k + 1)
                    dst = x1_dram[bass.ds((r * 2 + h) * GROUP + q, 1), :, BANK * c:BANK * c + BANK]
                    sp.dma_start(dst.rearrange("b c l -> (b c) l"), x1[k % 2][CH:128, :]).then_inc(x1_out[k % 2], DMA)
            for i in range(2):
                sp.wait_ge(x1_out[i], START + ROUNDS * SKIPS // 2 * DMA)

        @block.tensor
        def _(pe):
            pe.wait_ge(weights_in, START + 7 * DMA)
            with pe.Fori(0, ROUNDS) as r:
                pe.wait_ge(x_in, START + (r + 1) * STREAMS * DMA)
                pe.wait_ge(state_zeroed, START + r + 1)
                pe.sem_inc(passed, 1)
                with pe.Fori(0, STEPS) as t:
                    for s in range(STREAMS):
                        pe.wait_ge(rows_in[s], START + (r * STEPS + t) * MOVES * DMA)
                        for c in range(CHUNKS):
                            k = s * CHUNKS + c
                            if k >= CHUNKS:
                                pe.wait_ge(gates_ready, START + (r * STEPS + t) * SLOTS + k - CHUNKS + 1)
                            else:
                                pe.wait_ge(gates_ready, START + (r * STEPS + t) * SLOTS)
                            for g in range(4):
                                for q in range(GROUP):
                                    mm = pe.matmul(pre[c][32 * q:32 * q + 32, g, :],
                                                   weights[side(s)][:, 32 * g:32 * g + 32],
                                                   image(rows[s][:, q, :], MARGIN + CIMG * c),
                                                   start=True, stop=True)
                            mm.then_inc(pre_ready, 1)
                for s in range(STREAMS):
                    pe.wait_ge(rows_in[s], START + (r + 1) * STEPS * MOVES * DMA)
                for k in range(SKIPS):
                    h, q, c = k // (GROUP * CHUNKS), k // CHUNKS % GROUP, k % CHUNKS
                    if k >= 4:
                        pe.wait_ge(x1_ready, START + r * SKIPS + k - 3)
                    out = pre[k // 2 % 2][CH:128, k % 2, :]
                    pe.matmul(out, skip_w[0][:, :], image(rows[h][:, q, :], MARGIN + 1 + CIMG * c),
                              start=True, stop=False)
                    pe.matmul(out, skip_w[1][:, :], image(rows[2 + h][:, q, :], MARGIN - 1 + CIMG * c),
                              start=False, stop=True).then_inc(skip_ready, 1)

        @block.scalar
        def _(act):
            act.wait_ge(weights_in, START + 7 * DMA)
            with act.Fori(0, ROUNDS * STEPS) as t:
                def gate_values(k):
                    c = k % CHUNKS
                    act.wait_ge(pre_ready, START + t * SLOTS + k + 1)
                    if k >= CHUNKS:
                        act.wait_ge(feat_ready, START + t * SLOTS + k - CHUNKS + 1)
                    else:
                        act.wait_ge(feat_ready, START + t * SLOTS)
                    for g in range(4):
                        a = act.activation(gates[c][:, g, :], pre[c][:, g, :], ACT.Sigmoid,
                                           bias=biases[side(k // CHUNKS)][:, g:g + 1])
                    a.then_inc(gates_ready, 1)

                def squash(k):
                    c, s = k % CHUNKS, k // CHUNKS
                    act.wait_ge(cell_ready, START + t * SLOTS + k + 1)
                    act.activation(squashed[c][:, :], cell[s][:, BANK * c:BANK * c + BANK],
                                   ACT.Tanh).then_inc(squashed_ready, 1)

                gate_values(0)
                for k in range(SLOTS):
                    if k + 1 < SLOTS:
                        gate_values(k + 1)
                    squash(k)

        @block.gpsimd
        def _(pool):
            for s in range(STREAMS):
                z = pool.memset(rows[s][:, :, :], 0.0)
                z = pool.memset(feat[s][:, :], 0.0)
            z.then_inc(zeroed, 1)
            pool.wait_ge(zeroed, START + 1)
            with pool.Fori(0, ROUNDS) as r:
                pool.wait_ge(x1_ready, START + r * SKIPS)
                pool.sem_inc(passed, 1)
                for s in range(STREAMS):
                    pool.memset(rows[s][0:CH, :, :], 0.0)
                    z = pool.memset(cell[s][:, :], 0.0)
                z.then_inc(state_zeroed, 1)
                with pool.Fori(0, STEPS) as t:
                    for k in range(SLOTS):
                        c = k % CHUNKS
                        pool.wait_ge(gates_ready, START + (r * STEPS + t) * SLOTS + k + 1)
                        if k >= CHUNKS:
                            pool.wait_ge(cell_ready, START + (r * STEPS + t) * SLOTS + k - CHUNKS + 1)
                        else:
                            pool.wait_ge(cell_ready, START + (r * STEPS + t) * SLOTS)
                        pool.tensor_tensor(entered[c][:, :], gates[c][:, 2, :], gates[c][:, 3, :],
                                           ALU.mult).then_inc(entered_ready, 1)

        @block.vector
        def _(dve):
            dve.wait_ge(zeroed, START + 1)
            dve.wait_ge(weights_in, START + 7 * DMA)
            with dve.Fori(0, ROUNDS) as r:
                dve.wait_ge(state_zeroed, START + r + 1)
                dve.sem_inc(passed, 1)
                with dve.Fori(0, STEPS) as t:
                    def new_cell(k):
                        c, s = k % CHUNKS, k // CHUNKS
                        now = cell[s][:, BANK * c:BANK * c + BANK]
                        at = (r * STEPS + t) * SLOTS + k + 1
                        dve.wait_ge(gates_ready, START + at)
                        dve.tensor_tensor(forgot[c][:, :], gates[c][:, 1, :], now, ALU.mult).then_inc(forgot_ready, 1)
                        dve.wait_ge(entered_ready, START + at)
                        dve.wait_ge(forgot_ready, START + at)
                        dve.tensor_tensor(now, forgot[c][:, :], entered[c][:, :], ALU.add).then_inc(cell_ready, 1)

                    def new_features(k):
                        c, s = k % CHUNKS, k // CHUNKS
                        at = (r * STEPS + t) * SLOTS + k + 1
                        dve.wait_ge(squashed_ready, START + at)
                        dve.wait_ge(rows_in[s], START + (r * STEPS + t) * MOVES * DMA)
                        dve.tensor_tensor(image(feat[s][:, :], CIMG * c), gates[c][:, 0, :].rearrange(
                            "p (h w) -> p h w", w=SIDE), squashed[c][:, :].rearrange("p (h w) -> p h w", w=SIDE),
                            ALU.mult).then_inc(feat_ready, 1)

                    new_cell(0)
                    for k in range(SLOTS):
                        if k + 1 < SLOTS:
                            new_cell(k + 1)
                        new_features(k)
                for k in range(SKIPS):
                    h, q, c = k // (GROUP * CHUNKS), k // CHUNKS % GROUP, k % CHUNKS
                    dve.wait_ge(skip_ready, START + r * SKIPS + k + 1)
                    if k >= 2:
                        dve.wait_ge(x1_out[k % 2], START + (r * (SKIPS // 2) + k // 2) * DMA)
                    else:
                        dve.wait_ge(x1_out[k % 2], START + r * (SKIPS // 2) * DMA)
                    dve.scalar_tensor_tensor(
                        out=x1[k % 2][CH:128, :].rearrange("p (h w) -> p h w", w=SIDE),
                        in0=pre[k // 2 % 2][CH:128, k % 2, :].rearrange("p (h w) -> p h w", w=SIDE),
                        scalar=skip_b[CH:128, :],
                        in1=image(rows[h][CH:128, q, :], MARGIN + CIMG * c),
                        op0=ALU.add, op1=ALU.add).then_inc(x1_ready, 1)


SPLITS = 3
PAIRS = BATCH * CHUNKS


def project_phase(nc, x1_dram, w_in, w_delta, w_b, w_c, mean_w, delta_dram, input_dram, readout_dram, z_dram):
    with ExitStack() as ctx:
        def sb(name, shape, dt=F32):
            return ctx.enter_context(nc.sbuf_tensor(name, shape, dt))

        sem = Semaphores(nc, ctx, "proj")
        win, wdelta, wb, wc, wmean = (sb("win", [CH, 2 * INNER]), sb("wdelta", [INNER, INNER]),
                                      sb("wb", [INNER, STATE]), sb("wc", [INNER, INNER]), sb("wmean", [CH, CH]))
        eps = sb("eps", [CH, 1])
        x = [sb(f"px{c}", [CH, BANK]) for c in range(2)]
        centred = [sb(f"centred{c}", [CH, BANK]) for c in range(2)]
        square = [sb(f"square{c}", [CH, BANK]) for c in range(2)]
        std = [sb(f"std{c}", [CH, BANK]) for c in range(2)]
        normed = [sb(f"normed{c}", [CH, BANK]) for c in range(2)]
        xs = [sb(f"xs{c}", [INNER, BANK]) for c in range(2)]
        z = [sb(f"z{c}", [INNER, BANK]) for c in range(2)]
        readout = [sb(f"readout{c}", [INNER, BANK]) for c in range(2)]
        inputs = [sb(f"inputs{c}", [INNER, BANK]) for c in range(2)]
        parts = [sb(f"parts{c}", [INNER, SPLITS, BANK], BF16) for c in range(2)]
        rest = [sb(f"rest{c}", [INNER, BANK]) for c in range(2)]

        def ps(name, rows):
            return ctx.enter_context(nc.psum_tensor(name, [rows, BANK], F32))

        mean_ps, var_ps = ps("mean_ps", CH), ps("var_ps", CH)
        xs_ps, z_ps, delta_ps, b_ps, c_ps = (ps(n, INNER) for n in ("xs_ps", "z_ps", "delta_ps", "b_ps", "c_ps"))

        weights_in, eps_set = sem("weights_in"), sem("eps_set")
        x_in = [sem(f"x_in{c}") for c in range(2)]
        stored = [sem(f"stored{c}") for c in range(2)]
        mean_ready, centred_ready, square_ready, var_ready, std_ready = (
            sem("mean"), sem("centred"), sem("square"), sem("var"), sem("std"))
        inverse_ready, normed_ready = sem("inverse"), sem("normed")
        in_ready, xs_ready, z_ready = sem("in_ready"), sem("xs_ready"), sem("z_ready")
        out_ready, part1_ready, rest1_ready, part2_ready, part3_ready = (
            sem("out_ready"), sem("part1"), sem("rest1"), sem("part2"), sem("part3"))
        readout_ready, input_ready = sem("readout"), sem("input")
        STORES = 4
        passed = sem("passed")
        block = ctx.enter_context(nc.Block())

        @block.sync
        def _(sp):
            for s in sem.made:
                sp.sem_inc(s, START)
            for d, s in ((win, w_in), (wdelta, w_delta), (wb, w_b), (wc, w_c), (wmean, mean_w)):
                sp.dma_start(d[:, :], s).then_inc(weights_in, DMA)
            with sp.Fori(0, BATCH) as b:
                for c in range(CHUNKS):
                    sp.wait_ge(centred_ready, START + b * CHUNKS)
                    sp.dma_start(x[c][:, :], x1_dram[bass.ds(b, 1), :, BANK * c:BANK * c + BANK].rearrange(
                        "b c l -> (b c) l")).then_inc(x_in[c], DMA)
                for c in range(CHUNKS):
                    n = b * CHUNKS + c + 1
                    for ready, tile, dram in ((z_ready, z, z_dram), (readout_ready, readout, readout_dram),
                                              (input_ready, inputs, input_dram)):
                        sp.wait_ge(ready, START + n)
                        sp.dma_start(dram[bass.ds(b * CHUNKS + c, 1), :, :].rearrange("n p l -> (n p) l"),
                                     tile[c][:, :]).then_inc(stored[c], DMA)
                    sp.wait_ge(part3_ready, START + n)
                    sp.dma_start(delta_dram[bass.ds(b * CHUNKS + c, 1), :, :, :].rearrange("n s p l -> (n p) s l"),
                                 parts[c][:, :, :]).then_inc(stored[c], DMA)
            for c in range(CHUNKS):
                sp.wait_ge(stored[c], START + BATCH * STORES * DMA)

        @block.tensor
        def _(pe):
            pe.wait_ge(weights_in, START + 5 * DMA)
            with pe.Fori(0, BATCH) as b:
                def statistics(c):
                    n = b * CHUNKS + c
                    pe.wait_ge(x_in[c], START + (b + 1) * DMA)
                    pe.wait_ge(centred_ready, START + n)
                    pe.sem_inc(passed, 1)
                    pe.matmul(mean_ps[:, :], wmean[:, :], x[c][:, :], start=True, stop=True).then_inc(mean_ready, 1)
                    pe.wait_ge(square_ready, START + n + 1)
                    pe.wait_ge(std_ready, START + n)
                    pe.sem_inc(passed, 1)
                    pe.matmul(var_ps[:, :], wmean[:, :], square[c][:, :], start=True, stop=True).then_inc(var_ready, 1)

                def projections(c):
                    n = b * CHUNKS + c
                    pe.wait_ge(normed_ready, START + n + 1)
                    pe.wait_ge(z_ready, START + n)
                    pe.matmul(xs_ps[:, :], win[:, 0:INNER], normed[c][:, :], start=True, stop=True)
                    pe.matmul(z_ps[:, :], win[:, INNER:], normed[c][:, :], start=True, stop=True).then_inc(in_ready, 1)
                    pe.wait_ge(xs_ready, START + n + 1)
                    pe.wait_ge(rest1_ready, START + n)
                    pe.wait_ge(readout_ready, START + n)
                    pe.wait_ge(input_ready, START + n)
                    pe.matmul(delta_ps[:, :], wdelta[:, :], xs[c][:, :], start=True, stop=True)
                    pe.matmul(b_ps[:, :], wb[:, :], xs[c][:, :], start=True, stop=True)
                    pe.matmul(c_ps[:, :], wc[:, :], xs[c][:, :], start=True, stop=True).then_inc(out_ready, 1)

                statistics(0)
                statistics(1)
                projections(0)
                projections(1)

        @block.scalar
        def _(act):
            act.wait_ge(eps_set, START + 1)
            with act.Fori(0, BATCH) as b:
                for c in range(CHUNKS):
                    n = b * CHUNKS + c
                    act.wait_ge(var_ready, START + n + 1)
                    act.wait_ge(inverse_ready, START + b * CHUNKS)
                    act.activation(std[c][:, :], var_ps[:, :], ACT.Sqrt, bias=eps[:, :]).then_inc(std_ready, 1)
                for c in range(CHUNKS):
                    n = b * CHUNKS + c
                    act.wait_ge(in_ready, START + n + 1)
                    act.wait_ge(stored[c], START + b * STORES * DMA)
                    act.wait_ge(input_ready, START + b * CHUNKS)
                    act.copy(xs[c][:, :], xs_ps[:, :]).then_inc(xs_ready, 1)
                    act.copy(z[c][:, :], z_ps[:, :]).then_inc(z_ready, 1)
                    act.wait_ge(out_ready, START + n + 1)
                    act.copy(parts[c][:, 0, :], delta_ps[:, :]).then_inc(part1_ready, 1)
                    act.copy(readout[c][:, :], c_ps[:, :]).then_inc(readout_ready, 1)

        @block.gpsimd
        def _(pool):
            pool.memset(eps[:, :], 1e-5).then_inc(eps_set, 1)
            with pool.Fori(0, BATCH) as b:
                for c in range(CHUNKS):
                    n = b * CHUNKS + c
                    pool.wait_ge(centred_ready, START + n + 1)
                    pool.wait_ge(var_ready, START + b * CHUNKS)
                    pool.tensor_tensor(square[c][:, :], centred[c][:, :], centred[c][:, :],
                                       ALU.mult).then_inc(square_ready, 1)
                for c in range(CHUNKS):
                    pool.wait_ge(rest1_ready, START + b * CHUNKS + c + 1)
                    pool.sem_inc(passed, 1)
                    pool.tensor_copy(parts[c][:, 1, :], rest[c][:, :]).then_inc(part2_ready, 1)

        @block.vector
        def _(dve):
            with dve.Fori(0, BATCH) as b:
                for c in range(CHUNKS):
                    n = b * CHUNKS + c
                    dve.wait_ge(mean_ready, START + n + 1)
                    dve.wait_ge(normed_ready, START + b * CHUNKS)
                    dve.tensor_tensor(centred[c][:, :], x[c][:, :], mean_ps[:, :],
                                      ALU.subtract).then_inc(centred_ready, 1)
                for c in range(CHUNKS):
                    n = b * CHUNKS + c
                    dve.wait_ge(std_ready, START + n + 1)
                    dve.reciprocal(std[c][:, :], std[c][:, :]).then_inc(inverse_ready, 1)
                    dve.wait_ge(inverse_ready, START + n + 1)
                    dve.wait_ge(in_ready, START + b * CHUNKS)
                    dve.tensor_tensor(normed[c][:, :], centred[c][:, :], std[c][:, :],
                                      ALU.mult).then_inc(normed_ready, 1)
                for c in range(CHUNKS):
                    n = b * CHUNKS + c
                    dve.wait_ge(out_ready, START + n + 1)
                    dve.wait_ge(part1_ready, START + n + 1)
                    dve.tensor_tensor(rest[c][:, :], delta_ps[:, :], parts[c][:, 0, :],
                                      ALU.subtract).then_inc(rest1_ready, 1)
                    dve.wait_ge(stored[c], START + b * STORES * DMA)
                    dve.tensor_tensor(inputs[c][:, :], b_ps[:, :], xs[c][:, :], ALU.mult).then_inc(input_ready, 1)
                    dve.wait_ge(part2_ready, START + n + 1)
                    dve.tensor_tensor(parts[c][:, 2, :], rest[c][:, :], parts[c][:, 1, :],
                                      ALU.subtract).then_inc(part3_ready, 1)


GROUPS = 4
WIDTH = INNER // GROUPS
UNITS = PAIRS * GROUPS * WIDTH
FOLD = 4
RING = 3


def scan_phase(nc, delta_dram, input_dram, readout_dram, a_t, selectors, y_dram):
    direct = [k % 3 == 2 for k in range(WIDTH)]
    V = sum(direct)
    G = WIDTH - V
    BLOCKS = CHUNKS * GROUPS

    with ExitStack() as ctx:
        def sb(name, shape, dt=F32):
            return ctx.enter_context(nc.sbuf_tensor(name, shape, dt))

        sem = Semaphores(nc, ctx, "scan")
        states = [sb(f"states{j}", [STATE, WIDTH, BANK]) for j in range(2)]
        spread = sb("spread", [STATE, FOLD * BANK + FOLD])
        readout = sb("s_readout", [STATE, BANK])
        entering = [sb(f"entering{c}", [STATE, BANK]) for c in range(2)]
        parts = sb("s_parts", [SPLITS * WIDTH, GROUPS, BANK], BF16)
        sel = sb("pick", [SPLITS * WIDTH, WIDTH, STATE], BF16)
        decay_rate = sb("decay_rate", [STATE, INNER])
        carry = sb("carry", [STATE, INNER])
        copied = [sb(f"copied{i}", [STATE, BANK]) for i in range(RING)]
        enter_g = [sb(f"enter_g{i}", [STATE, BANK]) for i in range(RING)]
        enter_v = [sb(f"enter_v{i}", [STATE, BANK]) for i in range(2)]
        y_sb = sb("y_sb", [128, WIDTH, INNER])
        delta_ps = [ctx.enter_context(nc.psum_tensor(f"delta_ps{i}", [STATE, BANK], F32)) for i in range(RING)]
        decay = [ctx.enter_context(nc.psum_tensor(f"decay{i}", [STATE, BANK], F32)) for i in range(RING)]
        y_ps = [ctx.enter_context(nc.psum_tensor(f"y_ps{h}", [128, BANK], F32)) for h in range(2)]

        consts_in = sem("consts_in")
        zeroed, y_zeroed = sem("zeroed"), sem("y_zeroed")
        parts_in = [sem(f"parts_in{g}") for g in range(GROUPS)]
        entering_in = [sem(f"entering_in{c}") for c in range(2)]
        readout_in, spread_ready = sem("readout_in"), sem("spread_ready")
        delta_ready, decay_ready, copied_ready = sem("delta_ready"), sem("decay_ready"), sem("copied_ready")
        enter_g_ready, enter_v_ready = sem("enter_g_ready"), sem("enter_v_ready")
        scanned, carried = sem("scanned"), sem("carried")
        y_half, y_moved = sem("y_half"), sem("y_moved")
        y_out = sem("y_out")
        block = ctx.enter_context(nc.Block())

        BU = BLOCKS * WIDTH

        def unit(X, k):
            v = sum(direct[:k])
            return X * WIDTH + k, X * V + v, X * G + (k - v)

        def ahead(X, k, by):
            n = X * WIDTH + k + by
            return (n // WIDTH, n % WIDTH)

        LATE = 4
        slots = [[] for _ in range(WIDTH)]
        for i in range(WIDTH):
            slots[LATE + i * (WIDTH - LATE) // WIDTH].append(i)
        HALF = WIDTH // 2

        def slots_of(i):
            return next(k for k in range(WIDTH) if i in slots[k])

        @block.sync
        def _(sp):
            for s in sem.made:
                sp.sem_inc(s, START)
            def load_tokens(p, c):
                sp.dma_start(entering[c][:, :], input_dram[bass.ds(p, 1), :, :].rearrange("n p l -> (n p) l")
                             ).then_inc(entering_in[c], DMA)

            def load_readout(p):
                sp.dma_start(readout[:, :], readout_dram[bass.ds(p, 1), :, :].rearrange("n p l -> (n p) l")
                             ).then_inc(readout_in, DMA)

            def load_parts(p, g):
                src = delta_dram[bass.ds(p, 1), :, WIDTH * g:WIDTH * g + WIDTH, :].rearrange("n s k l -> (n s) k l")
                for s in range(SPLITS):
                    sp.dma_start(parts[WIDTH * s:WIDTH * s + WIDTH, g, :], src[s, :, :]).then_inc(parts_in[g], DMA)

            def store_y(p):
                sp.wait_ge(y_moved, START + (p * GROUPS + 1) * 2)
                for j in range(4):
                    dst = y_dram[bass.ds(p, 1), FOLD * j:FOLD * j + FOLD, :]
                    sp.dma_start(dst.rearrange("n p l -> (n p) l"),
                                 y_sb[32 * j:32 * j + FOLD, :, :].rearrange("p i d -> p (i d)")).then_inc(y_out, DMA)

            def pair(p, c, load_next):
                if load_next:
                    sp.wait_ge(scanned, START + p * (GROUPS * WIDTH))
                    load_tokens(p + 1, 1 - c)
                for g in range(GROUPS):
                    if g == 1:
                        store_y(p)
                    if load_next:
                        sp.wait_ge(delta_ready, START + (p * GROUPS + g + 1) * WIDTH)
                        load_parts(p + 1, g)
                        if g == 1:
                            sp.wait_ge(spread_ready, START + p + 1)
                            load_readout(p + 1)

            sp.dma_start(sel[:, :, :], selectors).then_inc(consts_in, DMA)
            sp.dma_start(decay_rate[:, :], a_t).then_inc(consts_in, DMA)
            for g in range(GROUPS):
                load_parts(0, g)
                if g == 0:
                    load_tokens(0, 0)
                    load_readout(0)
            with sp.Fori(0, BATCH - 1) as b:
                for c in range(CHUNKS):
                    pair(b * CHUNKS + c, c, True)
            pair(PAIRS - 2, 0, True)
            pair(PAIRS - 1, 1, False)
            store_y(PAIRS)
            sp.wait_ge(y_out, START + (PAIRS + 1) * 4 * DMA)

        def broadcast(pe, b, X, k):
            n = unit(X, k)[0]
            g = X % GROUPS
            if k == 0:
                pe.wait_ge(parts_in[g], START + (b * CHUNKS + X // GROUPS + 1) * SPLITS * DMA)
            if n >= RING:
                Xl, kl = ahead(X, k, -RING)
                n0, v0, g0 = unit(Xl, kl)
                pe.wait_ge(decay_ready, START + b * BU + n0 + 1)
                if direct[kl]:
                    pe.wait_ge(enter_v_ready, START + b * BLOCKS * V + v0 + 1)
                else:
                    pe.wait_ge(copied_ready, START + b * BLOCKS * G + g0 + 1)
            elif n == 0:
                pe.wait_ge(decay_ready, START + b * BU)
                pe.wait_ge(enter_v_ready, START + b * BLOCKS * V)
                pe.wait_ge(copied_ready, START + b * BLOCKS * G)
            pe.matmul(delta_ps[n % RING][:, :], sel[:, k, :], parts[:, g, :],
                      start=True, stop=True).then_inc(delta_ready, 1)

        def contract(pe, states, i):
            for m in range(FOLD):
                for j in range(4):
                    l = 16 * i + 4 * j + m
                    mm = pe.matmul(y_ps[i // HALF][32 * j:32 * j + FOLD, WIDTH * (i % HALF):WIDTH * (i % HALF) + WIDTH],
                                   spread[:, 4 * l + 3 - m:4 * l + 3 - m + FOLD], states[:, :, l],
                                   start=(m == 0), stop=(m == FOLD - 1))
            if i % HALF == HALF - 1:
                mm.then_inc(y_half, 1)

        @block.tensor
        def _(pe):
            pe.wait_ge(consts_in, START + 2 * DMA)
            pe.wait_ge(zeroed, START + 4)
            pe.wait_ge(y_zeroed, START + 2)
            with pe.Fori(0, BATCH) as b:
                for X in range(BLOCKS):
                    for k in range(WIDTH):
                        broadcast(pe, b, X, k)
                        for i in slots[k]:
                            if i == 0:
                                pe.wait_ge(scanned, START + b * BU + X * WIDTH)
                                pe.wait_ge(spread_ready, START + b * CHUNKS + (X + GROUPS - 1) // GROUPS)
                                pe.wait_ge(y_moved, START + (b * BLOCKS + X) * 2)
                            contract(pe, states[(X + 1) % 2], i)
            pe.wait_ge(scanned, START + UNITS)
            pe.wait_ge(spread_ready, START + PAIRS)
            pe.wait_ge(y_moved, START + BATCH * BLOCKS * 2)
            for i in range(WIDTH):
                contract(pe, states[(BLOCKS + 1) % 2], i)

        @block.scalar
        def _(act):
            act.wait_ge(consts_in, START + 2 * DMA)
            act.wait_ge(zeroed, START + 4)

            def move_y(B, X, h):
                act.wait_ge(y_half, START + B * 2 + h + 1)
                if X % GROUPS == 1 and h == 0:
                    act.wait_ge(y_out, START + (B - 1) * DMA + 4 * DMA)
                at = (X - 1) % GROUPS * WIDTH
                act.copy(y_sb[:, HALF * h:HALF * h + HALF, at:at + WIDTH],
                         y_ps[h][:, :].rearrange("p (i d) -> p i d", d=WIDTH)).then_inc(y_moved, 1)

            with act.Fori(0, BATCH) as b:
                for X in range(BLOCKS):
                    for k in range(WIDTH):
                        n, v, g = unit(X, k)
                        d = (X % GROUPS) * WIDTH + k
                        act.wait_ge(delta_ready, START + b * BU + n + 1)
                        if n >= RING:
                            act.wait_ge(scanned, START + b * BU + n - RING + 1)
                        elif n == 0:
                            act.wait_ge(scanned, START + b * BU)
                        act.activation(decay[n % RING][:, :], delta_ps[n % RING][:, :], ACT.Exp,
                                       scale=decay_rate[:, d:d + 1]).then_inc(decay_ready, 1)
                        if not direct[k]:
                            if g >= RING:
                                act.wait_ge(enter_g_ready, START + b * BLOCKS * G + g - RING + 1)
                            elif g == 0:
                                act.wait_ge(enter_g_ready, START + b * BLOCKS * G)
                            act.copy(copied[g % RING][:, :], delta_ps[n % RING][:, :]).then_inc(copied_ready, 1)
                        if k == slots_of(HALF - 1) + 2:
                            move_y(b * BLOCKS + X, X, 0)
                    move_y(b * BLOCKS + X, X, 1)
            for h in range(2):
                move_y(BATCH * BLOCKS, 0, h)

        @block.gpsimd
        def _(pool):
            for j in range(2):
                pool.memset(states[j][:, :, :], 0.0).then_inc(zeroed, 1)
            pool.memset(spread[:, :], 0.0).then_inc(zeroed, 1)
            pool.memset(y_sb[:, :, :], 0.0).then_inc(zeroed, 1)

            with pool.Fori(0, BATCH) as b:
                for X in range(BLOCKS):
                    c = X // GROUPS
                    for k in range(WIDTH):
                        n, v, g = unit(X, k)
                        if n in (0, GROUPS * WIDTH):
                            pool.wait_ge(entering_in[c], START + (b + 1) * DMA)
                        if not direct[k]:
                            pool.wait_ge(copied_ready, START + b * BLOCKS * G + g + 1)
                            if g >= RING:
                                back = g - RING
                                Xb, kb = back // G, [i for i in range(WIDTH) if not direct[i]][back % G]
                                pool.wait_ge(scanned, START + b * BU + Xb * WIDTH + kb + 1)
                            elif g == 0:
                                pool.wait_ge(scanned, START + b * BU)
                            pool.tensor_tensor(enter_g[g % RING][:, :], copied[g % RING][:, :], entering[c][:, :],
                                               ALU.mult).then_inc(enter_g_ready, 1)

        @block.vector
        def _(dve):
            dve.memset(carry[:, :], 0.0).then_inc(carried, 1)
            for h in range(2):
                dve.memset(y_ps[h][:, :], 0.0).then_inc(y_zeroed, 1)
            dve.wait_ge(consts_in, START + 2 * DMA)
            dve.wait_ge(zeroed, START + 4)

            def product(b, X, k):
                n, v, g = unit(X, k)
                dve.wait_ge(decay_ready, START + b * BU + n + 1)
                dve.tensor_tensor(enter_v[v % 2][:, :], delta_ps[n % RING][:, :], entering[X // GROUPS][:, :],
                                  ALU.mult).then_inc(enter_v_ready, 1)

            with dve.Fori(0, BATCH) as b:
                for X in range(BLOCKS):
                    d0 = (X % GROUPS) * WIDTH
                    for k in range(WIDTH):
                        n, v, g = unit(X, k)
                        if n in (0, GROUPS * WIDTH):
                            dve.wait_ge(entering_in[n // (GROUPS * WIDTH)], START + (b + 1) * DMA)
                        Xa, ka = ahead(X, k, 1)
                        if Xa == X and direct[ka]:
                            product(b, Xa, ka)
                        if k == 0 and direct[0]:
                            product(b, X, 0)
                        if k == 0:
                            dve.wait_ge(y_half, START + (b * BLOCKS + X) * 2)
                            dve.wait_ge(carried, START + b * BLOCKS + X + 1)
                        dve.wait_ge(decay_ready, START + b * BU + n + 1)
                        if direct[k]:
                            dve.wait_ge(enter_v_ready, START + b * BLOCKS * V + v + 1)
                            enter = enter_v[v % 2]
                        else:
                            dve.wait_ge(enter_g_ready, START + b * BLOCKS * G + g + 1)
                            enter = enter_g[g % RING]
                        dve.tensor_tensor_scan(states[X % 2][:, k, :], decay[n % RING][:, :], enter[:, :],
                                               carry[:, d0 + k:d0 + k + 1], ALU.mult, ALU.add).then_inc(scanned, 1)
                    dve.wait_ge(scanned, START + b * BU + (X + 1) * WIDTH)
                    if X < GROUPS:
                        dve.tensor_copy(carry[:, d0:d0 + WIDTH], states[X % 2][:, :, BANK - 1]).then_inc(carried, 1)
                    else:
                        dve.memset(carry[:, d0:d0 + WIDTH], 0.0).then_inc(carried, 1)
                    if X % GROUPS == 0:
                        dve.wait_ge(readout_in, START + (b * CHUNKS + X // GROUPS + 1) * DMA)
                        dve.wait_ge(y_half, START + (b * BLOCKS + X + 1) * 2)
                        dve.tensor_copy(spread[:, FOLD - 1:FOLD - 1 + FOLD * BANK:FOLD], readout[:, :]
                                        ).then_inc(spread_ready, 1)


def gate_phase(nc, y_dram, z_dram, x1_dram, w_out, mean_w, identity, gate_w, gate_b, x2_dram, normed_dram, logit_dram):
    TILES = BANK // 128
    COLS = 128 // (4 * FOLD)
    with ExitStack() as ctx:
        def sb(name, shape, dt=F32):
            return ctx.enter_context(nc.sbuf_tensor(name, shape, dt))

        def ps(name, rows):
            return ctx.enter_context(nc.psum_tensor(name, [rows, BANK], F32))

        sem = Semaphores(nc, ctx, "gate")
        wout, wmean, ident = sb("wout", [INNER, CH]), sb("g_wmean", [CH, CH]), sb("g_ident", [128, 128])
        wgate, bgate, eps = sb("wgate", [CH, EXPERTS]), sb("bgate", [EXPERTS, 1]), sb("g_eps", [CH, 1])
        y = [sb(f"g_y{c}", [128, TILES, INNER]) for c in range(2)]
        z = [sb(f"g_z{c}", [INNER, BANK]) for c in range(2)]
        x1 = [sb(f"g_x1{c}", [CH, BANK]) for c in range(2)]
        swish = [sb(f"swish{c}", [INNER, BANK]) for c in range(2)]
        gated = [sb(f"gated{c}", [INNER, BANK]) for c in range(2)]
        x2 = [sb(f"g_x2{c}", [CH, BANK]) for c in range(2)]
        centred = [sb(f"g_centred{c}", [CH, BANK]) for c in range(2)]
        square = [sb(f"g_square{c}", [CH, BANK]) for c in range(2)]
        std = [sb(f"g_std{c}", [CH, BANK]) for c in range(2)]
        normed = [sb(f"g_normed{c}", [CH, BANK]) for c in range(2)]
        logits = [sb(f"g_logits{c}", [EXPERTS, BANK]) for c in range(2)]
        yt_ps = [ps(f"yt_ps{c}", INNER) for c in range(2)]
        out_ps = [ps(f"out_ps{c}", CH) for c in range(2)]
        mean_ps, var_ps, logit_ps = ps("g_mean_ps", CH), ps("g_var_ps", CH), ps("logit_ps", EXPERTS)

        weights_in, eps_set = sem("weights_in"), sem("eps_set")
        loaded = [sem(f"loaded{c}") for c in range(2)]
        stored = [sem(f"stored{c}") for c in range(2)]
        turned, swish_ready, gated_ready, out_ready, x2_ready = (
            sem("turned"), sem("swish"), sem("gated"), sem("out"), sem("x2"))
        mean_ready, centred_ready, square_ready, var_ready, std_ready = (
            sem("mean"), sem("centred"), sem("square"), sem("var"), sem("std"))
        inverse_ready, normed_ready, logit_ready, logits_ready = (
            sem("inverse"), sem("normed"), sem("logit"), sem("logits"))
        LOADS, STORES = COLS + 2, 3
        passed = sem("passed")
        block = ctx.enter_context(nc.Block())

        @block.sync
        def _(sp):
            for s in sem.made:
                sp.sem_inc(s, START)
            for d, s in ((wout, w_out), (wmean, mean_w), (ident, identity), (wgate, gate_w), (bgate, gate_b)):
                sp.dma_start(d[:, :], s).then_inc(weights_in, DMA)
            with sp.Fori(0, BATCH) as b:
                for c in range(CHUNKS):
                    sp.wait_ge(x2_ready, START + b * CHUNKS)
                    pair = bass.ds(b * CHUNKS + c, 1)
                    src = y_dram[bass.ds(b * CHUNKS + c + 1, 1), :, :].rearrange(
                        "n r (t i d) -> (n i) r t d", i=COLS, d=INNER)
                    for i in range(COLS):
                        sp.dma_start(y[c][16 * i:16 * i + 16, :, :], src[i, :, :, :]).then_inc(loaded[c], DMA)
                    sp.dma_start(z[c][:, :], z_dram[pair, :, :].rearrange("n p l -> (n p) l")).then_inc(loaded[c], DMA)
                    sp.dma_start(x1[c][:, :], x1_dram[bass.ds(b, 1), :, BANK * c:BANK * c + BANK].rearrange(
                        "b c l -> (b c) l")).then_inc(loaded[c], DMA)
                for c in range(CHUNKS):
                    n = b * CHUNKS + c + 1
                    for ready, tile, dram in ((x2_ready, x2, x2_dram), (normed_ready, normed, normed_dram),
                                              (logits_ready, logits, logit_dram)):
                        sp.wait_ge(ready, START + n)
                        sp.dma_start(dram[bass.ds(b, 1), :, BANK * c:BANK * c + BANK].rearrange("b c l -> (b c) l"),
                                     tile[c][:, :]).then_inc(stored[c], DMA)
            for c in range(CHUNKS):
                sp.wait_ge(stored[c], START + BATCH * STORES * DMA)

        @block.tensor
        def _(pe):
            pe.wait_ge(weights_in, START + 5 * DMA)
            with pe.Fori(0, BATCH) as b:
                for c in range(CHUNKS):
                    pe.wait_ge(loaded[c], START + (b + 1) * LOADS * DMA)
                    pe.wait_ge(gated_ready, START + b * CHUNKS + c)
                    for t in range(TILES):
                        mm = pe.transpose(yt_ps[c][:, 128 * t:128 * t + 128], y[c][:, t, :], ident[:, :])
                    mm.then_inc(turned, 1)
                for c in range(CHUNKS):
                    pe.wait_ge(gated_ready, START + b * CHUNKS + c + 1)
                    pe.wait_ge(x2_ready, START + b * CHUNKS + c)
                    pe.sem_inc(passed, 1)
                    pe.matmul(out_ps[c][:, :], wout[:, :], gated[c][:, :], start=True, stop=True).then_inc(out_ready, 1)
                for c in range(CHUNKS):
                    n = b * CHUNKS + c
                    pe.wait_ge(x2_ready, START + n + 1)
                    pe.wait_ge(centred_ready, START + n)
                    pe.sem_inc(passed, 1)
                    pe.matmul(mean_ps[:, :], wmean[:, :], x2[c][:, :], start=True, stop=True).then_inc(mean_ready, 1)
                    pe.wait_ge(square_ready, START + n + 1)
                    pe.wait_ge(std_ready, START + n)
                    pe.sem_inc(passed, 1)
                    pe.matmul(var_ps[:, :], wmean[:, :], square[c][:, :], start=True, stop=True).then_inc(var_ready, 1)
                for c in range(CHUNKS):
                    n = b * CHUNKS + c
                    pe.wait_ge(normed_ready, START + n + 1)
                    pe.wait_ge(logits_ready, START + n)
                    pe.sem_inc(passed, 1)
                    pe.matmul(logit_ps[:, :], wgate[:, :], normed[c][:, :], start=True, stop=True
                              ).then_inc(logit_ready, 1)

        @block.scalar
        def _(act):
            act.wait_ge(eps_set, START + 1)
            act.wait_ge(weights_in, START + 5 * DMA)
            with act.Fori(0, BATCH) as b:
                for c in range(CHUNKS):
                    act.wait_ge(loaded[c], START + (b + 1) * LOADS * DMA)
                    act.wait_ge(gated_ready, START + b * CHUNKS)
                    act.activation(swish[c][:, :], z[c][:, :], ACT.Silu).then_inc(swish_ready, 1)
                for c in range(CHUNKS):
                    act.wait_ge(var_ready, START + b * CHUNKS + c + 1)
                    act.wait_ge(inverse_ready, START + b * CHUNKS)
                    act.activation(std[c][:, :], var_ps[:, :], ACT.Sqrt, bias=eps[:, :]).then_inc(std_ready, 1)
                for c in range(CHUNKS):
                    act.wait_ge(logit_ready, START + b * CHUNKS + c + 1)
                    act.wait_ge(stored[c], START + b * STORES * DMA)
                    act.activation(logits[c][:, :], logit_ps[:, :], ACT.Identity, bias=bgate[:, :]
                                   ).then_inc(logits_ready, 1)

        @block.gpsimd
        def _(pool):
            pool.memset(eps[:, :], 1e-5).then_inc(eps_set, 1)
            with pool.Fori(0, BATCH) as b:
                for c in range(CHUNKS):
                    pool.wait_ge(centred_ready, START + b * CHUNKS + c + 1)
                    pool.wait_ge(var_ready, START + b * CHUNKS)
                    pool.tensor_tensor(square[c][:, :], centred[c][:, :], centred[c][:, :],
                                       ALU.mult).then_inc(square_ready, 1)

        @block.vector
        def _(dve):
            with dve.Fori(0, BATCH) as b:
                for c in range(CHUNKS):
                    n = b * CHUNKS + c
                    dve.wait_ge(turned, START + n + 1)
                    dve.wait_ge(swish_ready, START + n + 1)
                    dve.wait_ge(out_ready, START + b * CHUNKS)
                    dve.tensor_tensor(gated[c][:, :], yt_ps[c][:, :], swish[c][:, :], ALU.mult).then_inc(gated_ready, 1)
                for c in range(CHUNKS):
                    n = b * CHUNKS + c
                    dve.wait_ge(out_ready, START + n + 1)
                    dve.wait_ge(stored[c], START + b * STORES * DMA)
                    dve.tensor_tensor(x2[c][:, :], out_ps[c][:, :], x1[c][:, :], ALU.add).then_inc(x2_ready, 1)
                for c in range(CHUNKS):
                    n = b * CHUNKS + c
                    dve.wait_ge(mean_ready, START + n + 1)
                    dve.wait_ge(normed_ready, START + b * CHUNKS)
                    dve.tensor_tensor(centred[c][:, :], x2[c][:, :], mean_ps[:, :],
                                      ALU.subtract).then_inc(centred_ready, 1)
                for c in range(CHUNKS):
                    n = b * CHUNKS + c
                    dve.wait_ge(std_ready, START + n + 1)
                    dve.reciprocal(std[c][:, :], std[c][:, :]).then_inc(inverse_ready, 1)
                    dve.wait_ge(inverse_ready, START + n + 1)
                    dve.tensor_tensor(normed[c][:, :], centred[c][:, :], std[c][:, :],
                                      ALU.mult).then_inc(normed_ready, 1)


QUADS = BATCH // GROUP


def expert_phase(nc, logit_dram, normed_dram, x2_dram, identity, weight1, weight2, expert_dram, out_dram):
    TILES = LEN // 128
    ROWS1 = CH + 1
    with ExitStack() as ctx:
        def sb(name, shape, dt=F32):
            return ctx.enter_context(nc.sbuf_tensor(name, shape, dt))

        sem = Semaphores(nc, ctx, "expert")
        ident = sb("e_ident", [128, 128])
        w1 = sb("w1", [ROWS1, EXPERTS, HIDDEN])
        w2 = sb("w2", [128, HIDDEN // 128, EXPERTS, CH])
        w2_bias = sb("w2_bias", [1, EXPERTS, CH])
        ones = sb("ones", [1, BATCH])
        logits = [sb(f"e_logits{i}", [128, LEN]) for i in range(2)]
        probs = [sb(f"probs{i}", [128, LEN]) for i in range(2)]
        marked = [sb(f"marked{i}", [128, LEN]) for i in range(2)]
        chosen = [sb(f"chosen{q}", [128, LEN]) for q in range(QUADS)]
        tops = sb("tops", [128, QUADS, TOPK])
        best = sb("best", [128, QUADS, TOPK])
        minus = sb("minus", [128, QUADS])
        total = sb("total", [128, QUADS])
        share = sb("share", [128, QUADS])
        chosen_t = sb("chosen_t", [128, TILES, 128])
        normed = [sb(f"e_normed{i}", [CH, LEN]) for i in range(2)]
        normed_t = [sb(f"normed_t{i}", [128, TILES, CH]) for i in range(2)]
        pooled = sb("pooled", [ROWS1, BATCH, EXPERTS])
        hidden = sb("hidden", [128, EXPERTS, HIDDEN // 128, BATCH])
        results = sb("results", [BATCH, EXPERTS, CH])
        spread = sb("e_spread", [128, QUADS, GROUP, CH])
        x2 = [sb(f"e_x2{i}", [CH, BANK]) for i in range(2)]
        final = [sb(f"final{i}", [CH, BANK]) for i in range(2)]
        chosen_ps = ctx.enter_context(nc.psum_tensor("chosen_ps", [128, TILES, 128], F32))
        normed_ps = ctx.enter_context(nc.psum_tensor("normed_ps", [128, TILES, CH], F32))
        pooled_ps = ctx.enter_context(nc.psum_tensor("pooled_ps", [CH, BANK], F32))
        work_ps = ctx.enter_context(nc.psum_tensor("work_ps", [128, 4, BANK], F32))

        consts_in, weights_in, ones_set, spread_zeroed = (
            sem("consts_in"), sem("weights_in"), sem("ones_set"), sem("spread_zeroed"))
        logits_in = [sem(f"logits_in{i}") for i in range(2)]
        normed_in = [sem(f"normed_in{i}") for i in range(2)]
        top_ready, minus_ready, exp_ready, share_ready, probs_ready = (
            sem("top"), sem("minus"), sem("exp"), sem("share"), sem("probs"))
        best_ready, marked_ready, chosen_ready = sem("best"), sem("marked"), sem("chosen")
        chosen_turned, chosen_t_ready, normed_turned, normed_t_ready = (
            sem("chosen_turned"), sem("chosen_t"), sem("normed_turned"), sem("normed_t"))
        pooled_summed, pooled_ready = sem("pooled_summed"), sem("pooled")
        hidden_summed, hidden_ready, results_summed, results_ready = (
            sem("hidden_summed"), sem("hidden"), sem("results_summed"), sem("results"))
        results_out, spread_in = sem("results_out"), sem("spread_in")
        x2_in = [sem(f"x2_in{i}") for i in range(2)]
        scattered, final_ready = sem("scattered"), sem("final")
        stored = [sem(f"stored{i}") for i in range(2)]
        PIECES = BATCH * CHUNKS
        block = ctx.enter_context(nc.Block())

        @block.sync
        def _(sp):
            sp.dma_start(ident[:, :], identity).then_inc(consts_in, DMA)
            for q in range(QUADS):
                if q >= 2:
                    sp.wait_ge(probs_ready, q - 1)
                sp.dma_start(logits[q % 2][:, :], logit_dram[GROUP * q:GROUP * q + GROUP, :, :].rearrange(
                    "b e l -> (b e) l")).then_inc(logits_in[q % 2], DMA)
                if q == 0:
                    sp.dma_start(w1[:, :, :], weight1.rearrange("e d h -> d e h")).then_inc(weights_in, DMA)
                    for h in range(2):
                        sp.dma_start(w2[:, h, :, :], weight2[:, 128 * h:128 * h + 128, :].rearrange("e h o -> h e o")
                                     ).then_inc(weights_in, DMA)
                    sp.dma_start(w2_bias[:, :, :], weight2[:, HIDDEN:HIDDEN + 1, :].rearrange("e h o -> h e o")
                                 ).then_inc(weights_in, DMA)
                for i in range(GROUP):
                    b = q * GROUP + i
                    if b >= 2:
                        sp.wait_ge(normed_turned, b - 1)
                    sp.dma_start(normed[b % 2][:, :], normed_dram[b, :, :]).then_inc(normed_in[b % 2], DMA)
            sp.wait_ge(results_ready, 4)
            sp.dma_start(expert_dram, results[:, :, :]).then_inc(results_out, DMA)
            sp.wait_ge(results_out, DMA)
            sp.wait_ge(spread_zeroed, 1)
            for i in range(GROUP):
                sp.dma_start(spread[EXPERTS * i:EXPERTS * i + EXPERTS, :, i, :],
                             expert_dram.rearrange("(q i) e o -> i e q o", i=GROUP)[i, :, :, :]).then_inc(spread_in, DMA)
            for n in range(PIECES + 2):
                if n < PIECES:
                    b, c = n // CHUNKS, n % CHUNKS
                    if n >= 2:
                        sp.wait_ge(final_ready, n - 1)
                    sp.dma_start(x2[n % 2][:, :], x2_dram[b, :, BANK * c:BANK * c + BANK]).then_inc(x2_in[n % 2], DMA)
                if n >= 2:
                    b, c = (n - 2) // CHUNKS, n % CHUNKS
                    sp.wait_ge(final_ready, n - 1)
                    sp.dma_start(out_dram[b, :, BANK * c:BANK * c + BANK], final[n % 2][:, :]).then_inc(stored[n % 2], DMA)
            for i in range(2):
                sp.wait_ge(stored[i], PIECES // 2 * DMA)

        @block.tensor
        def _(pe):
            pe.wait_ge(consts_in, DMA)
            for q in range(QUADS):
                pe.wait_ge(chosen_ready, q + 1)
                if q:
                    pe.wait_ge(chosen_t_ready, q)
                for t in range(TILES):
                    mm = pe.transpose(chosen_ps[:, t, :], chosen[q][:, 128 * t:128 * t + 128], ident[:, :])
                mm.then_inc(chosen_turned, 1)
                for i in range(GROUP):
                    b = q * GROUP + i
                    pe.wait_ge(normed_in[b % 2], (b // 2 + 1) * DMA)
                    if b:
                        pe.wait_ge(normed_t_ready, b)
                    for t in range(TILES):
                        mm = pe.transpose(normed_ps[:, t, :], normed[b % 2][:, 128 * t:128 * t + 128], ident[0:CH, 0:CH])
                    mm.then_inc(normed_turned, 1)
                    if i == 0:
                        pe.wait_ge(chosen_t_ready, q + 1)
                    pe.wait_ge(normed_t_ready, b + 1)
                    if b:
                        pe.wait_ge(pooled_ready, b)
                    for t in range(TILES):
                        mm = pe.matmul(pooled_ps[:, 0:EXPERTS], normed_t[b % 2][:, t, :],
                                       chosen_t[:, t, EXPERTS * i:EXPERTS * i + EXPERTS],
                                       start=(t == 0), stop=(t == TILES - 1))
                    mm.then_inc(pooled_summed, 1)
            pe.wait_ge(weights_in, 4 * DMA)
            pe.wait_ge(ones_set, 2)
            pe.wait_ge(pooled_ready, BATCH)
            for e in range(EXPERTS):
                for h in range(2):
                    at = (e % 16 * 2 + h) * BATCH
                    mm = pe.matmul(work_ps[:, e // 16, at:at + BATCH], w1[:, e, 128 * h:128 * h + 128],
                                   pooled[:, :, e], start=True, stop=True)
                if e % 16 == 15:
                    mm.then_inc(hidden_summed, 1)
            for e in range(EXPERTS):
                if e % 16 == 0:
                    pe.wait_ge(hidden_ready, 2)
                out = work_ps[0:BATCH, e // 8, e % 8 * CH:e % 8 * CH + CH]
                for h in range(2):
                    pe.matmul(out, hidden[:, e, h, :], w2[:, h, e, :], start=(h == 0), stop=False)
                mm = pe.matmul(out, ones[:, :], w2_bias[:, e, :], start=False, stop=True)
                if e % 8 == 7:
                    mm.then_inc(results_summed, 1)
            pe.wait_ge(spread_in, GROUP * DMA)
            pe.wait_ge(results_ready, 4)
            for n in range(PIECES):
                b, c = n // CHUNKS, n % CHUNKS
                if n >= 4:
                    pe.wait_ge(final_ready, n - 3)
                pe.matmul(work_ps[0:CH, n % 4, :], spread[:, b // GROUP, b % GROUP, :],
                          chosen[b // GROUP][:, BANK * c:BANK * c + BANK], start=True, stop=True).then_inc(scattered, 1)

        @block.scalar
        def _(act):
            for q in range(QUADS):
                act.wait_ge(minus_ready, q + 1)
                if q >= 2:
                    act.wait_ge(chosen_ready, q - 1)
                act.activation(probs[q % 2][:, :], logits[q % 2][:, :], ACT.Exp, bias=minus[:, q:q + 1],
                               accum_out=total[:, q:q + 1]).then_inc(exp_ready, 1)
                act.wait_ge(chosen_turned, q + 1)
                if q:
                    act.wait_ge(pooled_summed, GROUP * q)
                act.copy(chosen_t[:, 0:4, :], chosen_ps[:, 0:4, :])
                act.copy(chosen_t[:, 4:8, :], chosen_ps[:, 4:8, :]).then_inc(chosen_t_ready, 1)
                for i in range(GROUP):
                    b = q * GROUP + i
                    act.wait_ge(normed_turned, b + 1)
                    if b >= 2:
                        act.wait_ge(pooled_summed, b - 1)
                    act.copy(normed_t[b % 2][:, :, :], normed_ps[:, :, :]).then_inc(normed_t_ready, 1)
            for h in range(2):
                act.wait_ge(hidden_summed, h + 1)
                act.activation(hidden[:, 16 * h:16 * h + 16, :, :].rearrange("p e h b -> p (e h b)"),
                               work_ps[:, h, :], ACT.Gelu).then_inc(hidden_ready, 1)

        @block.gpsimd
        def _(pool):
            pool.memset(ones[:, :], 1.0).then_inc(ones_set, 1)
            pool.memset(spread[:, :, :, :], 0.0).then_inc(spread_zeroed, 1)

        @block.vector
        def _(dve):
            def top(q):
                dve.wait_ge(logits_in[q % 2], (q // 2 + 1) * DMA)
                dve.max(tops[:, q, :], logits[q % 2][:, :]).then_inc(top_ready, 1)
                dve.wait_ge(top_ready, q + 1)
                dve.tensor_scalar(minus[:, q:q + 1], tops[:, q, 0:1], -1.0, None, ALU.mult).then_inc(minus_ready, 1)

            def choose(q):
                dve.wait_ge(exp_ready, q + 1)
                dve.reciprocal(share[:, q:q + 1], total[:, q:q + 1]).then_inc(share_ready, 1)
                dve.wait_ge(share_ready, q + 1)
                dve.tensor_scalar(probs[q % 2][:, :], probs[q % 2][:, :], share[:, q:q + 1], None,
                                  ALU.mult).then_inc(probs_ready, 1)
                dve.wait_ge(probs_ready, q + 1)
                dve.max(best[:, q, :], probs[q % 2][:, :]).then_inc(best_ready, 1)
                dve.wait_ge(best_ready, q + 1)
                dve.match_replace(out=marked[q % 2][:, :], in_to_replace=best[:, q, :], in_values=probs[q % 2][:, :],
                                  imm_value=-1.0).then_inc(marked_ready, 1)
                dve.wait_ge(marked_ready, q + 1)
                dve.scalar_tensor_tensor(out=chosen[q][:, :], in0=marked[q % 2][:, :], scalar=-1.0,
                                         in1=probs[q % 2][:, :], op0=ALU.is_equal, op1=ALU.mult
                                         ).then_inc(chosen_ready, 1)

            dve.memset(pooled[CH:ROWS1, :, :], 1.0).then_inc(ones_set, 1)
            top(0)
            for q in range(QUADS):
                choose(q)
                if q + 1 < QUADS:
                    top(q + 1)
                for i in range(GROUP):
                    b = q * GROUP + i
                    dve.wait_ge(pooled_summed, b + 1)
                    dve.tensor_copy(pooled[0:CH, b, :], pooled_ps[:, 0:EXPERTS]).then_inc(pooled_ready, 1)
            for h in range(4):
                dve.wait_ge(results_summed, h + 1)
                dve.tensor_copy(results[:, 8 * h:8 * h + 8, :].rearrange("p e o -> p (e o)"),
                                work_ps[0:BATCH, h, :]).then_inc(results_ready, 1)
            for n in range(PIECES):
                dve.wait_ge(scattered, n + 1)
                dve.wait_ge(x2_in[n % 2], (n // 2 + 1) * DMA)
                if n >= 2:
                    dve.wait_ge(stored[n % 2], (n // 2) * DMA)
                dve.tensor_tensor(final[n % 2][:, :], work_ps[0:CH, n % 4, :], x2[n % 2][:, :],
                                  ALU.add).then_inc(final_ready, 1)


def kernel(**inputs):
    import numpy as np
    from ml_dtypes import bfloat16
    import concourse.bacc as bacc
    from concourse.bass_utils import run_bass_kernel_spmd

    x = np.asarray(inputs["x"])
    f32 = np.float32
    arrays = {"x_pad": np.pad(x, ((0, 0), (0, 0), (0, 0), (0, PITCH - SIDE))).reshape(BATCH, CH, IMG)}
    i2s = np.asarray(inputs["L0_conv_w_i2s"])
    skip = np.asarray(inputs["L0_conv_w_skip"])
    for side in ("left", "right"):
        w = np.asarray(inputs[f"L0_conv_w_{side}"])
        arrays[f"w_{side}"] = np.concatenate([w[:, :, 0].T, w[:, :, 1].T, i2s.T], 0)
        arrays[f"bias_{side}"] = np.tile(np.asarray(inputs[f"L0_conv_b_{side}"]).reshape(4, FEAT).T, (GROUP, 1))
        rows = np.zeros((128, CH), f32)
        at = FEAT if side == "left" else 0
        rows[at:at + FEAT] = skip.T
        arrays[f"w_skip_{side}"] = rows
    arrays["b_skip"] = np.asarray(inputs["L0_conv_b_skip"]).reshape(CH, 1)
    for name in ("W_in", "W_delta", "W_B", "W_C", "W_out"):
        arrays[name] = np.asarray(inputs[f"L1_attn_{name}"])
    arrays["A_t"] = np.asarray(inputs["L1_attn_A"]).T
    arrays["gate_w"] = np.asarray(inputs["L1_ffn_gate_w"]).T
    arrays["gate_b"] = np.asarray(inputs["L1_ffn_gate_b"]).reshape(EXPERTS, 1)
    arrays["weight1"] = np.asarray(inputs["L1_ffn_weight1"])
    arrays["weight2"] = np.asarray(inputs["L1_ffn_weight2"])
    arrays["mean_w"] = np.full((CH, CH), 1.0 / CH, f32)
    arrays["identity"] = np.eye(128, dtype=f32)
    arrays["selectors"] = np.tile(np.eye(WIDTH, dtype=f32)[:, :, None], (SPLITS, 1, STATE)).astype(bfloat16)
    arrays = {k: np.ascontiguousarray(v) for k, v in arrays.items()}

    nc = bacc.Bacc("TRN2", target_bir_lowering=False, num_devices=1)
    a = {k: nc.dram_tensor(k, v.shape, mybir.dt.from_np(v.dtype), kind="ExternalInput").ap()
         for k, v in arrays.items()}
    out = nc.dram_tensor("out", (BATCH, CH, LEN), F32, kind="ExternalOutput").ap()

    def scratch(name, shape, dt=F32):
        return nc.dram_tensor(name, shape, dt, kind="Internal").ap()

    x1 = scratch("x1_dram", (BATCH, CH, LEN))
    delta = scratch("delta_dram", (PAIRS, SPLITS, INNER, BANK), BF16)
    entering = scratch("input_dram", (PAIRS, STATE, BANK))
    readout = scratch("readout_dram", (PAIRS, STATE, BANK))
    z = scratch("z_dram", (PAIRS, INNER, BANK))
    y = scratch("y_dram", (PAIRS + 1, 4 * FOLD, WIDTH * INNER))
    x2 = scratch("x2_dram", (BATCH, CH, LEN))
    normed = scratch("normed_dram", (BATCH, CH, LEN))
    logits = scratch("logit_dram", (BATCH, EXPERTS, LEN))
    experts = scratch("expert_dram", (BATCH, EXPERTS, CH))

    conv_phase(nc, a["x_pad"], a["w_left"], a["w_right"], a["bias_left"], a["bias_right"],
               a["w_skip_left"], a["w_skip_right"], a["b_skip"], x1)
    project_phase(nc, x1, a["W_in"], a["W_delta"], a["W_B"], a["W_C"], a["mean_w"], delta, entering, readout, z)
    scan_phase(nc, delta, entering, readout, a["A_t"], a["selectors"], y)
    gate_phase(nc, y, z, x1, a["W_out"], a["mean_w"], a["identity"], a["gate_w"], a["gate_b"], x2, normed, logits)
    expert_phase(nc, logits, normed, x2, a["identity"], a["weight1"], a["weight2"], experts, out)

    r = run_bass_kernel_spmd(nc, [arrays], core_ids=[0])
    return r.results[0]["out"].reshape(BATCH, CH, SIDE, SIDE)
```

```python
from contextlib import ExitStack

import concourse.bass as bass
from concourse import mybir

F32 = mybir.dt.float32
BF16 = mybir.dt.bfloat16
ALU = mybir.AluOpType
ACT = mybir.ActivationFunctionType
AX = mybir.AxisListType

BATCH = 16
CH = 64
SIDE = 32
LEN = SIDE * SIDE
FEAT = CH // 2
STEPS = SIDE
INNER = 128
STATE = 128
EXPERTS = 32
TOPK = 8
HIDDEN = 256
BANK = 512
DMA = 16
START = 8

GROUP = 4
PITCH = SIDE + 1
IMG = SIDE * PITCH
MARGIN = 2
RW = MARGIN + IMG + 2
GATE_RING = 4
STREAMS = 4
ROUNDS = BATCH // (2 * GROUP)
CHUNKS = LEN // BANK
CROWS = BANK // SIDE
CIMG = CROWS * PITCH


class Semaphores:

    def __init__(self, nc, ctx, phase):
        self.nc, self.ctx, self.phase, self.made = nc, ctx, phase, []

    def __call__(self, name):
        self.made.append(self.ctx.enter_context(self.nc.semaphore(f"{self.phase}_{name}")))
        return self.made[-1]


def conv_phase(nc, x_pad, w_left, w_right, bias_left, bias_right, w_skip_left, w_skip_right, b_skip, x1_dram):
    with ExitStack() as ctx:
        def sb(name, shape, dt=F32):
            return ctx.enter_context(nc.sbuf_tensor(name, shape, dt))

        sem = Semaphores(nc, ctx, "conv")
        rows = [sb(f"rows{s}", [128, GROUP, RW]) for s in range(STREAMS)]
        feat = [sb(f"feat{s}", [128, IMG]) for s in range(STREAMS)]
        cell = [sb(f"cell{s}", [128, LEN]) for s in range(STREAMS)]
        gates = [sb(f"gates{i}", [128, 4, BANK]) for i in range(GATE_RING)]
        forgot = [sb(f"forgot{c}", [128, BANK]) for c in range(CHUNKS)]
        entered = [sb(f"entered{c}", [128, BANK]) for c in range(CHUNKS)]
        squashed = [sb(f"squashed{c}", [128, BANK]) for c in range(CHUNKS)]
        weights = [sb("weights_left", [128, 128]), sb("weights_right", [128, 128])]
        biases = [sb("biases_left", [128, 4]), sb("biases_right", [128, 4])]
        skip_w = [sb("skip_w_left", [128, CH]), sb("skip_w_right", [128, CH])]
        skip_b = sb("skip_b", [128, 1])
        x1 = [sb(f"x1_{i}", [128, BANK]) for i in range(2)]
        pre = [ctx.enter_context(nc.psum_tensor(f"pre{c}", [128, 4, BANK], F32)) for c in range(CHUNKS)]

        weights_in, x_in, zeroed, state_zeroed = sem("weights_in"), sem("x_in"), sem("zeroed"), sem("state_zeroed")
        pre_ready, gates_ready, forgot_ready, entered_ready = (
            sem("pre_ready"), sem("gates_ready"), sem("forgot_ready"), sem("entered_ready"))
        cell_ready, squashed_ready, feat_ready = sem("cell_ready"), sem("squashed_ready"), sem("feat_ready")
        rows_in = [sem(f"rows_in{s}") for s in range(STREAMS)]
        skip_ready, x1_ready = sem("skip_ready"), sem("x1_ready")
        x1_out = [sem(f"x1_out{i}") for i in range(2)]
        passed = sem("passed")
        block = ctx.enter_context(nc.Block())

        def side(s):
            return s // 2

        def half(s):
            return s % 2

        SLOTS = STREAMS * CHUNKS
        SKIPS = 2 * GROUP * CHUNKS

        def image(tile, at):
            return tile[..., at:at + CIMG].rearrange("p (h w) -> p h w", w=PITCH)[:, :, 0:SIDE]

        above = [(PITCH + 1, IMG - PITCH - 1), (PITCH - 1, IMG - PITCH + 1)]
        same = [(1, IMG), (-1, IMG)]
        MOVES = 2 * GROUP

        @block.sync
        def _(sp):
            for s in sem.made:
                sp.sem_inc(s, START)
            for d, s in ((weights[0], w_left), (weights[1], w_right), (biases[0], bias_left),
                         (biases[1], bias_right), (skip_w[0], w_skip_left), (skip_w[1], w_skip_right)):
                sp.dma_start(d[:, :], s).then_inc(weights_in, DMA)
            sp.dma_start(skip_b[CH:128, :], b_skip).then_inc(weights_in, DMA)
            sp.wait_ge(zeroed, START + 1)
            with sp.Fori(0, ROUNDS) as r:
                sp.wait_ge(x1_ready, START + r * SKIPS)
                for s in range(STREAMS):
                    src = x_pad[bass.ds((r * 2 + half(s)) * GROUP, GROUP), :, :].rearrange("q c p -> c q p")
                    sp.dma_start(rows[s][CH:128, :, MARGIN:MARGIN + IMG], src).then_inc(x_in, DMA)
                with sp.Fori(0, STEPS) as t:
                    for s in range(STREAMS):
                        sp.wait_ge(feat_ready, START + (r * STEPS + t) * SLOTS + CHUNKS * (s + 1))
                        for q in range(GROUP):
                            for part, (to, n) in ((0, above[side(s)]), (1, same[side(s)])):
                                sp.dma_start(rows[s][32 * part:32 * part + 32, q, MARGIN + to:MARGIN + to + n],
                                             feat[s][32 * q:32 * q + 32, 0:n]).then_inc(rows_in[s], DMA)
                for k in range(SKIPS):
                    h, q, c = k // (GROUP * CHUNKS), k // CHUNKS % GROUP, k % CHUNKS
                    sp.wait_ge(x1_ready, START + r * SKIPS + k + 1)
                    dst = x1_dram[bass.ds((r * 2 + h) * GROUP + q, 1), :, BANK * c:BANK * c + BANK]
                    sp.dma_start(dst.rearrange("b c l -> (b c) l"), x1[k % 2][CH:128, :]).then_inc(x1_out[k % 2], DMA)
            for i in range(2):
                sp.wait_ge(x1_out[i], START + ROUNDS * SKIPS // 2 * DMA)

        @block.tensor
        def _(pe):
            pe.wait_ge(weights_in, START + 7 * DMA)
            with pe.Fori(0, ROUNDS) as r:
                pe.wait_ge(x_in, START + (r + 1) * STREAMS * DMA)
                pe.wait_ge(state_zeroed, START + r + 1)
                pe.sem_inc(passed, 1)
                with pe.Fori(0, STEPS) as t:
                    for s in range(STREAMS):
                        pe.wait_ge(rows_in[s], START + (r * STEPS + t) * MOVES * DMA)
                        for c in range(CHUNKS):
                            k = s * CHUNKS + c
                            pe.wait_ge(gates_ready, START + (r * STEPS + t) * SLOTS + k - CHUNKS + 1)
                            for g in range(4):
                                for q in range(GROUP):
                                    mm = pe.matmul(pre[c][32 * q:32 * q + 32, g, :],
                                                   weights[side(s)][:, 32 * g:32 * g + 32],
                                                   image(rows[s][:, q, :], MARGIN + CIMG * c),
                                                   start=True, stop=True)
                            mm.then_inc(pre_ready, 1)
                for s in range(STREAMS):
                    pe.wait_ge(rows_in[s], START + (r + 1) * STEPS * MOVES * DMA)
                for k in range(SKIPS):
                    h, q, c = k // (GROUP * CHUNKS), k // CHUNKS % GROUP, k % CHUNKS
                    if k >= 4:
                        pe.wait_ge(x1_ready, START + r * SKIPS + k - 3)
                    out = pre[k // 2 % 2][CH:128, k % 2, :]
                    pe.matmul(out, skip_w[0][:, :], image(rows[h][:, q, :], MARGIN + 1 + CIMG * c),
                              start=True, stop=False)
                    pe.matmul(out, skip_w[1][:, :], image(rows[2 + h][:, q, :], MARGIN - 1 + CIMG * c),
                              start=False, stop=True).then_inc(skip_ready, 1)

        def slot(r, t, k):
            return START + (r * STEPS + t) * SLOTS + k + 1

        def steps(eng, r, first, body):
            first(0)
            with eng.Fori(0, STEPS - 1) as t:
                for k in range(SLOTS):
                    body(t, k, True)
            for k in range(SLOTS):
                body(STEPS - 1, k, k + 1 < SLOTS)

        @block.scalar
        def _(act):
            act.wait_ge(weights_in, START + 7 * DMA)

            def gate_values(r, t, k):
                act.wait_ge(pre_ready, slot(r, t, k))
                act.wait_ge(feat_ready, slot(r, t, k - GATE_RING))
                for g in range(4):
                    a = act.activation(gates[k % GATE_RING][:, g, :], pre[k % CHUNKS][:, g, :], ACT.Sigmoid,
                                       bias=biases[side(k // CHUNKS)][:, g:g + 1])
                a.then_inc(gates_ready, 1)

            def squash(r, t, k):
                c, s = k % CHUNKS, k // CHUNKS
                act.wait_ge(cell_ready, slot(r, t, k))
                act.activation(squashed[c][:, :], cell[s][:, BANK * c:BANK * c + BANK],
                               ACT.Tanh).then_inc(squashed_ready, 1)

            with act.Fori(0, ROUNDS) as r:
                def body(t, k, following):
                    if following:
                        gate_values(r, t + (k + 1) // SLOTS, (k + 1) % SLOTS)
                    squash(r, t, k)

                steps(act, r, lambda t: gate_values(r, t, 0), body)

        @block.gpsimd
        def _(pool):
            for s in range(STREAMS):
                z = pool.memset(rows[s][:, :, :], 0.0)
                z = pool.memset(feat[s][:, :], 0.0)
            z.then_inc(zeroed, 1)
            pool.wait_ge(zeroed, START + 1)
            with pool.Fori(0, ROUNDS) as r:
                pool.wait_ge(x1_ready, START + r * SKIPS)
                pool.sem_inc(passed, 1)
                for s in range(STREAMS):
                    pool.memset(rows[s][0:CH, :, :], 0.0)
                    z = pool.memset(cell[s][:, :], 0.0)
                z.then_inc(state_zeroed, 1)
                with pool.Fori(0, STEPS) as t:
                    for k in range(SLOTS):
                        c = k % CHUNKS
                        pool.wait_ge(gates_ready, slot(r, t, k))
                        pool.wait_ge(cell_ready, slot(r, t, k - CHUNKS))
                        pool.tensor_tensor(entered[c][:, :], gates[k % GATE_RING][:, 2, :],
                                           gates[k % GATE_RING][:, 3, :], ALU.mult).then_inc(entered_ready, 1)

        @block.vector
        def _(dve):
            dve.wait_ge(zeroed, START + 1)
            dve.wait_ge(weights_in, START + 7 * DMA)
            with dve.Fori(0, ROUNDS) as r:
                dve.wait_ge(state_zeroed, START + r + 1)
                dve.sem_inc(passed, 1)
                def forget(t, k):
                    c, s = k % CHUNKS, k // CHUNKS
                    dve.wait_ge(gates_ready, slot(r, t, k))
                    dve.tensor_tensor(forgot[c][:, :], gates[k % GATE_RING][:, 1, :],
                                      cell[s][:, BANK * c:BANK * c + BANK], ALU.mult).then_inc(forgot_ready, 1)

                def enter(t, k):
                    c, s = k % CHUNKS, k // CHUNKS
                    dve.wait_ge(entered_ready, slot(r, t, k))
                    dve.wait_ge(forgot_ready, slot(r, t, k))
                    dve.tensor_tensor(cell[s][:, BANK * c:BANK * c + BANK], forgot[c][:, :], entered[c][:, :],
                                      ALU.add).then_inc(cell_ready, 1)

                def new_features(t, k):
                    c, s = k % CHUNKS, k // CHUNKS
                    dve.wait_ge(squashed_ready, slot(r, t, k))
                    dve.wait_ge(rows_in[s], START + (r * STEPS + t) * MOVES * DMA)
                    dve.tensor_tensor(image(feat[s][:, :], CIMG * c), gates[k % GATE_RING][:, 0, :].rearrange(
                        "p (h w) -> p h w", w=SIDE), squashed[c][:, :].rearrange("p (h w) -> p h w", w=SIDE),
                        ALU.mult).then_inc(feat_ready, 1)

                def first(t):
                    forget(t, 0)
                    enter(t, 0)

                def body(t, k, following):
                    after = t + (k + 1) // SLOTS, (k + 1) % SLOTS
                    if following:
                        forget(*after)
                    new_features(t, k)
                    if following:
                        enter(*after)

                steps(dve, r, first, body)
                for k in range(SKIPS):
                    h, q, c = k // (GROUP * CHUNKS), k // CHUNKS % GROUP, k % CHUNKS
                    dve.wait_ge(skip_ready, START + r * SKIPS + k + 1)
                    if k >= 2:
                        dve.wait_ge(x1_out[k % 2], START + (r * (SKIPS // 2) + k // 2) * DMA)
                    else:
                        dve.wait_ge(x1_out[k % 2], START + r * (SKIPS // 2) * DMA)
                    dve.scalar_tensor_tensor(
                        out=x1[k % 2][CH:128, :].rearrange("p (h w) -> p h w", w=SIDE),
                        in0=pre[k // 2 % 2][CH:128, k % 2, :].rearrange("p (h w) -> p h w", w=SIDE),
                        scalar=skip_b[CH:128, :],
                        in1=image(rows[h][CH:128, q, :], MARGIN + CIMG * c),
                        op0=ALU.add, op1=ALU.add).then_inc(x1_ready, 1)


SPLITS = 3
PAIRS = BATCH * CHUNKS


def in_pairs(eng, *pieces):
    def run(early, late, both=(0, 1)):
        for behind, piece in pieces:
            if behind in both:
                piece(*(late if behind else early))

    LAST = BATCH // 2 - 1
    run((0, 0, 0), None, (0,))
    with eng.Fori(0, LAST) as turn:
        run((turn * 2 + 1, 1, turn), (turn * 2, 0, turn))
        run((turn * 2 + 2, 0, turn + 1), (turn * 2 + 1, 1, turn))
    run((BATCH - 1, 1, LAST), (BATCH - 2, 0, LAST))
    run(None, (BATCH - 1, 1, LAST), (1,))


def load_ahead(eng, load, store):
    LAST = BATCH // 2 - 1
    for i in range(2):
        load(i, i, 0)
    with eng.Fori(0, LAST) as turn:
        for i in range(2):
            load(turn * 2 + 2 + i, i, turn + 1)
            store(turn * 2 + i, i, turn)
    for i in range(2):
        store(BATCH - 2 + i, i, LAST)


def project_phase(nc, x1_dram, w_in, w_delta, w_b, w_c, mean_w, delta_dram, input_dram, readout_dram, z_dram):
    with ExitStack() as ctx:
        def sb(name, shape, dt=F32):
            return ctx.enter_context(nc.sbuf_tensor(name, shape, dt))

        sem = Semaphores(nc, ctx, "proj")
        win = sb("win", [128, CHUNKS, 2 * INNER])
        wdelta, wb, wc, wmean = (sb("wdelta", [INNER, INNER]), sb("wb", [INNER, STATE]),
                                 sb("wc", [INNER, INNER]), sb("wmean", [128, 128]))
        eps = sb("eps", [128, 1])
        x = [sb(f"px{i}", [128, BANK]) for i in range(2)]
        centred, square, std = sb("centred", [128, BANK]), sb("square", [128, BANK]), sb("std", [128, BANK])
        normed = [sb(f"normed{i}", [128, BANK]) for i in range(2)]
        xs = [sb(f"xs{c}", [INNER, BANK]) for c in range(2)]
        z = [sb(f"z{c}", [INNER, BANK]) for c in range(2)]
        readout = [sb(f"readout{c}", [INNER, BANK]) for c in range(2)]
        inputs = [sb(f"inputs{c}", [INNER, BANK]) for c in range(2)]
        parts = [sb(f"parts{c}", [INNER, SPLITS, BANK], BF16) for c in range(2)]
        rest = [sb(f"rest{c}", [INNER, BANK]) for c in range(2)]

        def ps(name):
            return ctx.enter_context(nc.psum_tensor(name, [128, BANK], F32))

        mean_ps, var_ps, z_ps, delta_ps, b_ps, c_ps = (
            ps(n) for n in ("mean_ps", "var_ps", "z_ps", "delta_ps", "b_ps", "c_ps"))
        xs_ps = [ps("xs_ps0"), ps("xs_ps1")]

        weights_in, eps_set = sem("weights_in"), sem("eps_set")
        x_in = [sem(f"x_in{i}") for i in range(2)]
        stored = [sem(f"stored{c}") for c in range(2)]
        mean_ready, centred_ready, square_ready, var_ready, std_ready = (
            sem("mean"), sem("centred"), sem("square"), sem("var"), sem("std"))
        inverse_ready, normed_ready = sem("inverse"), sem("normed")
        in_ready, xs_ready, z_ready = sem("in_ready"), sem("xs_ready"), sem("z_ready")
        out_ready, part1_ready, rest1_ready, part2_ready, part3_ready = (
            sem("out_ready"), sem("part1"), sem("rest1"), sem("part2"), sem("part3"))
        readout_ready, input_ready = sem("readout"), sem("input")
        STORES = 4
        WEIGHTS = 4 + CHUNKS
        passed = sem("passed")
        block = ctx.enter_context(nc.Block())

        @block.sync
        def _(sp):
            for s in sem.made:
                sp.sem_inc(s, START)
            for d, s in ((wdelta, w_delta), (wb, w_b), (wc, w_c), (wmean, mean_w)):
                sp.dma_start(d[:, :], s).then_inc(weights_in, DMA)
            for c in range(CHUNKS):
                sp.dma_start(win[:, c, :], w_in[c, :, :]).then_inc(weights_in, DMA)

            def load(b, i, turn):
                sp.wait_ge(centred_ready, START + turn * 2)
                for c in range(CHUNKS):
                    sp.dma_start(x[i][CH * c:CH * c + CH, :],
                                 x1_dram[bass.ds(b, 1), :, BANK * c:BANK * c + BANK].rearrange("b c l -> (b c) l")
                                 ).then_inc(x_in[i], DMA)

            def store(b, i, turn):
                for c in range(CHUNKS):
                    n = b * CHUNKS + c
                    for ready, tile, dram in ((z_ready, z, z_dram), (readout_ready, readout, readout_dram),
                                              (input_ready, inputs, input_dram)):
                        sp.wait_ge(ready, START + n + 1)
                        sp.dma_start(dram[bass.ds(n, 1), :, :].rearrange("n p l -> (n p) l"),
                                     tile[c][:, :]).then_inc(stored[c], DMA)
                    sp.wait_ge(part3_ready, START + n + 1)
                    sp.dma_start(delta_dram[bass.ds(n, 1), :, :, :].rearrange("n s p l -> (n p) s l"),
                                 parts[c][:, :, :]).then_inc(stored[c], DMA)

            load_ahead(sp, load, store)
            for c in range(CHUNKS):
                sp.wait_ge(stored[c], START + BATCH * STORES * DMA)

        @block.tensor
        def _(pe):
            pe.wait_ge(weights_in, START + WEIGHTS * DMA)

            def norm(b, i, turn):
                pe.wait_ge(x_in[i], START + (turn + 1) * CHUNKS * DMA)
                pe.wait_ge(centred_ready, START + b)
                pe.matmul(mean_ps[:, :], wmean[:, :], x[i][:, :], start=True, stop=True).then_inc(mean_ready, 1)
                pe.wait_ge(square_ready, START + b + 1)
                pe.wait_ge(std_ready, START + b)
                pe.matmul(var_ps[:, :], wmean[:, :], square[:, :], start=True, stop=True).then_inc(var_ready, 1)

            def project(b, i, turn):
                pe.wait_ge(normed_ready, START + b + 1)
                for c in range(CHUNKS):
                    pe.wait_ge(xs_ready, START + b * CHUNKS)
                    pe.matmul(xs_ps[c][:, :], win[:, c, 0:INNER], normed[i][:, :], start=True, stop=True)
                    pe.wait_ge(z_ready, START + b * CHUNKS + c)
                    pe.matmul(z_ps[:, :], win[:, c, INNER:], normed[i][:, :], start=True, stop=True
                              ).then_inc(in_ready, 1)
                for c in range(CHUNKS):
                    n = b * CHUNKS + c
                    pe.wait_ge(xs_ready, START + n + 1)
                    pe.wait_ge(rest1_ready, START + n)
                    pe.matmul(delta_ps[:, :], wdelta[:, :], xs[c][:, :], start=True, stop=True)
                    pe.wait_ge(input_ready, START + n)
                    pe.matmul(b_ps[:, :], wb[:, :], xs[c][:, :], start=True, stop=True)
                    pe.wait_ge(readout_ready, START + n)
                    pe.matmul(c_ps[:, :], wc[:, :], xs[c][:, :], start=True, stop=True).then_inc(out_ready, 1)

            in_pairs(pe, (0, norm), (1, project))

        @block.scalar
        def _(act):
            act.wait_ge(eps_set, START + 1)

            def norm(b, i, turn):
                act.wait_ge(var_ready, START + b + 1)
                act.wait_ge(normed_ready, START + b)
                act.activation(std[:, :], var_ps[:, :], ACT.Sqrt, bias=eps[:, :]).then_inc(std_ready, 1)

            def project(b, i, turn):
                for c in range(CHUNKS):
                    act.wait_ge(in_ready, START + b * CHUNKS + c + 1)
                    act.wait_ge(stored[c], START + b * STORES * DMA)
                    act.wait_ge(input_ready, START + b * CHUNKS)
                    act.copy(xs[c][:, :], xs_ps[c][:, :]).then_inc(xs_ready, 1)
                    act.copy(z[c][:, :], z_ps[:, :]).then_inc(z_ready, 1)
                for c in range(CHUNKS):
                    act.wait_ge(out_ready, START + b * CHUNKS + c + 1)
                    act.copy(parts[c][:, 0, :], delta_ps[:, :]).then_inc(part1_ready, 1)
                    act.copy(readout[c][:, :], c_ps[:, :]).then_inc(readout_ready, 1)

            in_pairs(act, (0, norm), (1, project))

        @block.gpsimd
        def _(pool):
            pool.memset(eps[:, :], 1e-5).then_inc(eps_set, 1)

            def norm(b, i, turn):
                pool.wait_ge(centred_ready, START + b + 1)
                pool.wait_ge(var_ready, START + b)
                pool.tensor_tensor(square[:, :], centred[:, :], centred[:, :], ALU.mult).then_inc(square_ready, 1)

            def project(b, i, turn):
                for c in range(CHUNKS):
                    pool.wait_ge(rest1_ready, START + b * CHUNKS + c + 1)
                    pool.sem_inc(passed, 1)
                    pool.tensor_copy(parts[c][:, 1, :], rest[c][:, :]).then_inc(part2_ready, 1)

            in_pairs(pool, (0, norm), (1, project))

        @block.vector
        def _(dve):
            def norm(b, i, turn):
                dve.wait_ge(mean_ready, START + b + 1)
                dve.wait_ge(normed_ready, START + b)
                dve.tensor_tensor(centred[:, :], x[i][:, :], mean_ps[:, :], ALU.subtract).then_inc(centred_ready, 1)
                dve.wait_ge(std_ready, START + b + 1)
                dve.reciprocal(std[:, :], std[:, :]).then_inc(inverse_ready, 1)
                dve.wait_ge(inverse_ready, START + b + 1)
                dve.tensor_tensor(normed[i][:, :], centred[:, :], std[:, :], ALU.mult).then_inc(normed_ready, 1)

            def project(b, i, turn):
                for c in range(CHUNKS):
                    n = b * CHUNKS + c
                    dve.wait_ge(out_ready, START + n + 1)
                    dve.wait_ge(part1_ready, START + n + 1)
                    dve.wait_ge(stored[c], START + b * STORES * DMA)
                    dve.tensor_tensor(rest[c][:, :], delta_ps[:, :], parts[c][:, 0, :],
                                      ALU.subtract).then_inc(rest1_ready, 1)
                    dve.tensor_tensor(inputs[c][:, :], b_ps[:, :], xs[c][:, :], ALU.mult).then_inc(input_ready, 1)
                for c in range(CHUNKS):
                    dve.wait_ge(part2_ready, START + b * CHUNKS + c + 1)
                    dve.tensor_tensor(parts[c][:, 2, :], rest[c][:, :], parts[c][:, 1, :],
                                      ALU.subtract).then_inc(part3_ready, 1)

            in_pairs(dve, (0, norm), (1, project))


GROUPS = 4
WIDTH = INNER // GROUPS
UNITS = PAIRS * GROUPS * WIDTH
FOLD = 4
RING = 4


def scan_phase(nc, delta_dram, input_dram, readout_dram, a_t, selectors, y_dram):
    direct = [k % 4 == 3 for k in range(WIDTH)]
    V = sum(direct)
    G = WIDTH - V
    BLOCKS = CHUNKS * GROUPS

    with ExitStack() as ctx:
        def sb(name, shape, dt=F32):
            return ctx.enter_context(nc.sbuf_tensor(name, shape, dt))

        sem = Semaphores(nc, ctx, "scan")
        states = [sb(f"states{j}", [STATE, WIDTH, BANK]) for j in range(2)]
        spread = sb("spread", [STATE, FOLD * BANK + FOLD])
        readout = sb("s_readout", [STATE, BANK])
        entering = [sb(f"entering{c}", [STATE, BANK]) for c in range(2)]
        parts = sb("s_parts", [128, GROUPS, BANK], BF16)
        sel = sb("pick", [128, WIDTH, STATE], BF16)
        decay_rate = sb("decay_rate", [STATE, INNER])
        carry = sb("carry", [STATE, INNER])
        copied = [sb(f"copied{i}", [STATE, BANK]) for i in range(RING)]
        enter_g = [sb(f"enter_g{i}", [STATE, BANK]) for i in range(RING)]
        enter_v = [sb(f"enter_v{i}", [STATE, BANK]) for i in range(2)]
        y_sb = sb("y_sb", [128, WIDTH, INNER])
        delta_ps = [ctx.enter_context(nc.psum_tensor(f"delta_ps{i}", [STATE, BANK], F32)) for i in range(RING)]
        decay = [sb(f"decay{i}", [STATE, BANK]) for i in range(RING)]
        y_ps = [ctx.enter_context(nc.psum_tensor(f"y_ps{h}", [128, BANK], F32)) for h in range(2)]

        consts_in = sem("consts_in")
        zeroed, y_zeroed = sem("zeroed"), sem("y_zeroed")
        parts_in = [sem(f"parts_in{g}") for g in range(GROUPS)]
        entering_in = [sem(f"entering_in{c}") for c in range(2)]
        readout_in, spread_ready = sem("readout_in"), sem("spread_ready")
        delta_ready, decay_ready, copied_ready = sem("delta_ready"), sem("decay_ready"), sem("copied_ready")
        enter_g_ready, enter_v_ready = sem("enter_g_ready"), sem("enter_v_ready")
        scanned, carried = sem("scanned"), sem("carried")
        y_half, y_moved = sem("y_half"), sem("y_moved")
        y_out = sem("y_out")
        block = ctx.enter_context(nc.Block())

        BU = BLOCKS * WIDTH

        def unit(X, k):
            v = sum(direct[:k])
            return X * WIDTH + k, X * V + v, X * G + (k - v)

        def ahead(X, k, by):
            n = X * WIDTH + k + by
            return (n // WIDTH, n % WIDTH)

        LATE = 4
        slots = [[] for _ in range(WIDTH)]
        for i in range(WIDTH):
            slots[LATE + i * (WIDTH - LATE) // WIDTH].append(i)
        HALF = WIDTH // 2

        def slots_of(i):
            return next(k for k in range(WIDTH) if i in slots[k])

        @block.sync
        def _(sp):
            for s in sem.made:
                sp.sem_inc(s, START)
            def load_tokens(p, c):
                sp.dma_start(entering[c][:, :], input_dram[bass.ds(p, 1), :, :].rearrange("n p l -> (n p) l")
                             ).then_inc(entering_in[c], DMA)

            def load_readout(p):
                sp.dma_start(readout[:, :], readout_dram[bass.ds(p, 1), :, :].rearrange("n p l -> (n p) l")
                             ).then_inc(readout_in, DMA)

            def load_parts(p, g):
                src = delta_dram[bass.ds(p, 1), :, WIDTH * g:WIDTH * g + WIDTH, :].rearrange("n s k l -> (n s) k l")
                for s in range(SPLITS):
                    sp.dma_start(parts[WIDTH * s:WIDTH * s + WIDTH, g, :], src[s, :, :]).then_inc(parts_in[g], DMA)

            def store_y(p):
                sp.wait_ge(y_moved, START + (p * GROUPS + 1) * 2)
                for j in range(4):
                    dst = y_dram[bass.ds(p, 1), FOLD * j:FOLD * j + FOLD, :]
                    sp.dma_start(dst.rearrange("n p l -> (n p) l"),
                                 y_sb[32 * j:32 * j + FOLD, :, :].rearrange("p i d -> p (i d)")).then_inc(y_out, DMA)

            def pair(p, c, load_next):
                if load_next:
                    sp.wait_ge(scanned, START + p * (GROUPS * WIDTH))
                    load_tokens(p + 1, 1 - c)
                for g in range(GROUPS):
                    if g == 1:
                        store_y(p)
                    if load_next:
                        sp.wait_ge(delta_ready, START + (p * GROUPS + g + 1) * WIDTH)
                        load_parts(p + 1, g)
                        if g == 1:
                            sp.wait_ge(spread_ready, START + p + 1)
                            load_readout(p + 1)

            sp.dma_start(sel[:, :, :], selectors).then_inc(consts_in, DMA)
            sp.dma_start(decay_rate[:, :], a_t).then_inc(consts_in, DMA)
            for g in range(GROUPS):
                load_parts(0, g)
                if g == 0:
                    load_tokens(0, 0)
                    load_readout(0)
            with sp.Fori(0, BATCH - 1) as b:
                for c in range(CHUNKS):
                    pair(b * CHUNKS + c, c, True)
            pair(PAIRS - 2, 0, True)
            pair(PAIRS - 1, 1, False)
            store_y(PAIRS)
            sp.wait_ge(y_out, START + (PAIRS + 1) * 4 * DMA)

        def broadcast(pe, b, X, k):
            n = unit(X, k)[0]
            g = X % GROUPS
            if k == 0:
                pe.wait_ge(parts_in[g], START + (b * CHUNKS + X // GROUPS + 1) * SPLITS * DMA)
            Xl, kl = ahead(X, k, -RING)
            n0, v0, g0 = unit(Xl, kl)
            pe.wait_ge(decay_ready, START + b * BU + n0 + 1)
            if direct[kl]:
                pe.wait_ge(enter_v_ready, START + b * BLOCKS * V + v0 + 1)
            else:
                pe.wait_ge(copied_ready, START + b * BLOCKS * G + g0 + 1)
            pe.matmul(delta_ps[n % RING][:, :], sel[:, k, :], parts[:, g, :],
                      start=True, stop=True).then_inc(delta_ready, 1)

        def contract(pe, states, i):
            for m in range(FOLD):
                for j in range(4):
                    l = 16 * i + 4 * j + m
                    mm = pe.matmul(y_ps[i // HALF][32 * j:32 * j + FOLD, WIDTH * (i % HALF):WIDTH * (i % HALF) + WIDTH],
                                   spread[:, 4 * l + 3 - m:4 * l + 3 - m + FOLD], states[:, :, l],
                                   start=(m == 0), stop=(m == FOLD - 1))
            if i % HALF == HALF - 1:
                mm.then_inc(y_half, 1)

        @block.tensor
        def _(pe):
            pe.wait_ge(consts_in, START + 2 * DMA)
            pe.wait_ge(zeroed, START + 5)
            pe.wait_ge(y_zeroed, START + 2)
            with pe.Fori(0, BATCH) as b:
                for X in range(BLOCKS):
                    for k in range(WIDTH):
                        broadcast(pe, b, X, k)
                        for i in slots[k]:
                            if i == 0:
                                pe.wait_ge(scanned, START + b * BU + X * WIDTH)
                                pe.wait_ge(spread_ready, START + b * CHUNKS + (X + GROUPS - 1) // GROUPS)
                                pe.wait_ge(y_moved, START + (b * BLOCKS + X) * 2)
                            contract(pe, states[(X + 1) % 2], i)
            pe.wait_ge(scanned, START + UNITS)
            pe.wait_ge(spread_ready, START + PAIRS)
            pe.wait_ge(y_moved, START + BATCH * BLOCKS * 2)
            for i in range(WIDTH):
                contract(pe, states[(BLOCKS + 1) % 2], i)

        @block.scalar
        def _(act):
            act.wait_ge(consts_in, START + 2 * DMA)
            act.wait_ge(zeroed, START + 5)

            def move_y(B, X, h):
                act.wait_ge(y_half, START + B * 2 + h + 1)
                if X % GROUPS == 1 and h == 0:
                    act.wait_ge(y_out, START + (B - 1) * DMA + 4 * DMA)
                at = (X - 1) % GROUPS * WIDTH
                act.copy(y_sb[:, HALF * h:HALF * h + HALF, at:at + WIDTH],
                         y_ps[h][:, :].rearrange("p (i d) -> p i d", d=WIDTH)).then_inc(y_moved, 1)

            with act.Fori(0, BATCH) as b:
                for X in range(BLOCKS):
                    for k in range(WIDTH):
                        n, v, g = unit(X, k)
                        d = (X % GROUPS) * WIDTH + k
                        act.wait_ge(delta_ready, START + b * BU + n + 1)
                        act.wait_ge(scanned, START + b * BU + n - RING + 1)
                        act.activation(decay[n % RING][:, :], delta_ps[n % RING][:, :], ACT.Exp,
                                       scale=decay_rate[:, d:d + 1]).then_inc(decay_ready, 1)
                        if not direct[k]:
                            act.wait_ge(enter_g_ready, START + b * BLOCKS * G + g - RING + 1)
                            act.copy(copied[g % RING][:, :], delta_ps[n % RING][:, :]).then_inc(copied_ready, 1)
                        if k == slots_of(HALF - 1) + 2:
                            move_y(b * BLOCKS + X, X, 0)
                    move_y(b * BLOCKS + X, X, 1)
            for h in range(2):
                move_y(BATCH * BLOCKS, 0, h)

        @block.gpsimd
        def _(pool):
            for j in range(2):
                pool.memset(states[j][:, :, :], 0.0).then_inc(zeroed, 1)
            pool.memset(spread[:, :], 0.0).then_inc(zeroed, 1)
            pool.wait_ge(zeroed, START + 3)
            pool.memset(parts[SPLITS * WIDTH:128, :, :], 0.0).then_inc(zeroed, 1)
            pool.wait_ge(zeroed, START + 4)
            pool.memset(y_sb[:, :, :], 0.0).then_inc(zeroed, 1)

            with pool.Fori(0, BATCH) as b:
                for X in range(BLOCKS):
                    c = X // GROUPS
                    for k in range(WIDTH):
                        n, v, g = unit(X, k)
                        if n in (0, GROUPS * WIDTH):
                            pool.wait_ge(entering_in[c], START + (b + 1) * DMA)
                        if not direct[k]:
                            pool.wait_ge(copied_ready, START + b * BLOCKS * G + g + 1)
                            Xb, kb = (g - RING) // G, [i for i in range(WIDTH) if not direct[i]][(g - RING) % G]
                            pool.wait_ge(scanned, START + b * BU + Xb * WIDTH + kb + 1)
                            pool.tensor_tensor(enter_g[g % RING][:, :], copied[g % RING][:, :], entering[c][:, :],
                                               ALU.mult).then_inc(enter_g_ready, 1)

        @block.vector
        def _(dve):
            dve.memset(carry[:, :], 0.0).then_inc(carried, 1)
            for h in range(2):
                dve.memset(y_ps[h][:, :], 0.0).then_inc(y_zeroed, 1)
            dve.wait_ge(consts_in, START + 2 * DMA)
            dve.wait_ge(zeroed, START + 5)

            def product(b, X, k):
                n, v, g = unit(X, k)
                dve.wait_ge(decay_ready, START + b * BU + n + 1)
                dve.tensor_tensor(enter_v[v % 2][:, :], delta_ps[n % RING][:, :], entering[X // GROUPS][:, :],
                                  ALU.mult).then_inc(enter_v_ready, 1)

            with dve.Fori(0, BATCH) as b:
                for X in range(BLOCKS):
                    d0 = (X % GROUPS) * WIDTH
                    for k in range(WIDTH):
                        n, v, g = unit(X, k)
                        if n in (0, GROUPS * WIDTH):
                            dve.wait_ge(entering_in[n // (GROUPS * WIDTH)], START + (b + 1) * DMA)
                        Xa, ka = ahead(X, k, 1)
                        if Xa == X and direct[ka]:
                            product(b, Xa, ka)
                        if k == 0 and direct[0]:
                            product(b, X, 0)
                        if k == 0:
                            dve.wait_ge(y_half, START + (b * BLOCKS + X) * 2)
                            dve.wait_ge(carried, START + b * BLOCKS + X + 1)
                        dve.wait_ge(decay_ready, START + b * BU + n + 1)
                        if direct[k]:
                            dve.wait_ge(enter_v_ready, START + b * BLOCKS * V + v + 1)
                            enter = enter_v[v % 2]
                        else:
                            dve.wait_ge(enter_g_ready, START + b * BLOCKS * G + g + 1)
                            enter = enter_g[g % RING]
                        dve.tensor_tensor_scan(states[X % 2][:, k, :], decay[n % RING][:, :], enter[:, :],
                                               carry[:, d0 + k:d0 + k + 1], ALU.mult, ALU.add).then_inc(scanned, 1)
                    dve.wait_ge(scanned, START + b * BU + (X + 1) * WIDTH)
                    if X < GROUPS:
                        dve.tensor_copy(carry[:, d0:d0 + WIDTH], states[X % 2][:, :, BANK - 1]).then_inc(carried, 1)
                    else:
                        dve.memset(carry[:, d0:d0 + WIDTH], 0.0).then_inc(carried, 1)
                    if X % GROUPS == 0:
                        dve.wait_ge(readout_in, START + (b * CHUNKS + X // GROUPS + 1) * DMA)
                        dve.wait_ge(y_half, START + (b * BLOCKS + X + 1) * 2)
                        dve.tensor_copy(spread[:, FOLD - 1:FOLD - 1 + FOLD * BANK:FOLD], readout[:, :]
                                        ).then_inc(spread_ready, 1)


def gate_phase(nc, y_dram, z_dram, x1_dram, w_out, mean_w, identity, gate_w, gate_b, x2_dram, normed_dram, logit_dram):
    ROWS = 4 * FOLD
    SPAN = 128 // ROWS
    TILES = INNER * WIDTH * ROWS // 128 // INNER
    with ExitStack() as ctx:
        def sb(name, shape, dt=F32):
            return ctx.enter_context(nc.sbuf_tensor(name, shape, dt))

        def ps(name, rows=128):
            return ctx.enter_context(nc.psum_tensor(name, [rows, BANK], F32))

        sem = Semaphores(nc, ctx, "gate")
        wout, wmean, ident = sb("wout", [INNER, CH]), sb("g_wmean", [128, 128]), sb("g_ident", [128, 128])
        wgate, bgate = sb("wgate", [128, CHUNKS, EXPERTS]), sb("bgate", [CHUNKS * EXPERTS, 1])
        eps = sb("g_eps", [128, 1])
        y = [sb(f"g_y{i}", [128, CHUNKS, TILES, INNER]) for i in range(2)]
        z = [sb(f"g_z{i}", [INNER, CHUNKS, BANK]) for i in range(2)]
        x1 = [sb(f"g_x1{i}", [128, BANK]) for i in range(2)]
        swish, gated = sb("swish", [INNER, CHUNKS, BANK]), sb("gated", [INNER, CHUNKS, BANK])
        x2 = [sb(f"g_x2{i}", [128, BANK]) for i in range(2)]
        centred, square, std = sb("g_centred", [128, BANK]), sb("g_square", [128, BANK]), sb("g_std", [128, BANK])
        normed = [sb(f"g_normed{i}", [128, BANK]) for i in range(2)]
        logits = [sb(f"g_logits{i}", [CHUNKS * EXPERTS, BANK]) for i in range(2)]
        turned_ps = [ps(f"turned_ps{c}") for c in range(CHUNKS)]
        out_ps, mean_ps, var_ps, logit_ps = ps("out_ps"), ps("g_mean_ps"), ps("g_var_ps"), ps("logit_ps")

        weights_in, eps_set = sem("weights_in"), sem("eps_set")
        loaded = [sem(f"loaded{i}") for i in range(2)]
        stored = [sem(f"stored{i}") for i in range(2)]
        turned, swish_ready, gated_ready, out_ready, x2_ready = (
            sem("turned"), sem("swish"), sem("gated"), sem("out"), sem("x2"))
        mean_ready, centred_ready, square_ready, var_ready, std_ready = (
            sem("mean"), sem("centred"), sem("square"), sem("var"), sem("std"))
        inverse_ready, normed_ready, logit_ready, logits_ready = (
            sem("inverse"), sem("normed"), sem("logit"), sem("logits"))
        LOADS, STORES = 2 + CHUNKS, 3 * CHUNKS
        passed = sem("passed")
        block = ctx.enter_context(nc.Block())

        @block.sync
        def _(sp):
            for s in sem.made:
                sp.sem_inc(s, START)
            for d, s in ((wout, w_out), (wmean, mean_w), (ident, identity), (bgate, gate_b)):
                sp.dma_start(d[:, :], s).then_inc(weights_in, DMA)
            sp.dma_start(wgate[:, :, :], gate_w).then_inc(weights_in, DMA)

            def load(b, i, turn):
                if not (isinstance(b, int) and b == 0):
                    sp.wait_ge(x2_ready, START + b - 1)
                sp.dma_start(y[i][:, :, :, :], y_dram[bass.ds(b * CHUNKS + 1, CHUNKS), :, :].rearrange(
                    "n r (s t d) -> (r s) n t d", s=SPAN, d=INNER)).then_inc(loaded[i], DMA)
                sp.dma_start(z[i][:, :, :], z_dram[bass.ds(b * CHUNKS, CHUNKS), :, :].rearrange("n p l -> p n l")
                             ).then_inc(loaded[i], DMA)
                for c in range(CHUNKS):
                    sp.dma_start(x1[i][CH * c:CH * c + CH, :],
                                 x1_dram[bass.ds(b, 1), :, BANK * c:BANK * c + BANK].rearrange("b c l -> (b c) l")
                                 ).then_inc(loaded[i], DMA)

            def store(b, i, turn):
                for ready, tile, dram, height in ((x2_ready, x2, x2_dram, CH), (normed_ready, normed, normed_dram, CH),
                                                  (logits_ready, logits, logit_dram, EXPERTS)):
                    sp.wait_ge(ready, START + b + 1)
                    for c in range(CHUNKS):
                        sp.dma_start(dram[bass.ds(b, 1), :, BANK * c:BANK * c + BANK].rearrange("b c l -> (b c) l"),
                                     tile[i][height * c:height * c + height, :]).then_inc(stored[i], DMA)

            load_ahead(sp, load, store)
            for i in range(2):
                sp.wait_ge(stored[i], START + BATCH // 2 * STORES * DMA)

        @block.tensor
        def _(pe):
            pe.wait_ge(weights_in, START + 5 * DMA)

            def turn_y(b, i, turn):
                pe.wait_ge(loaded[i], START + (turn + 1) * LOADS * DMA)
                for c in range(CHUNKS):
                    pe.wait_ge(gated_ready, START + b * CHUNKS)
                    for t in range(TILES):
                        mm = pe.transpose(turned_ps[c][:, 128 * t:128 * t + 128], y[i][:, c, t, :], ident[:, :])
                    mm.then_inc(turned, 1)

            def project_out(b, i, turn):
                pe.wait_ge(x2_ready, START + b)
                for c in range(CHUNKS):
                    pe.wait_ge(gated_ready, START + b * CHUNKS + c + 1)
                    pe.sem_inc(passed, 1)
                    mm = pe.matmul(out_ps[CH * c:CH * c + CH, :], wout[:, :], gated[:, c, :], start=True, stop=True)
                mm.then_inc(out_ready, 1)

            def mean(b, i, turn):
                pe.wait_ge(x2_ready, START + b + 1)
                pe.wait_ge(centred_ready, START + b)
                pe.matmul(mean_ps[:, :], wmean[:, :], x2[i][:, :], start=True, stop=True).then_inc(mean_ready, 1)

            def variance(b, i, turn):
                pe.wait_ge(square_ready, START + b + 1)
                pe.wait_ge(std_ready, START + b)
                pe.matmul(var_ps[:, :], wmean[:, :], square[:, :], start=True, stop=True).then_inc(var_ready, 1)

            def score(b, i, turn):
                pe.wait_ge(normed_ready, START + b + 1)
                pe.wait_ge(logits_ready, START + b)
                for c in range(CHUNKS):
                    mm = pe.matmul(logit_ps[EXPERTS * c:EXPERTS * c + EXPERTS, :], wgate[:, c, :], normed[i][:, :],
                                   start=True, stop=True)
                mm.then_inc(logit_ready, 1)

            in_pairs(pe, (0, turn_y), (1, mean), (0, project_out), (1, variance), (1, score))

        @block.scalar
        def _(act):
            act.wait_ge(eps_set, START + 1)
            act.wait_ge(weights_in, START + 5 * DMA)

            def gate_values(b, i, turn):
                act.wait_ge(loaded[i], START + (turn + 1) * LOADS * DMA)
                act.wait_ge(gated_ready, START + b * CHUNKS)
                act.activation(swish[:, :, :], z[i][:, :, :], ACT.Silu).then_inc(swish_ready, 1)

            def deviation(b, i, turn):
                act.wait_ge(var_ready, START + b + 1)
                act.wait_ge(normed_ready, START + b)
                act.activation(std[:, :], var_ps[:, :], ACT.Sqrt, bias=eps[:, :]).then_inc(std_ready, 1)

            def add_bias(b, i, turn):
                act.wait_ge(logit_ready, START + b + 1)
                act.wait_ge(stored[i], START + turn * STORES * DMA)
                act.activation(logits[i][:, :], logit_ps[0:CHUNKS * EXPERTS, :], ACT.Identity, bias=bgate[:, :]
                               ).then_inc(logits_ready, 1)

            in_pairs(act, (0, gate_values), (1, deviation), (1, add_bias))

        @block.gpsimd
        def _(pool):
            pool.memset(eps[:, :], 1e-5).then_inc(eps_set, 1)
            with pool.Fori(0, BATCH) as b:
                pool.wait_ge(centred_ready, START + b + 1)
                pool.wait_ge(var_ready, START + b)
                pool.tensor_tensor(square[:, :], centred[:, :], centred[:, :], ALU.mult).then_inc(square_ready, 1)

        @block.vector
        def _(dve):
            def gate(b, i, turn):
                dve.wait_ge(swish_ready, START + b + 1)
                dve.wait_ge(out_ready, START + b)
                for c in range(CHUNKS):
                    dve.wait_ge(turned, START + b * CHUNKS + c + 1)
                    order = turned_ps[c][:, :].rearrange("p (t r s) -> p s t r", t=TILES, s=SPAN)
                    dve.tensor_tensor(gated[:, c, :].rearrange("p (s t r) -> p s t r", s=SPAN, t=TILES), order,
                                      swish[:, c, :].rearrange("p (s t r) -> p s t r", s=SPAN, t=TILES),
                                      ALU.mult).then_inc(gated_ready, 1)

            def residual(b, i, turn):
                dve.wait_ge(out_ready, START + b + 1)
                dve.wait_ge(stored[i], START + turn * STORES * DMA)
                dve.tensor_tensor(x2[i][:, :], out_ps[:, :], x1[i][:, :], ALU.add).then_inc(x2_ready, 1)

            def centre(b, i, turn):
                dve.wait_ge(mean_ready, START + b + 1)
                dve.wait_ge(normed_ready, START + b)
                dve.tensor_tensor(centred[:, :], x2[i][:, :], mean_ps[:, :], ALU.subtract).then_inc(centred_ready, 1)

            def normalise(b, i, turn):
                dve.wait_ge(std_ready, START + b + 1)
                dve.reciprocal(std[:, :], std[:, :]).then_inc(inverse_ready, 1)
                dve.wait_ge(inverse_ready, START + b + 1)
                dve.tensor_tensor(normed[i][:, :], centred[:, :], std[:, :], ALU.mult).then_inc(normed_ready, 1)

            in_pairs(dve, (0, gate), (1, centre), (0, residual), (1, normalise))


QUADS = BATCH // GROUP


def expert_phase(nc, logit_dram, normed_dram, x2_dram, identity, weight1, weight2, expert_dram, out_dram):
    TILES = LEN // 128
    ROWS1 = CH + 1
    with ExitStack() as ctx:
        def sb(name, shape, dt=F32):
            return ctx.enter_context(nc.sbuf_tensor(name, shape, dt))

        sem = Semaphores(nc, ctx, "expert")
        ident = sb("e_ident", [128, 128])
        w1 = sb("w1", [ROWS1, EXPERTS, HIDDEN])
        w2 = sb("w2", [128, HIDDEN // 128, EXPERTS, CH])
        w2_bias = sb("w2_bias", [1, EXPERTS, CH])
        ones = sb("ones", [1, BATCH])
        logits = [sb(f"e_logits{i}", [128, LEN]) for i in range(2)]
        probs = [sb(f"probs{i}", [128, LEN]) for i in range(2)]
        marked = [sb(f"marked{i}", [128, LEN]) for i in range(2)]
        chosen = [sb(f"chosen{q}", [128, LEN]) for q in range(QUADS)]
        tops = sb("tops", [128, QUADS, TOPK])
        best = sb("best", [128, QUADS, TOPK])
        minus = sb("minus", [128, QUADS])
        total = sb("total", [128, QUADS])
        share = sb("share", [128, QUADS])
        chosen_t = sb("chosen_t", [128, TILES, 128])
        normed = [sb(f"e_normed{i}", [CH, LEN]) for i in range(2)]
        normed_t = [sb(f"normed_t{i}", [128, TILES, CH]) for i in range(2)]
        pooled = sb("pooled", [ROWS1, BATCH, EXPERTS])
        hidden = sb("hidden", [128, EXPERTS, HIDDEN // 128, BATCH])
        results = sb("results", [BATCH, EXPERTS, CH])
        spread = sb("e_spread", [128, QUADS, GROUP, CH])
        x2 = [sb(f"e_x2{i}", [CH, BANK]) for i in range(2)]
        final = [sb(f"final{i}", [CH, BANK]) for i in range(2)]
        chosen_ps = ctx.enter_context(nc.psum_tensor("chosen_ps", [128, TILES, 128], F32))
        normed_ps = ctx.enter_context(nc.psum_tensor("normed_ps", [128, TILES, CH], F32))
        pooled_ps = ctx.enter_context(nc.psum_tensor("pooled_ps", [CH, BANK], F32))
        work_ps = ctx.enter_context(nc.psum_tensor("work_ps", [128, 4, BANK], F32))

        consts_in, weights_in, ones_set, spread_zeroed = (
            sem("consts_in"), sem("weights_in"), sem("ones_set"), sem("spread_zeroed"))
        logits_in = [sem(f"logits_in{i}") for i in range(2)]
        normed_in = [sem(f"normed_in{i}") for i in range(2)]
        top_ready, minus_ready, exp_ready, share_ready, probs_ready = (
            sem("top"), sem("minus"), sem("exp"), sem("share"), sem("probs"))
        best_ready, marked_ready, chosen_ready = sem("best"), sem("marked"), sem("chosen")
        chosen_turned, chosen_t_ready, normed_turned, normed_t_ready = (
            sem("chosen_turned"), sem("chosen_t"), sem("normed_turned"), sem("normed_t"))
        pooled_summed, pooled_ready = sem("pooled_summed"), sem("pooled")
        hidden_summed, hidden_ready, results_summed, results_ready = (
            sem("hidden_summed"), sem("hidden"), sem("results_summed"), sem("results"))
        results_out, spread_in = sem("results_out"), sem("spread_in")
        x2_in = [sem(f"x2_in{i}") for i in range(2)]
        scattered, final_ready = sem("scattered"), sem("final")
        stored = [sem(f"stored{i}") for i in range(2)]
        PIECES = BATCH * CHUNKS
        block = ctx.enter_context(nc.Block())

        @block.sync
        def _(sp):
            sp.dma_start(ident[:, :], identity).then_inc(consts_in, DMA)
            for q in range(QUADS):
                if q >= 2:
                    sp.wait_ge(probs_ready, q - 1)
                sp.dma_start(logits[q % 2][:, :], logit_dram[GROUP * q:GROUP * q + GROUP, :, :].rearrange(
                    "b e l -> (b e) l")).then_inc(logits_in[q % 2], DMA)
                if q == 0:
                    sp.dma_start(w1[:, :, :], weight1.rearrange("e d h -> d e h")).then_inc(weights_in, DMA)
                    for h in range(2):
                        sp.dma_start(w2[:, h, :, :], weight2[:, 128 * h:128 * h + 128, :].rearrange("e h o -> h e o")
                                     ).then_inc(weights_in, DMA)
                    sp.dma_start(w2_bias[:, :, :], weight2[:, HIDDEN:HIDDEN + 1, :].rearrange("e h o -> h e o")
                                 ).then_inc(weights_in, DMA)
                for i in range(GROUP):
                    b = q * GROUP + i
                    if b >= 2:
                        sp.wait_ge(normed_turned, b - 1)
                    sp.dma_start(normed[b % 2][:, :], normed_dram[b, :, :]).then_inc(normed_in[b % 2], DMA)
            sp.wait_ge(results_ready, 4)
            sp.dma_start(expert_dram, results[:, :, :]).then_inc(results_out, DMA)
            sp.wait_ge(results_out, DMA)
            sp.wait_ge(spread_zeroed, 1)
            for i in range(GROUP):
                sp.dma_start(spread[EXPERTS * i:EXPERTS * i + EXPERTS, :, i, :],
                             expert_dram.rearrange("(q i) e o -> i e q o", i=GROUP)[i, :, :, :]).then_inc(spread_in, DMA)
            for n in range(PIECES + 2):
                if n < PIECES:
                    b, c = n // CHUNKS, n % CHUNKS
                    if n >= 2:
                        sp.wait_ge(final_ready, n - 1)
                    sp.dma_start(x2[n % 2][:, :], x2_dram[b, :, BANK * c:BANK * c + BANK]).then_inc(x2_in[n % 2], DMA)
                if n >= 2:
                    b, c = (n - 2) // CHUNKS, n % CHUNKS
                    sp.wait_ge(final_ready, n - 1)
                    sp.dma_start(out_dram[b, :, BANK * c:BANK * c + BANK], final[n % 2][:, :]).then_inc(stored[n % 2], DMA)
            for i in range(2):
                sp.wait_ge(stored[i], PIECES // 2 * DMA)

        @block.tensor
        def _(pe):
            pe.wait_ge(consts_in, DMA)
            for q in range(QUADS):
                pe.wait_ge(chosen_ready, q + 1)
                if q:
                    pe.wait_ge(chosen_t_ready, q)
                for t in range(TILES):
                    mm = pe.transpose(chosen_ps[:, t, :], chosen[q][:, 128 * t:128 * t + 128], ident[:, :])
                mm.then_inc(chosen_turned, 1)
                for i in range(GROUP):
                    b = q * GROUP + i
                    pe.wait_ge(normed_in[b % 2], (b // 2 + 1) * DMA)
                    if b:
                        pe.wait_ge(normed_t_ready, b)
                    for t in range(TILES):
                        mm = pe.transpose(normed_ps[:, t, :], normed[b % 2][:, 128 * t:128 * t + 128], ident[0:CH, 0:CH])
                    mm.then_inc(normed_turned, 1)
                    if i == 0:
                        pe.wait_ge(chosen_t_ready, q + 1)
                    pe.wait_ge(normed_t_ready, b + 1)
                    if b:
                        pe.wait_ge(pooled_ready, b)
                    for t in range(TILES):
                        mm = pe.matmul(pooled_ps[:, 0:EXPERTS], normed_t[b % 2][:, t, :],
                                       chosen_t[:, t, EXPERTS * i:EXPERTS * i + EXPERTS],
                                       start=(t == 0), stop=(t == TILES - 1))
                    mm.then_inc(pooled_summed, 1)
            pe.wait_ge(weights_in, 4 * DMA)
            pe.wait_ge(ones_set, 2)
            pe.wait_ge(pooled_ready, BATCH)
            for e in range(EXPERTS):
                for h in range(2):
                    at = (e % 16 * 2 + h) * BATCH
                    mm = pe.matmul(work_ps[:, e // 16, at:at + BATCH], w1[:, e, 128 * h:128 * h + 128],
                                   pooled[:, :, e], start=True, stop=True)
                if e % 16 == 15:
                    mm.then_inc(hidden_summed, 1)
            for e in range(EXPERTS):
                if e % 16 == 0:
                    pe.wait_ge(hidden_ready, 2)
                out = work_ps[0:BATCH, e // 8, e % 8 * CH:e % 8 * CH + CH]
                for h in range(2):
                    pe.matmul(out, hidden[:, e, h, :], w2[:, h, e, :], start=(h == 0), stop=False)
                mm = pe.matmul(out, ones[:, :], w2_bias[:, e, :], start=False, stop=True)
                if e % 8 == 7:
                    mm.then_inc(results_summed, 1)
            pe.wait_ge(spread_in, GROUP * DMA)
            pe.wait_ge(results_ready, 4)
            for n in range(PIECES):
                b, c = n // CHUNKS, n % CHUNKS
                if n >= 4:
                    pe.wait_ge(final_ready, n - 3)
                pe.matmul(work_ps[0:CH, n % 4, :], spread[:, b // GROUP, b % GROUP, :],
                          chosen[b // GROUP][:, BANK * c:BANK * c + BANK], start=True, stop=True).then_inc(scattered, 1)

        @block.scalar
        def _(act):
            for q in range(QUADS):
                act.wait_ge(minus_ready, q + 1)
                if q >= 2:
                    act.wait_ge(chosen_ready, q - 1)
                act.activation(probs[q % 2][:, :], logits[q % 2][:, :], ACT.Exp, bias=minus[:, q:q + 1],
                               accum_out=total[:, q:q + 1]).then_inc(exp_ready, 1)
                act.wait_ge(chosen_turned, q + 1)
                if q:
                    act.wait_ge(pooled_summed, GROUP * q)
                act.copy(chosen_t[:, 0:4, :], chosen_ps[:, 0:4, :])
                act.copy(chosen_t[:, 4:8, :], chosen_ps[:, 4:8, :]).then_inc(chosen_t_ready, 1)
                for i in range(GROUP):
                    b = q * GROUP + i
                    act.wait_ge(normed_turned, b + 1)
                    if b >= 2:
                        act.wait_ge(pooled_summed, b - 1)
                    act.copy(normed_t[b % 2][:, :, :], normed_ps[:, :, :]).then_inc(normed_t_ready, 1)
            for h in range(2):
                act.wait_ge(hidden_summed, h + 1)
                act.activation(hidden[:, 16 * h:16 * h + 16, :, :].rearrange("p e h b -> p (e h b)"),
                               work_ps[:, h, :], ACT.Gelu).then_inc(hidden_ready, 1)

        @block.gpsimd
        def _(pool):
            pool.memset(ones[:, :], 1.0).then_inc(ones_set, 1)
            pool.memset(spread[:, :, :, :], 0.0).then_inc(spread_zeroed, 1)

        @block.vector
        def _(dve):
            def top(q):
                dve.wait_ge(logits_in[q % 2], (q // 2 + 1) * DMA)
                dve.max(tops[:, q, :], logits[q % 2][:, :]).then_inc(top_ready, 1)
                dve.wait_ge(top_ready, q + 1)
                dve.tensor_scalar(minus[:, q:q + 1], tops[:, q, 0:1], -1.0, None, ALU.mult).then_inc(minus_ready, 1)

            def choose(q):
                dve.wait_ge(exp_ready, q + 1)
                dve.reciprocal(share[:, q:q + 1], total[:, q:q + 1]).then_inc(share_ready, 1)
                dve.wait_ge(share_ready, q + 1)
                dve.tensor_scalar(probs[q % 2][:, :], probs[q % 2][:, :], share[:, q:q + 1], None,
                                  ALU.mult).then_inc(probs_ready, 1)
                dve.wait_ge(probs_ready, q + 1)
                dve.max(best[:, q, :], probs[q % 2][:, :]).then_inc(best_ready, 1)
                dve.wait_ge(best_ready, q + 1)
                dve.match_replace(out=marked[q % 2][:, :], in_to_replace=best[:, q, :], in_values=probs[q % 2][:, :],
                                  imm_value=-1.0).then_inc(marked_ready, 1)
                dve.wait_ge(marked_ready, q + 1)
                dve.scalar_tensor_tensor(out=chosen[q][:, :], in0=marked[q % 2][:, :], scalar=-1.0,
                                         in1=probs[q % 2][:, :], op0=ALU.is_equal, op1=ALU.mult
                                         ).then_inc(chosen_ready, 1)

            dve.memset(pooled[CH:ROWS1, :, :], 1.0).then_inc(ones_set, 1)
            top(0)
            for q in range(QUADS):
                choose(q)
                if q + 1 < QUADS:
                    top(q + 1)
                for i in range(GROUP):
                    b = q * GROUP + i
                    dve.wait_ge(pooled_summed, b + 1)
                    dve.tensor_copy(pooled[0:CH, b, :], pooled_ps[:, 0:EXPERTS]).then_inc(pooled_ready, 1)
            for h in range(4):
                dve.wait_ge(results_summed, h + 1)
                dve.tensor_copy(results[:, 8 * h:8 * h + 8, :].rearrange("p e o -> p (e o)"),
                                work_ps[0:BATCH, h, :]).then_inc(results_ready, 1)
            for n in range(PIECES):
                dve.wait_ge(scattered, n + 1)
                dve.wait_ge(x2_in[n % 2], (n // 2 + 1) * DMA)
                if n >= 2:
                    dve.wait_ge(stored[n % 2], (n // 2) * DMA)
                dve.tensor_tensor(final[n % 2][:, :], work_ps[0:CH, n % 4, :], x2[n % 2][:, :],
                                  ALU.add).then_inc(final_ready, 1)


def kernel(**inputs):
    import numpy as np
    from ml_dtypes import bfloat16
    import concourse.bacc as bacc
    from concourse.bass_utils import run_bass_kernel_spmd

    x = np.asarray(inputs["x"])
    f32 = np.float32
    arrays = {"x_pad": np.pad(x, ((0, 0), (0, 0), (0, 0), (0, PITCH - SIDE))).reshape(BATCH, CH, IMG)}
    i2s = np.asarray(inputs["L0_conv_w_i2s"])
    skip = np.asarray(inputs["L0_conv_w_skip"])
    for side in ("left", "right"):
        w = np.asarray(inputs[f"L0_conv_w_{side}"])
        arrays[f"w_{side}"] = np.concatenate([w[:, :, 0].T, w[:, :, 1].T, i2s.T], 0)
        arrays[f"bias_{side}"] = np.tile(np.asarray(inputs[f"L0_conv_b_{side}"]).reshape(4, FEAT).T, (GROUP, 1))
        rows = np.zeros((128, CH), f32)
        at = FEAT if side == "left" else 0
        rows[at:at + FEAT] = skip.T
        arrays[f"w_skip_{side}"] = rows
    arrays["b_skip"] = np.asarray(inputs["L0_conv_b_skip"]).reshape(CH, 1)
    for name in ("W_delta", "W_B", "W_C", "W_out"):
        arrays[name] = np.asarray(inputs[f"L1_attn_{name}"])
    w_in = np.asarray(inputs["L1_attn_W_in"])
    arrays["W_in"] = np.stack([np.pad(w_in, ((CH * c, CH * (CHUNKS - 1 - c)), (0, 0))) for c in range(CHUNKS)])
    arrays["A_t"] = np.asarray(inputs["L1_attn_A"]).T
    gate_w = np.asarray(inputs["L1_ffn_gate_w"]).T
    arrays["gate_w"] = np.stack([np.pad(gate_w, ((CH * c, CH * (CHUNKS - 1 - c)), (0, 0))) for c in range(CHUNKS)], 1)
    arrays["gate_b"] = np.tile(np.asarray(inputs["L1_ffn_gate_b"]), CHUNKS).reshape(CHUNKS * EXPERTS, 1)
    arrays["weight1"] = np.asarray(inputs["L1_ffn_weight1"])
    arrays["weight2"] = np.asarray(inputs["L1_ffn_weight2"])
    arrays["mean_w"] = np.kron(np.eye(2, dtype=f32), np.full((CH, CH), 1.0 / CH, f32))
    arrays["identity"] = np.eye(128, dtype=f32)
    arrays["selectors"] = np.pad(
        np.tile(np.eye(WIDTH, dtype=f32)[:, :, None], (SPLITS, 1, STATE)),
        ((0, 128 - SPLITS * WIDTH), (0, 0), (0, 0))).astype(bfloat16)
    arrays = {k: np.ascontiguousarray(v) for k, v in arrays.items()}

    nc = bacc.Bacc("TRN2", target_bir_lowering=False, num_devices=1)
    a = {k: nc.dram_tensor(k, v.shape, mybir.dt.from_np(v.dtype), kind="ExternalInput").ap()
         for k, v in arrays.items()}
    out = nc.dram_tensor("out", (BATCH, CH, LEN), F32, kind="ExternalOutput").ap()

    def scratch(name, shape, dt=F32):
        return nc.dram_tensor(name, shape, dt, kind="Internal").ap()

    x1 = scratch("x1_dram", (BATCH, CH, LEN))
    delta = scratch("delta_dram", (PAIRS, SPLITS, INNER, BANK), BF16)
    entering = scratch("input_dram", (PAIRS, STATE, BANK))
    readout = scratch("readout_dram", (PAIRS, STATE, BANK))
    z = scratch("z_dram", (PAIRS, INNER, BANK))
    y = scratch("y_dram", (PAIRS + 1, 4 * FOLD, WIDTH * INNER))
    x2 = scratch("x2_dram", (BATCH, CH, LEN))
    normed = scratch("normed_dram", (BATCH, CH, LEN))
    logits = scratch("logit_dram", (BATCH, EXPERTS, LEN))
    experts = scratch("expert_dram", (BATCH, EXPERTS, CH))

    conv_phase(nc, a["x_pad"], a["w_left"], a["w_right"], a["bias_left"], a["bias_right"],
               a["w_skip_left"], a["w_skip_right"], a["b_skip"], x1)
    project_phase(nc, x1, a["W_in"], a["W_delta"], a["W_B"], a["W_C"], a["mean_w"], delta, entering, readout, z)
    scan_phase(nc, delta, entering, readout, a["A_t"], a["selectors"], y)
    gate_phase(nc, y, z, x1, a["W_out"], a["mean_w"], a["identity"], a["gate_w"], a["gate_b"], x2, normed, logits)
    expert_phase(nc, logits, normed, x2, a["identity"], a["weight1"], a["weight2"], experts, out)

    r = run_bass_kernel_spmd(nc, [arrays], core_ids=[0])
    return r.results[0]["out"].reshape(BATCH, CH, SIDE, SIDE)
```

```python
from contextlib import ExitStack

import concourse.bass as bass
from concourse import mybir

F32 = mybir.dt.float32
BF16 = mybir.dt.bfloat16
ALU = mybir.AluOpType
ACT = mybir.ActivationFunctionType
AX = mybir.AxisListType

BATCH = 16
CH = 64
SIDE = 32
LEN = SIDE * SIDE
FEAT = CH // 2
STEPS = SIDE
INNER = 128
STATE = 128
EXPERTS = 32
TOPK = 8
HIDDEN = 256
BANK = 512
DMA = 16
START = 16

OUT_RING = 4
GROUP = 4
PITCH = SIDE + 1
IMG = SIDE * PITCH
MARGIN = 2
RW = MARGIN + IMG + 2
GATE_RING = 4
STREAMS = 4
ROUNDS = BATCH // (2 * GROUP)
CHUNKS = LEN // BANK
CROWS = BANK // SIDE
CIMG = CROWS * PITCH


class Semaphores:

    def __init__(self, nc, ctx, phase):
        self.nc, self.ctx, self.phase, self.made = nc, ctx, phase, []

    def __call__(self, name):
        self.made.append(self.ctx.enter_context(self.nc.semaphore(f"{self.phase}_{name}")))
        return self.made[-1]


def conv_phase(nc, x_pad, w_left, w_right, bias_left, bias_right, w_skip_left, w_skip_right, b_skip, x1_dram):
    with ExitStack() as ctx:
        def sb(name, shape, dt=F32):
            return ctx.enter_context(nc.sbuf_tensor(name, shape, dt))

        sem = Semaphores(nc, ctx, "conv")
        rows = [sb(f"rows{s}", [128, GROUP, RW]) for s in range(STREAMS)]
        feat = [sb(f"feat{s}", [128, IMG]) for s in range(STREAMS)]
        cell = [sb(f"cell{s}", [128, LEN]) for s in range(STREAMS)]
        gates = [sb(f"gates{i}", [128, 4, BANK]) for i in range(GATE_RING)]
        forgot = [sb(f"forgot{c}", [128, BANK]) for c in range(CHUNKS)]
        entered = [sb(f"entered{c}", [128, BANK]) for c in range(CHUNKS)]
        squashed = [sb(f"squashed{c}", [128, BANK]) for c in range(CHUNKS)]
        weights = [sb("weights_left", [128, 128]), sb("weights_right", [128, 128])]
        biases = [sb("biases_left", [128, 4]), sb("biases_right", [128, 4])]
        skip_w = [sb("skip_w_left", [128, CH]), sb("skip_w_right", [128, CH])]
        skip_b = sb("skip_b", [128, 1])
        x1 = [sb(f"x1_{i}", [128, BANK]) for i in range(OUT_RING)]
        pre = [ctx.enter_context(nc.psum_tensor(f"pre{c}", [128, 4, BANK], F32)) for c in range(CHUNKS)]

        weights_in, zeroed, state_zeroed = sem("weights_in"), sem("zeroed"), sem("state_zeroed")
        x_in = [sem(f"x_in{s}") for s in range(STREAMS)]
        pre_ready, gates_ready, forgot_ready, entered_ready = (
            sem("pre_ready"), sem("gates_ready"), sem("forgot_ready"), sem("entered_ready"))
        cell_ready, squashed_ready, feat_ready = sem("cell_ready"), sem("squashed_ready"), sem("feat_ready")
        rows_in = [sem(f"rows_in{s}") for s in range(STREAMS)]
        skip_ready, x1_ready = sem("skip_ready"), sem("x1_ready")
        x1_out = [sem(f"x1_out{i}") for i in range(OUT_RING)]
        passed = sem("passed")
        block = ctx.enter_context(nc.Block())

        def side(s):
            return s // 2

        def half(s):
            return s % 2

        SLOTS = STREAMS * CHUNKS
        SKIPS = 2 * GROUP * CHUNKS

        def image(tile, at):
            return tile[..., at:at + CIMG].rearrange("p (h w) -> p h w", w=PITCH)[:, :, 0:SIDE]

        above = [(PITCH + 1, IMG - PITCH - 1), (PITCH - 1, IMG - PITCH + 1)]
        same = [(1, IMG), (-1, IMG)]
        MOVES = 2 * GROUP

        @block.sync
        def _(sp):
            for s in sem.made:
                sp.sem_inc(s, START)
            for d, s in ((weights[0], w_left), (weights[1], w_right), (biases[0], bias_left),
                         (biases[1], bias_right), (skip_w[0], w_skip_left), (skip_w[1], w_skip_right)):
                sp.dma_start(d[:, :], s).then_inc(weights_in, DMA)
            sp.dma_start(skip_b[CH:128, :], b_skip).then_inc(weights_in, DMA)
            sp.wait_ge(zeroed, START + 2)
            with sp.Fori(0, ROUNDS) as r:
                for s in (0, 2, 1, 3):
                    sp.wait_ge(x1_ready, START + r * SKIPS - (1 - half(s)) * SKIPS // 2)
                    src = x_pad[bass.ds((r * 2 + half(s)) * GROUP, GROUP), :, :].rearrange("q c p -> c q p")
                    sp.dma_start(rows[s][CH:128, :, MARGIN:MARGIN + IMG], src).then_inc(x_in[s], DMA)
                with sp.Fori(0, STEPS) as t:
                    for s in range(STREAMS):
                        sp.wait_ge(feat_ready, START + (r * STEPS + t) * SLOTS + CHUNKS * (s + 1))
                        for q in range(GROUP):
                            for part, (to, n) in ((0, above[side(s)]), (1, same[side(s)])):
                                sp.dma_start(rows[s][32 * part:32 * part + 32, q, MARGIN + to:MARGIN + to + n],
                                             feat[s][32 * q:32 * q + 32, 0:n]).then_inc(rows_in[s], DMA)
                for k in range(SKIPS):
                    h, q, c = k // (GROUP * CHUNKS), k // CHUNKS % GROUP, k % CHUNKS
                    sp.wait_ge(x1_ready, START + r * SKIPS + k + 1)
                    dst = x1_dram[bass.ds((r * 2 + h) * GROUP + q, 1), :, BANK * c:BANK * c + BANK]
                    sp.dma_start(dst.rearrange("b c l -> (b c) l"), x1[k % OUT_RING][CH:128, :]
                                 ).then_inc(x1_out[k % OUT_RING], DMA)
            for i in range(OUT_RING):
                sp.wait_ge(x1_out[i], START + ROUNDS * SKIPS // OUT_RING * DMA)

        @block.tensor
        def _(pe):
            pe.wait_ge(weights_in, START + 7 * DMA)
            with pe.Fori(0, ROUNDS) as r:
                pe.wait_ge(state_zeroed, START + (r + 1) * 2)
                pe.sem_inc(passed, 1)
                with pe.Fori(0, STEPS) as t:
                    for s in range(STREAMS):
                        pe.wait_ge(rows_in[s], START + (r * STEPS + t) * MOVES * DMA)
                        pe.wait_ge(x_in[s], START + (r + 1) * DMA)
                        for c in range(CHUNKS):
                            k = s * CHUNKS + c
                            pe.wait_ge(gates_ready, START + (r * STEPS + t) * SLOTS + k - CHUNKS + 1)
                            for g in range(4):
                                for q in range(GROUP):
                                    mm = pe.matmul(pre[c][32 * q:32 * q + 32, g, :],
                                                   weights[side(s)][:, 32 * g:32 * g + 32],
                                                   image(rows[s][:, q, :], MARGIN + CIMG * c),
                                                   start=True, stop=True)
                            mm.then_inc(pre_ready, 1)
                pe.wait_ge(gates_ready, START + (r + 1) * STEPS * SLOTS)
                for k in range(SKIPS):
                    h, q, c = k // (GROUP * CHUNKS), k // CHUNKS % GROUP, k % CHUNKS
                    if q == 0 and c == 0:
                        for s in (h, 2 + h):
                            pe.wait_ge(rows_in[s], START + (r + 1) * STEPS * MOVES * DMA)
                    if k >= 4:
                        pe.wait_ge(x1_ready, START + r * SKIPS + k - 3)
                    out = pre[k // 2 % 2][CH:128, k % 2, :]
                    pe.matmul(out, skip_w[0][:, :], image(rows[h][:, q, :], MARGIN + 1 + CIMG * c),
                              start=True, stop=False)
                    pe.matmul(out, skip_w[1][:, :], image(rows[2 + h][:, q, :], MARGIN - 1 + CIMG * c),
                              start=False, stop=True).then_inc(skip_ready, 1)

        def slot(r, t, k):
            return START + (r * STEPS + t) * SLOTS + k + 1

        def steps(eng, r, first, body):
            first(0)
            with eng.Fori(0, STEPS - 1) as t:
                for k in range(SLOTS):
                    body(t, k, True)
            for k in range(SLOTS):
                body(STEPS - 1, k, k + 1 < SLOTS)

        @block.scalar
        def _(act):
            act.wait_ge(weights_in, START + 7 * DMA)

            def gate_values(r, t, k):
                act.wait_ge(pre_ready, slot(r, t, k))
                act.wait_ge(feat_ready, slot(r, t, k - GATE_RING))
                for g in range(4):
                    a = act.activation(gates[k % GATE_RING][:, g, :], pre[k % CHUNKS][:, g, :], ACT.Sigmoid,
                                       bias=biases[side(k // CHUNKS)][:, g:g + 1])
                a.then_inc(gates_ready, 1)

            def squash(r, t, k):
                c, s = k % CHUNKS, k // CHUNKS
                act.wait_ge(cell_ready, slot(r, t, k))
                act.activation(squashed[c][:, :], cell[s][:, BANK * c:BANK * c + BANK],
                               ACT.Tanh).then_inc(squashed_ready, 1)

            with act.Fori(0, ROUNDS) as r:
                def body(t, k, following):
                    if following:
                        gate_values(r, t + (k + 1) // SLOTS, (k + 1) % SLOTS)
                    squash(r, t, k)

                steps(act, r, lambda t: gate_values(r, t, 0), body)

        @block.gpsimd
        def _(pool):
            for s in range(2):
                pool.memset(rows[s][:, :, :], 0.0)
                z = pool.memset(feat[s][:, :], 0.0)
            z.then_inc(zeroed, 1)
            pool.wait_ge(zeroed, START + 2)
            with pool.Fori(0, ROUNDS) as r:
                pool.wait_ge(x1_ready, START + r * SKIPS - SKIPS // 2)
                pool.sem_inc(passed, 1)
                for s in (0, 2):
                    pool.memset(rows[s][0:CH, :, :], 0.0)
                pool.wait_ge(x1_ready, START + r * SKIPS)
                pool.sem_inc(passed, 1)
                pool.memset(rows[1][0:CH, :, :], 0.0).then_inc(state_zeroed, 1)
                with pool.Fori(0, STEPS) as t:
                    for k in range(SLOTS):
                        c = k % CHUNKS
                        pool.wait_ge(gates_ready, slot(r, t, k))
                        pool.wait_ge(cell_ready, slot(r, t, k - CHUNKS))
                        pool.tensor_tensor(entered[c][:, :], gates[k % GATE_RING][:, 2, :],
                                           gates[k % GATE_RING][:, 3, :], ALU.mult).then_inc(entered_ready, 1)

        @block.vector
        def _(dve):
            for s in range(2, STREAMS):
                dve.memset(rows[s][:, :, :], 0.0)
                z = dve.memset(feat[s][:, :], 0.0)
            z.then_inc(zeroed, 1)
            dve.wait_ge(zeroed, START + 2)
            dve.wait_ge(weights_in, START + 7 * DMA)
            with dve.Fori(0, ROUNDS) as r:
                dve.wait_ge(x1_ready, START + r * SKIPS)
                dve.sem_inc(passed, 1)
                for s in range(STREAMS):
                    dve.memset(cell[s][:, :], 0.0)
                dve.memset(rows[3][0:CH, :, :], 0.0).then_inc(state_zeroed, 1)
                dve.wait_ge(state_zeroed, START + (r + 1) * 2)
                dve.sem_inc(passed, 1)
                def forget(t, k):
                    c, s = k % CHUNKS, k // CHUNKS
                    dve.wait_ge(gates_ready, slot(r, t, k))
                    dve.tensor_tensor(forgot[c][:, :], gates[k % GATE_RING][:, 1, :],
                                      cell[s][:, BANK * c:BANK * c + BANK], ALU.mult).then_inc(forgot_ready, 1)

                def enter(t, k):
                    c, s = k % CHUNKS, k // CHUNKS
                    dve.wait_ge(entered_ready, slot(r, t, k))
                    dve.wait_ge(forgot_ready, slot(r, t, k))
                    dve.tensor_tensor(cell[s][:, BANK * c:BANK * c + BANK], forgot[c][:, :], entered[c][:, :],
                                      ALU.add).then_inc(cell_ready, 1)

                def new_features(t, k):
                    c, s = k % CHUNKS, k // CHUNKS
                    dve.wait_ge(squashed_ready, slot(r, t, k))
                    dve.wait_ge(rows_in[s], START + (r * STEPS + t) * MOVES * DMA)
                    dve.tensor_tensor(image(feat[s][:, :], CIMG * c), gates[k % GATE_RING][:, 0, :].rearrange(
                        "p (h w) -> p h w", w=SIDE), squashed[c][:, :].rearrange("p (h w) -> p h w", w=SIDE),
                        ALU.mult).then_inc(feat_ready, 1)

                def first(t):
                    forget(t, 0)
                    enter(t, 0)

                def body(t, k, following):
                    after = t + (k + 1) // SLOTS, (k + 1) % SLOTS
                    if following:
                        forget(*after)
                    new_features(t, k)
                    if following:
                        enter(*after)

                steps(dve, r, first, body)
                for k in range(SKIPS):
                    h, q, c = k // (GROUP * CHUNKS), k // CHUNKS % GROUP, k % CHUNKS
                    dve.wait_ge(skip_ready, START + r * SKIPS + k + 1)
                    dve.wait_ge(x1_out[k % OUT_RING], START + (r * (SKIPS // OUT_RING) + k // OUT_RING) * DMA)
                    dve.scalar_tensor_tensor(
                        out=x1[k % OUT_RING][CH:128, :].rearrange("p (h w) -> p h w", w=SIDE),
                        in0=pre[k // 2 % 2][CH:128, k % 2, :].rearrange("p (h w) -> p h w", w=SIDE),
                        scalar=skip_b[CH:128, :],
                        in1=image(rows[h][CH:128, q, :], MARGIN + CIMG * c),
                        op0=ALU.add, op1=ALU.add).then_inc(x1_ready, 1)


SPLITS = 3
PAIRS = BATCH * CHUNKS


def pipelined(eng, *pieces):
    depth = max(behind for behind, _ in pieces)
    lead = (depth + 1) // 2 * 2

    def single_slot(n):
        for behind, piece in pieces:
            if 0 <= n - behind < BATCH:
                piece(n - behind, (n - behind) % 2, (n - behind) // 2)

    for n in range(lead):
        single_slot(n)
    with eng.Fori(lead // 2, BATCH // 2) as turn:
        for parity in range(2):
            for behind, piece in pieces:
                i, its_turn = (parity - behind) % 2, turn + (parity - behind) // 2
                piece(its_turn * 2 + i, i, its_turn)
    for n in range(BATCH, BATCH + depth):
        single_slot(n)


def project_phase(nc, x1_dram, w_in, w_delta, w_b, w_c, mean_w, delta_dram, input_dram, readout_dram, z_dram):
    with ExitStack() as ctx:
        def sb(name, shape, dt=F32):
            return ctx.enter_context(nc.sbuf_tensor(name, shape, dt))

        sem = Semaphores(nc, ctx, "proj")
        win = sb("win", [128, CHUNKS, 2 * INNER])
        wdelta, wb, wc, wmean = (sb("wdelta", [INNER, INNER]), sb("wb", [INNER, STATE]),
                                 sb("wc", [INNER, INNER]), sb("wmean", [128, 128]))
        eps = sb("eps", [128, 1])
        x = [sb(f"px{i}", [128, BANK]) for i in range(2)]
        centred, square, std = sb("centred", [128, BANK]), sb("square", [128, BANK]), sb("std", [128, BANK])
        normed = [sb(f"normed{i}", [128, BANK]) for i in range(2)]
        xs = [[sb(f"xs{i}{c}", [INNER, BANK]) for c in range(CHUNKS)] for i in range(2)]
        z = [[sb(f"z{i}{c}", [INNER, BANK]) for c in range(CHUNKS)] for i in range(2)]
        readout = [[sb(f"readout{i}{c}", [INNER, BANK]) for c in range(CHUNKS)] for i in range(2)]
        inputs = [[sb(f"inputs{i}{c}", [INNER, BANK]) for c in range(CHUNKS)] for i in range(2)]
        parts = [[sb(f"parts{i}{c}", [INNER, SPLITS, BANK], BF16) for c in range(CHUNKS)] for i in range(2)]
        rest = [[sb(f"rest{i}{c}", [INNER, BANK]) for c in range(CHUNKS)] for i in range(2)]

        def ps(name):
            return ctx.enter_context(nc.psum_tensor(name, [128, BANK], F32))

        mean_ps, var_ps, z_ps, delta_ps, b_ps, c_ps = (
            ps(n) for n in ("mean_ps", "var_ps", "z_ps", "delta_ps", "b_ps", "c_ps"))
        xs_ps = [ps("xs_ps0"), ps("xs_ps1")]

        weights_in, eps_set = sem("weights_in"), sem("eps_set")
        x_in = [sem(f"x_in{i}") for i in range(2)]
        stored = [sem(f"stored{i}") for i in range(2)]
        mean_ready, centred_ready, square_ready, var_ready, std_ready = (
            sem("mean"), sem("centred"), sem("square"), sem("var"), sem("std"))
        inverse_ready, normed_ready = sem("inverse"), sem("normed")
        in_ready, xs_ready, z_ready = sem("in_ready"), sem("xs_ready"), sem("z_ready")
        out_ready, part1_ready, rest1_ready, part2_ready, part3_ready = (
            sem("out_ready"), sem("part1"), sem("rest1"), sem("part2"), sem("part3"))
        readout_ready, input_ready = sem("readout"), sem("input")
        STORES = 4
        WEIGHTS = 4 + CHUNKS
        block = ctx.enter_context(nc.Block())

        @block.sync
        def _(sp):
            for s in sem.made:
                sp.sem_inc(s, START)
            for d, s in ((wdelta, w_delta), (wb, w_b), (wc, w_c), (wmean, mean_w)):
                sp.dma_start(d[:, :], s).then_inc(weights_in, DMA)
            for c in range(CHUNKS):
                sp.dma_start(win[:, c, :], w_in[c, :, :]).then_inc(weights_in, DMA)

            def load(b, i, turn):
                sp.wait_ge(centred_ready, START + turn * 2)
                for c in range(CHUNKS):
                    sp.dma_start(x[i][CH * c:CH * c + CH, :],
                                 x1_dram[bass.ds(b, 1), :, BANK * c:BANK * c + BANK].rearrange("b c l -> (b c) l")
                                 ).then_inc(x_in[i], DMA)

            def store(b, i, turn):
                for c in range(CHUNKS):
                    n = b * CHUNKS + c
                    for ready, tile, dram in ((z_ready, z, z_dram), (readout_ready, readout, readout_dram),
                                              (input_ready, inputs, input_dram)):
                        sp.wait_ge(ready, START + n + 1)
                        sp.dma_start(dram[bass.ds(n, 1), :, :].rearrange("n p l -> (n p) l"),
                                     tile[i][c][:, :]).then_inc(stored[i], DMA)
                    sp.wait_ge(part3_ready, START + n + 1)
                    sp.dma_start(delta_dram[bass.ds(n, 1), :, :, :].rearrange("n s p l -> (n p) s l"),
                                 parts[i][c][:, :, :]).then_inc(stored[i], DMA)

            pipelined(sp, (0, load), (3, store))
            for i in range(2):
                sp.wait_ge(stored[i], START + BATCH // 2 * CHUNKS * STORES * DMA)

        @block.tensor
        def _(pe):
            pe.wait_ge(weights_in, START + WEIGHTS * DMA)

            def mean(b, i, turn):
                pe.wait_ge(x_in[i], START + (turn + 1) * CHUNKS * DMA)
                pe.wait_ge(centred_ready, START + b)
                pe.matmul(mean_ps[:, :], wmean[:, :], x[i][:, :], start=True, stop=True).then_inc(mean_ready, 1)

            def variance(b, i, turn):
                pe.wait_ge(square_ready, START + b + 1)
                pe.wait_ge(std_ready, START + b)
                pe.matmul(var_ps[:, :], wmean[:, :], square[:, :], start=True, stop=True).then_inc(var_ready, 1)

            def project_in(b, i, turn):
                pe.wait_ge(normed_ready, START + b + 1)
                for c in range(CHUNKS):
                    pe.wait_ge(xs_ready, START + b * CHUNKS)
                    pe.matmul(xs_ps[c][:, :], win[:, c, 0:INNER], normed[i][:, :], start=True, stop=True)
                    pe.wait_ge(z_ready, START + b * CHUNKS + c)
                    pe.matmul(z_ps[:, :], win[:, c, INNER:], normed[i][:, :], start=True, stop=True
                              ).then_inc(in_ready, 1)

            def project_out(b, i, turn):
                for c in range(CHUNKS):
                    n = b * CHUNKS + c
                    pe.wait_ge(xs_ready, START + n + 1)
                    pe.wait_ge(rest1_ready, START + n)
                    pe.matmul(delta_ps[:, :], wdelta[:, :], xs[i][c][:, :], start=True, stop=True)
                    pe.wait_ge(input_ready, START + n)
                    pe.matmul(b_ps[:, :], wb[:, :], xs[i][c][:, :], start=True, stop=True)
                    pe.wait_ge(readout_ready, START + n)
                    pe.matmul(c_ps[:, :], wc[:, :], xs[i][c][:, :], start=True, stop=True).then_inc(out_ready, 1)

            pipelined(pe, (1, variance), (2, project_in), (0, mean), (2, project_out))

        @block.scalar
        def _(act):
            act.wait_ge(eps_set, START + 1)

            def deviation(b, i, turn):
                act.wait_ge(var_ready, START + b + 1)
                act.wait_ge(normed_ready, START + b)
                act.activation(std[:, :], var_ps[:, :], ACT.Sqrt, bias=eps[:, :]).then_inc(std_ready, 1)

            def move_in(b, i, turn):
                for c in range(CHUNKS):
                    act.wait_ge(in_ready, START + b * CHUNKS + c + 1)
                    act.wait_ge(stored[i], START + turn * CHUNKS * STORES * DMA)
                    act.wait_ge(input_ready, START + (b - 1) * CHUNKS)
                    act.copy(xs[i][c][:, :], xs_ps[c][:, :]).then_inc(xs_ready, 1)
                    act.copy(z[i][c][:, :], z_ps[:, :]).then_inc(z_ready, 1)

            def move_out(b, i, turn):
                for c in range(CHUNKS):
                    act.wait_ge(out_ready, START + b * CHUNKS + c + 1)
                    act.copy(parts[i][c][:, 0, :], delta_ps[:, :]).then_inc(part1_ready, 1)
                    act.copy(readout[i][c][:, :], c_ps[:, :]).then_inc(readout_ready, 1)
                for c in range(CHUNKS):
                    act.wait_ge(rest1_ready, START + b * CHUNKS + c + 1)
                    act.copy(parts[i][c][:, 1, :], rest[i][c][:, :]).then_inc(part2_ready, 1)

            pipelined(act, (1, deviation), (2, move_in), (2, move_out))

        @block.gpsimd
        def _(pool):
            pool.memset(eps[:, :], 1e-5).then_inc(eps_set, 1)

            def squares(b, i, turn):
                pool.wait_ge(centred_ready, START + b + 1)
                pool.wait_ge(var_ready, START + b)
                pool.tensor_tensor(square[:, :], centred[:, :], centred[:, :], ALU.mult).then_inc(square_ready, 1)

            pipelined(pool, (0, squares))

        @block.vector
        def _(dve):
            def centre(b, i, turn):
                dve.wait_ge(mean_ready, START + b + 1)
                dve.wait_ge(normed_ready, START + b)
                dve.tensor_tensor(centred[:, :], x[i][:, :], mean_ps[:, :], ALU.subtract).then_inc(centred_ready, 1)

            def normalise(b, i, turn):
                dve.wait_ge(std_ready, START + b + 1)
                dve.reciprocal(std[:, :], std[:, :]).then_inc(inverse_ready, 1)
                dve.wait_ge(inverse_ready, START + b + 1)
                dve.tensor_tensor(normed[i][:, :], centred[:, :], std[:, :], ALU.mult).then_inc(normed_ready, 1)

            def rest_and_input(b, i, turn):
                for c in range(CHUNKS):
                    n = b * CHUNKS + c
                    dve.wait_ge(out_ready, START + n + 1)
                    dve.wait_ge(part1_ready, START + n + 1)
                    dve.wait_ge(stored[i], START + turn * CHUNKS * STORES * DMA)
                    dve.tensor_tensor(rest[i][c][:, :], delta_ps[:, :], parts[i][c][:, 0, :],
                                      ALU.subtract).then_inc(rest1_ready, 1)
                    dve.tensor_tensor(inputs[i][c][:, :], b_ps[:, :], xs[i][c][:, :], ALU.mult).then_inc(input_ready, 1)

            def third_part(b, i, turn):
                for c in range(CHUNKS):
                    dve.wait_ge(part2_ready, START + b * CHUNKS + c + 1)
                    dve.tensor_tensor(parts[i][c][:, 2, :], rest[i][c][:, :], parts[i][c][:, 1, :],
                                      ALU.subtract).then_inc(part3_ready, 1)

            pipelined(dve, (1, normalise), (0, centre), (2, rest_and_input), (2, third_part))


GROUPS = 4
WIDTH = INNER // GROUPS
UNITS = PAIRS * GROUPS * WIDTH
FOLD = 4
RING = 4


def scan_phase(nc, delta_dram, input_dram, readout_dram, a_t, selectors, y_dram):
    direct = [k % 4 == 3 for k in range(WIDTH)]
    V = sum(direct)
    G = WIDTH - V
    BLOCKS = CHUNKS * GROUPS

    with ExitStack() as ctx:
        def sb(name, shape, dt=F32):
            return ctx.enter_context(nc.sbuf_tensor(name, shape, dt))

        sem = Semaphores(nc, ctx, "scan")
        states = [sb(f"states{j}", [STATE, WIDTH, BANK]) for j in range(2)]
        spread = sb("spread", [STATE, FOLD * BANK + FOLD])
        readout = sb("s_readout", [STATE, BANK])
        entering = [sb(f"entering{c}", [STATE, BANK]) for c in range(2)]
        parts = sb("s_parts", [128, GROUPS, BANK], BF16)
        sel = sb("pick", [128, WIDTH, STATE], BF16)
        decay_rate = sb("decay_rate", [STATE, INNER])
        carry = sb("carry", [STATE, INNER])
        copied = [sb(f"copied{i}", [STATE, BANK]) for i in range(RING)]
        enter_g = [sb(f"enter_g{i}", [STATE, BANK]) for i in range(RING)]
        enter_v = [sb(f"enter_v{i}", [STATE, BANK]) for i in range(2)]
        y_sb = sb("y_sb", [128, WIDTH, INNER])
        delta_ps = [ctx.enter_context(nc.psum_tensor(f"delta_ps{i}", [STATE, BANK], F32)) for i in range(RING)]
        decay = [sb(f"decay{i}", [STATE, BANK]) for i in range(RING)]
        y_ps = [ctx.enter_context(nc.psum_tensor(f"y_ps{h}", [128, BANK], F32)) for h in range(2)]

        consts_in = sem("consts_in")
        pool_zeroed, vector_zeroed = sem("pool_zeroed"), sem("vector_zeroed")
        parts_in = [sem(f"parts_in{g}") for g in range(GROUPS)]
        entering_in = [sem(f"entering_in{c}") for c in range(2)]
        readout_in, spread_ready = sem("readout_in"), sem("spread_ready")
        delta_ready, decay_ready, copied_ready = sem("delta_ready"), sem("decay_ready"), sem("copied_ready")
        enter_g_ready, enter_v_ready = sem("enter_g_ready"), sem("enter_v_ready")
        scanned, carried = sem("scanned"), sem("carried")
        y_half, y_moved = sem("y_half"), sem("y_moved")
        y_out = sem("y_out")
        block = ctx.enter_context(nc.Block())

        BU = BLOCKS * WIDTH

        def unit(X, k):
            v = sum(direct[:k])
            return X * WIDTH + k, X * V + v, X * G + (k - v)

        def ahead(X, k, by):
            n = X * WIDTH + k + by
            return (n // WIDTH, n % WIDTH)

        LATE = 4
        slots = [[] for _ in range(WIDTH)]
        for i in range(WIDTH):
            slots[LATE + i * (WIDTH - LATE) // WIDTH].append(i)
        HALF = WIDTH // 2

        def slots_of(i):
            return next(k for k in range(WIDTH) if i in slots[k])

        @block.sync
        def _(sp):
            for s in sem.made:
                sp.sem_inc(s, START)

            def load_tokens(p, c):
                sp.dma_start(entering[c][:, :], input_dram[bass.ds(p, 1), :, :].rearrange("n p l -> (n p) l")
                             ).then_inc(entering_in[c], DMA)

            def load_readout(p):
                sp.dma_start(readout[:, :], readout_dram[bass.ds(p, 1), :, :].rearrange("n p l -> (n p) l")
                             ).then_inc(readout_in, DMA)

            def load_parts(p, g):
                src = delta_dram[bass.ds(p, 1), :, WIDTH * g:WIDTH * g + WIDTH, :].rearrange("n s k l -> (n s) k l")
                for s in range(SPLITS):
                    sp.dma_start(parts[WIDTH * s:WIDTH * s + WIDTH, g, :], src[s, :, :]).then_inc(parts_in[g], DMA)

            def store_y(p):
                sp.wait_ge(y_moved, START + (p * GROUPS + 1) * 2)
                for j in range(4):
                    dst = y_dram[bass.ds(p, 1), FOLD * j:FOLD * j + FOLD, :]
                    sp.dma_start(dst.rearrange("n p l -> (n p) l"),
                                 y_sb[32 * j:32 * j + FOLD, :, :].rearrange("p i d -> p (i d)")).then_inc(y_out, DMA)

            def pair(p, c, load_next):
                if load_next:
                    sp.wait_ge(scanned, START + p * (GROUPS * WIDTH))
                    load_tokens(p + 1, 1 - c)
                for g in range(GROUPS):
                    if g == 1:
                        store_y(p)
                    if load_next:
                        sp.wait_ge(delta_ready, START + (p * GROUPS + g + 1) * WIDTH)
                        load_parts(p + 1, g)
                        if g == 1:
                            sp.wait_ge(spread_ready, START + p + 1)
                            load_readout(p + 1)

            sp.dma_start(sel[:, :, :], selectors).then_inc(consts_in, DMA)
            sp.dma_start(decay_rate[:, :], a_t).then_inc(consts_in, DMA)
            for g in range(GROUPS):
                load_parts(0, g)
                if g == 0:
                    load_tokens(0, 0)
                    load_readout(0)
            with sp.Fori(0, BATCH - 1) as b:
                for c in range(CHUNKS):
                    pair(b * CHUNKS + c, c, True)
            pair(PAIRS - 2, 0, True)
            pair(PAIRS - 1, 1, False)
            store_y(PAIRS)
            sp.wait_ge(y_out, START + (PAIRS + 1) * 4 * DMA)

        def broadcast(pe, b, X, k):
            n = unit(X, k)[0]
            g = X % GROUPS
            if k == 0:
                pe.wait_ge(parts_in[g], START + (b * CHUNKS + X // GROUPS + 1) * SPLITS * DMA)
            Xl, kl = ahead(X, k, -RING)
            n0, v0, g0 = unit(Xl, kl)
            pe.wait_ge(decay_ready, START + b * BU + n0 + 1)
            if direct[kl]:
                pe.wait_ge(enter_v_ready, START + b * BLOCKS * V + v0 + 1)
            else:
                pe.wait_ge(copied_ready, START + b * BLOCKS * G + g0 + 1)
            pe.matmul(delta_ps[n % RING][:, :], sel[:, k, :], parts[:, g, :],
                      start=True, stop=True).then_inc(delta_ready, 1)

        def contract(pe, states, i):
            for m in range(FOLD):
                for j in range(4):
                    l = 16 * i + 4 * j + m
                    mm = pe.matmul(y_ps[i // HALF][32 * j:32 * j + FOLD, WIDTH * (i % HALF):WIDTH * (i % HALF) + WIDTH],
                                   spread[:, 4 * l + 3 - m:4 * l + 3 - m + FOLD], states[:, :, l],
                                   start=(m == 0), stop=(m == FOLD - 1))
            if i % HALF == HALF - 1:
                mm.then_inc(y_half, 1)

        @block.tensor
        def _(pe):
            pe.wait_ge(consts_in, START + 2 * DMA)
            pe.wait_ge(pool_zeroed, START + 2)
            pe.wait_ge(vector_zeroed, START + 1)
            with pe.Fori(0, BATCH) as b:
                for X in range(BLOCKS):
                    for k in range(WIDTH):
                        broadcast(pe, b, X, k)
                        for i in slots[k]:
                            if i == 0:
                                pe.wait_ge(scanned, START + b * BU + X * WIDTH)
                                pe.wait_ge(spread_ready, START + b * CHUNKS + (X + GROUPS - 1) // GROUPS)
                                pe.wait_ge(y_moved, START + (b * BLOCKS + X) * 2)
                            contract(pe, states[(X + 1) % 2], i)
            pe.wait_ge(scanned, START + UNITS)
            pe.wait_ge(spread_ready, START + PAIRS)
            pe.wait_ge(y_moved, START + BATCH * BLOCKS * 2)
            for i in range(WIDTH):
                contract(pe, states[(BLOCKS + 1) % 2], i)

        @block.scalar
        def _(act):
            act.wait_ge(consts_in, START + 2 * DMA)
            act.wait_ge(vector_zeroed, START + 1)

            def move_y(B, X, h):
                act.wait_ge(y_half, START + B * 2 + h + 1)
                if X % GROUPS == 1 and h == 0:
                    act.wait_ge(y_out, START + (B - 1) * DMA + 4 * DMA)
                at = (X - 1) % GROUPS * WIDTH
                act.copy(y_sb[:, HALF * h:HALF * h + HALF, at:at + WIDTH],
                         y_ps[h][:, :].rearrange("p (i d) -> p i d", d=WIDTH)).then_inc(y_moved, 1)

            with act.Fori(0, BATCH) as b:
                for X in range(BLOCKS):
                    for k in range(WIDTH):
                        n, v, g = unit(X, k)
                        d = (X % GROUPS) * WIDTH + k
                        act.wait_ge(delta_ready, START + b * BU + n + 1)
                        act.wait_ge(scanned, START + b * BU + n - RING + 1)
                        act.activation(decay[n % RING][:, :], delta_ps[n % RING][:, :], ACT.Exp,
                                       scale=decay_rate[:, d:d + 1]).then_inc(decay_ready, 1)
                        if not direct[k]:
                            act.wait_ge(enter_g_ready, START + b * BLOCKS * G + g - RING + 1)
                            act.copy(copied[g % RING][:, :], delta_ps[n % RING][:, :]).then_inc(copied_ready, 1)
                        if k == slots_of(HALF - 1) + 2:
                            move_y(b * BLOCKS + X, X, 0)
                    move_y(b * BLOCKS + X, X, 1)
            for h in range(2):
                move_y(BATCH * BLOCKS, 0, h)

        @block.gpsimd
        def _(pool):
            pool.memset(states[1][:, 0:WIDTH // 2, :], 0.0)
            pool.memset(spread[:, :], 0.0).then_inc(pool_zeroed, 1)
            pool.wait_ge(pool_zeroed, START + 1)
            pool.memset(parts[SPLITS * WIDTH:128, :, :], 0.0).then_inc(pool_zeroed, 1)

            with pool.Fori(0, BATCH) as b:
                for X in range(BLOCKS):
                    c = X // GROUPS
                    for k in range(WIDTH):
                        n, v, g = unit(X, k)
                        if n in (0, GROUPS * WIDTH):
                            pool.wait_ge(entering_in[c], START + (b + 1) * DMA)
                        if not direct[k]:
                            pool.wait_ge(copied_ready, START + b * BLOCKS * G + g + 1)
                            Xb, kb = (g - RING) // G, [i for i in range(WIDTH) if not direct[i]][(g - RING) % G]
                            pool.wait_ge(scanned, START + b * BU + Xb * WIDTH + kb + 1)
                            pool.tensor_tensor(enter_g[g % RING][:, :], copied[g % RING][:, :], entering[c][:, :],
                                               ALU.mult).then_inc(enter_g_ready, 1)

        @block.vector
        def _(dve):
            dve.memset(carry[:, :], 0.0).then_inc(carried, 1)
            for h in range(2):
                dve.memset(y_ps[h][:, :], 0.0)
            dve.memset(states[1][:, WIDTH // 2:, :], 0.0)
            dve.memset(y_sb[:, :, :], 0.0).then_inc(vector_zeroed, 1)
            dve.wait_ge(consts_in, START + 2 * DMA)
            dve.wait_ge(pool_zeroed, START + 2)

            def product(b, X, k):
                n, v, g = unit(X, k)
                dve.wait_ge(decay_ready, START + b * BU + n + 1)
                dve.tensor_tensor(enter_v[v % 2][:, :], delta_ps[n % RING][:, :], entering[X // GROUPS][:, :],
                                  ALU.mult).then_inc(enter_v_ready, 1)

            with dve.Fori(0, BATCH) as b:
                for X in range(BLOCKS):
                    d0 = (X % GROUPS) * WIDTH
                    for k in range(WIDTH):
                        n, v, g = unit(X, k)
                        if n in (0, GROUPS * WIDTH):
                            dve.wait_ge(entering_in[n // (GROUPS * WIDTH)], START + (b + 1) * DMA)
                        Xa, ka = ahead(X, k, 1)
                        if Xa == X and direct[ka]:
                            product(b, Xa, ka)
                        if k == 0 and direct[0]:
                            product(b, X, 0)
                        if k == 0:
                            dve.wait_ge(y_half, START + (b * BLOCKS + X) * 2)
                            dve.wait_ge(carried, START + b * BLOCKS + X + 1)
                        dve.wait_ge(decay_ready, START + b * BU + n + 1)
                        if direct[k]:
                            dve.wait_ge(enter_v_ready, START + b * BLOCKS * V + v + 1)
                            enter = enter_v[v % 2]
                        else:
                            dve.wait_ge(enter_g_ready, START + b * BLOCKS * G + g + 1)
                            enter = enter_g[g % RING]
                        dve.tensor_tensor_scan(states[X % 2][:, k, :], decay[n % RING][:, :], enter[:, :],
                                               carry[:, d0 + k:d0 + k + 1], ALU.mult, ALU.add).then_inc(scanned, 1)
                    dve.wait_ge(scanned, START + b * BU + (X + 1) * WIDTH)
                    if X < GROUPS:
                        dve.tensor_copy(carry[:, d0:d0 + WIDTH], states[X % 2][:, :, BANK - 1]).then_inc(carried, 1)
                    else:
                        dve.memset(carry[:, d0:d0 + WIDTH], 0.0).then_inc(carried, 1)
                    if X % GROUPS == 0:
                        dve.wait_ge(readout_in, START + (b * CHUNKS + X // GROUPS + 1) * DMA)
                        dve.wait_ge(y_half, START + (b * BLOCKS + X + 1) * 2)
                        dve.tensor_copy(spread[:, FOLD - 1:FOLD - 1 + FOLD * BANK:FOLD], readout[:, :]
                                        ).then_inc(spread_ready, 1)


def gate_phase(nc, y_dram, z_dram, x1_dram, w_out, mean_w, identity, gate_w, gate_b, x2_dram, normed_dram, logit_dram):
    ROWS = 4 * FOLD
    SPAN = 128 // ROWS
    TILES = BANK // 128
    with ExitStack() as ctx:
        def sb(name, shape, dt=F32):
            return ctx.enter_context(nc.sbuf_tensor(name, shape, dt))

        def ps(name, rows=128):
            return ctx.enter_context(nc.psum_tensor(name, [rows, BANK], F32))

        sem = Semaphores(nc, ctx, "gate")
        wout, wmean, ident = sb("wout", [INNER, CH]), sb("g_wmean", [128, 128]), sb("g_ident", [128, 128])
        wgate, bgate = sb("wgate", [128, CHUNKS, EXPERTS]), sb("bgate", [CHUNKS * EXPERTS, 1])
        eps = sb("g_eps", [128, 1])
        y = [sb(f"g_y{i}", [128, CHUNKS, TILES, INNER]) for i in range(2)]
        z = [sb(f"g_z{i}", [INNER, CHUNKS, BANK]) for i in range(2)]
        x1 = [sb(f"g_x1{i}", [128, BANK]) for i in range(2)]
        swish, gated = sb("swish", [INNER, CHUNKS, BANK]), sb("gated", [INNER, CHUNKS, BANK])
        x2 = [sb(f"g_x2{i}", [128, BANK]) for i in range(2)]
        centred = [sb(f"g_centred{i}", [128, BANK]) for i in range(2)]
        std = [sb(f"g_std{i}", [128, BANK]) for i in range(2)]
        square = sb("g_square", [128, BANK])
        normed = [sb(f"g_normed{i}", [128, BANK]) for i in range(2)]
        logits = [sb(f"g_logits{i}", [CHUNKS * EXPERTS, BANK]) for i in range(2)]
        turned_ps = [ps(f"turned_ps{c}") for c in range(CHUNKS)]
        out_ps, mean_ps, var_ps, logit_ps = ps("out_ps"), ps("g_mean_ps"), ps("g_var_ps"), ps("logit_ps")

        weights_in, eps_set = sem("weights_in"), sem("eps_set")
        loaded = [sem(f"loaded{i}") for i in range(2)]
        x2_stored = [sem(f"x2_stored{i}") for i in range(2)]
        scores_stored = [sem(f"scores_stored{i}") for i in range(2)]
        turned, swish_ready, gated_ready, out_ready, x2_ready = (
            sem("turned"), sem("swish"), sem("gated"), sem("out"), sem("x2"))
        mean_ready, centred_ready, square_ready, var_ready, std_ready = (
            sem("mean"), sem("centred"), sem("square"), sem("var"), sem("std"))
        inverse_ready, normed_ready, logit_ready, logits_ready = (
            sem("inverse"), sem("normed"), sem("logit"), sem("logits"))
        LOADS = 2 + CHUNKS
        passed = sem("passed")
        block = ctx.enter_context(nc.Block())

        @block.sync
        def _(sp):
            for s in sem.made:
                sp.sem_inc(s, START)
            for d, s in ((wout, w_out), (wmean, mean_w), (ident, identity), (bgate, gate_b)):
                sp.dma_start(d[:, :], s).then_inc(weights_in, DMA)
            sp.dma_start(wgate[:, :, :], gate_w).then_inc(weights_in, DMA)

            def load(b, i, turn):
                if not (isinstance(b, int) and b == 0):
                    sp.wait_ge(x2_ready, START + b - 1)
                sp.dma_start(y[i][:, :, :, :], y_dram[bass.ds(b * CHUNKS + 1, CHUNKS), :, :].rearrange(
                    "n r (s t d) -> (r s) n t d", s=SPAN, d=INNER)).then_inc(loaded[i], DMA)
                sp.dma_start(z[i][:, :, :], z_dram[bass.ds(b * CHUNKS, CHUNKS), :, :].rearrange("n p l -> p n l")
                             ).then_inc(loaded[i], DMA)
                for c in range(CHUNKS):
                    sp.dma_start(x1[i][CH * c:CH * c + CH, :],
                                 x1_dram[bass.ds(b, 1), :, BANK * c:BANK * c + BANK].rearrange("b c l -> (b c) l")
                                 ).then_inc(loaded[i], DMA)

            def store(b, i, ready, tile, dram, height, stored):
                sp.wait_ge(ready, START + b + 1)
                for c in range(CHUNKS):
                    sp.dma_start(dram[bass.ds(b, 1), :, BANK * c:BANK * c + BANK].rearrange("b c l -> (b c) l"),
                                 tile[i][height * c:height * c + height, :]).then_inc(stored[i], DMA)

            def store_x2(b, i, turn):
                store(b, i, x2_ready, x2, x2_dram, CH, x2_stored)

            def store_scores(b, i, turn):
                store(b, i, normed_ready, normed, normed_dram, CH, scores_stored)
                store(b, i, logits_ready, logits, logit_dram, EXPERTS, scores_stored)

            pipelined(sp, (0, load), (2, store_x2), (4, store_scores))
            for i in range(2):
                sp.wait_ge(x2_stored[i], START + BATCH // 2 * CHUNKS * DMA)
                sp.wait_ge(scores_stored[i], START + BATCH // 2 * 2 * CHUNKS * DMA)

        @block.tensor
        def _(pe):
            pe.wait_ge(weights_in, START + 5 * DMA)

            def turn_y(b, i, turn):
                pe.wait_ge(loaded[i], START + (turn + 1) * LOADS * DMA)
                for c in range(CHUNKS):
                    pe.wait_ge(gated_ready, START + b * CHUNKS)
                    for t in range(TILES):
                        mm = pe.transpose(turned_ps[c][:, 128 * t:128 * t + 128], y[i][:, c, t, :], ident[:, :])
                    mm.then_inc(turned, 1)

            def project_out(b, i, turn):
                pe.wait_ge(x2_ready, START + b)
                for c in range(CHUNKS):
                    pe.wait_ge(gated_ready, START + b * CHUNKS + c + 1)
                    pe.sem_inc(passed, 1)
                    mm = pe.matmul(out_ps[CH * c:CH * c + CH, :], wout[:, :], gated[:, c, :], start=True, stop=True)
                mm.then_inc(out_ready, 1)

            def mean(b, i, turn):
                pe.wait_ge(x2_ready, START + b + 1)
                pe.wait_ge(centred_ready, START + b)
                pe.matmul(mean_ps[:, :], wmean[:, :], x2[i][:, :], start=True, stop=True).then_inc(mean_ready, 1)

            def variance(b, i, turn):
                pe.wait_ge(square_ready, START + b + 1)
                pe.wait_ge(std_ready, START + b)
                pe.matmul(var_ps[:, :], wmean[:, :], square[:, :], start=True, stop=True).then_inc(var_ready, 1)

            def score(b, i, turn):
                pe.wait_ge(normed_ready, START + b + 1)
                pe.wait_ge(logits_ready, START + b)
                for c in range(CHUNKS):
                    mm = pe.matmul(logit_ps[EXPERTS * c:EXPERTS * c + EXPERTS, :], wgate[:, c, :], normed[i][:, :],
                                   start=True, stop=True)
                mm.then_inc(logit_ready, 1)

            pipelined(pe, (1, project_out), (0, turn_y), (1, mean), (3, score), (1, variance))

        @block.scalar
        def _(act):
            act.wait_ge(eps_set, START + 1)
            act.wait_ge(weights_in, START + 5 * DMA)

            def gate_values(b, i, turn):
                act.wait_ge(loaded[i], START + (turn + 1) * LOADS * DMA)
                act.wait_ge(gated_ready, START + b * CHUNKS)
                act.activation(swish[:, :, :], z[i][:, :, :], ACT.Silu).then_inc(swish_ready, 1)

            def deviation(b, i, turn):
                act.wait_ge(var_ready, START + b + 1)
                act.wait_ge(normed_ready, START + b - 1)
                act.activation(std[i][:, :], var_ps[:, :], ACT.Sqrt, bias=eps[:, :]).then_inc(std_ready, 1)

            def add_bias(b, i, turn):
                act.wait_ge(logit_ready, START + b + 1)
                act.wait_ge(scores_stored[i], START + turn * 2 * CHUNKS * DMA)
                act.activation(logits[i][:, :], logit_ps[0:CHUNKS * EXPERTS, :], ACT.Identity, bias=bgate[:, :]
                               ).then_inc(logits_ready, 1)

            pipelined(act, (0, gate_values), (3, add_bias), (1, deviation))

        @block.gpsimd
        def _(pool):
            pool.memset(eps[:, :], 1e-5).then_inc(eps_set, 1)

            def squares(b, i, turn):
                pool.wait_ge(centred_ready, START + b + 1)
                pool.wait_ge(var_ready, START + b)
                pool.tensor_tensor(square[:, :], centred[i][:, :], centred[i][:, :], ALU.mult).then_inc(square_ready, 1)

            pipelined(pool, (0, squares))

        @block.vector
        def _(dve):
            def gate(b, i, turn):
                dve.wait_ge(swish_ready, START + b + 1)
                dve.wait_ge(out_ready, START + b)
                for c in range(CHUNKS):
                    dve.wait_ge(turned, START + b * CHUNKS + c + 1)
                    order = turned_ps[c][:, :].rearrange("p (t r s) -> p s t r", t=TILES, s=SPAN)
                    dve.tensor_tensor(gated[:, c, :].rearrange("p (s t r) -> p s t r", s=SPAN, t=TILES), order,
                                      swish[:, c, :].rearrange("p (s t r) -> p s t r", s=SPAN, t=TILES),
                                      ALU.mult).then_inc(gated_ready, 1)

            def residual(b, i, turn):
                dve.wait_ge(out_ready, START + b + 1)
                dve.wait_ge(x2_stored[i], START + turn * CHUNKS * DMA)
                dve.tensor_tensor(x2[i][:, :], out_ps[:, :], x1[i][:, :], ALU.add).then_inc(x2_ready, 1)

            def centre(b, i, turn):
                dve.wait_ge(mean_ready, START + b + 1)
                dve.wait_ge(normed_ready, START + b - 1)
                dve.tensor_tensor(centred[i][:, :], x2[i][:, :], mean_ps[:, :], ALU.subtract).then_inc(centred_ready, 1)

            def normalise(b, i, turn):
                dve.wait_ge(std_ready, START + b + 1)
                dve.wait_ge(scores_stored[i], START + turn * 2 * CHUNKS * DMA)
                dve.reciprocal(std[i][:, :], std[i][:, :]).then_inc(inverse_ready, 1)
                dve.wait_ge(inverse_ready, START + b + 1)
                dve.tensor_tensor(normed[i][:, :], centred[i][:, :], std[i][:, :], ALU.mult).then_inc(normed_ready, 1)

            pipelined(dve, (1, residual), (0, gate), (1, centre), (2, normalise))


QUADS = BATCH // GROUP


def expert_phase(nc, logit_dram, normed_dram, x2_dram, identity, weight1, weight2, expert_dram, out_dram):
    TILES = LEN // 128
    ROWS1 = CH + 1
    DUOS = BATCH // 2
    with ExitStack() as ctx:
        def sb(name, shape, dt=F32):
            return ctx.enter_context(nc.sbuf_tensor(name, shape, dt))

        sem = Semaphores(nc, ctx, "expert")
        ident = sb("e_ident", [128, 128])
        w1 = sb("w1", [ROWS1, EXPERTS, HIDDEN])
        w2 = sb("w2", [128, HIDDEN // 128, EXPERTS, CH])
        w2_bias = sb("w2_bias", [1, EXPERTS, CH])
        ones = sb("ones", [1, BATCH])
        logits = [sb(f"e_logits{i}", [128, LEN]) for i in range(2)]
        probs = [sb(f"probs{i}", [128, LEN]) for i in range(2)]
        marked = [sb(f"marked{i}", [128, LEN]) for i in range(2)]
        chosen = [sb(f"chosen{q}", [128, LEN]) for q in range(QUADS)]
        tops = sb("tops", [128, QUADS, TOPK])
        best = sb("best", [128, QUADS, TOPK])
        minus = sb("minus", [128, QUADS])
        total = sb("total", [128, QUADS])
        share = sb("share", [128, QUADS])
        chosen_t = sb("chosen_t", [128, TILES, 128])
        normed = [sb(f"e_normed{i}", [CH, LEN]) for i in range(2)]
        normed_t = [sb(f"normed_t{i}", [128, TILES, CH]) for i in range(2)]
        pooled = sb("pooled", [ROWS1, BATCH, EXPERTS])
        hidden = sb("hidden", [128, EXPERTS, HIDDEN // 128, BATCH])
        results = sb("results", [BATCH, EXPERTS, CH])
        spread = sb("e_spread", [128, QUADS, GROUP, CH])
        x2 = [sb(f"e_x2{j}", [2 * CH, LEN]) for j in range(DUOS)]
        chosen_ps = ctx.enter_context(nc.psum_tensor("chosen_ps", [128, TILES, 128], F32))
        normed_ps = ctx.enter_context(nc.psum_tensor("normed_ps", [128, TILES, CH], F32))
        pooled_ps = ctx.enter_context(nc.psum_tensor("pooled_ps", [CH, BANK], F32))
        work_ps = ctx.enter_context(nc.psum_tensor("work_ps", [128, 4, BANK], F32))
        turned_ps = [normed_ps[:, :, :], work_ps[:, 3, :].rearrange("p (t c) -> p t c", c=CH)]

        consts_in, weights_in, ones_set, spread_zeroed = (
            sem("consts_in"), sem("weights_in"), sem("ones_set"), sem("spread_zeroed"))
        logits_in = [sem(f"logits_in{i}") for i in range(2)]
        normed_in = [sem(f"normed_in{i}") for i in range(2)]
        top_ready, minus_ready, exp_ready, share_ready, probs_ready = (
            sem("top"), sem("minus"), sem("exp"), sem("share"), sem("probs"))
        best_ready, marked_ready, chosen_ready = sem("best"), sem("marked"), sem("chosen")
        chosen_turned, chosen_t_ready, normed_turned, normed_t_ready = (
            sem("chosen_turned"), sem("chosen_t"), sem("normed_turned"), sem("normed_t"))
        pooled_summed, pooled_ready = sem("pooled_summed"), sem("pooled")
        hidden_summed, hidden_ready, results_summed, results_ready = (
            sem("hidden_summed"), sem("hidden"), sem("results_summed"), sem("results"))
        results_out, spread_in = sem("results_out"), sem("spread_in")
        x2_in = sem("x2_in")
        scattered, final_ready = sem("scattered"), sem("final")
        stored = sem("stored")
        PIECES = DUOS * CHUNKS
        block = ctx.enter_context(nc.Block())

        @block.sync
        def _(sp):
            sp.dma_start(ident[:, :], identity).then_inc(consts_in, DMA)

            def load_logits(q):
                if q >= 2:
                    sp.wait_ge(probs_ready, q - 1)
                sp.dma_start(logits[q % 2][:, :], logit_dram[GROUP * q:GROUP * q + GROUP, :, :].rearrange(
                    "b e l -> (b e) l")).then_inc(logits_in[q % 2], DMA)

            def load_tokens(b):
                if b >= 2:
                    sp.wait_ge(normed_turned, b - 1)
                sp.dma_start(normed[b % 2][:, :], normed_dram[b, :, :]).then_inc(normed_in[b % 2], DMA)

            load_logits(0)
            load_logits(1)
            load_tokens(0)
            load_tokens(1)
            sp.dma_start(w1[:, :, :], weight1.rearrange("e d h -> d e h")).then_inc(weights_in, DMA)
            for h in range(2):
                sp.dma_start(w2[:, h, :, :], weight2[:, 128 * h:128 * h + 128, :].rearrange("e h o -> h e o")
                             ).then_inc(weights_in, DMA)
            sp.dma_start(w2_bias[:, :, :], weight2[:, HIDDEN:HIDDEN + 1, :].rearrange("e h o -> h e o")
                         ).then_inc(weights_in, DMA)
            for b in range(2, BATCH):
                load_tokens(b)
                if b % GROUP == 2 and b // GROUP + 2 < QUADS:
                    load_logits(b // GROUP + 2)
            for j in range(DUOS):
                sp.dma_start(x2[j][:, :], x2_dram[2 * j:2 * j + 2, :, :].rearrange("b c l -> (b c) l")).then_inc(x2_in, DMA)
            sp.wait_ge(results_ready, 4)
            sp.dma_start(expert_dram, results[:, :, :]).then_inc(results_out, DMA)
            sp.wait_ge(results_out, DMA)
            sp.wait_ge(spread_zeroed, 1)
            for i in range(GROUP):
                sp.dma_start(spread[EXPERTS * i:EXPERTS * i + EXPERTS, :, i, :],
                             expert_dram.rearrange("(q i) e o -> i e q o", i=GROUP)[i, :, :, :]).then_inc(spread_in, DMA)
            for j in range(DUOS):
                sp.wait_ge(final_ready, (j + 1) * CHUNKS)
                sp.dma_start(out_dram[2 * j:2 * j + 2, :, :].rearrange("b c l -> (b c) l"), x2[j][:, :]).then_inc(stored, DMA)
            sp.wait_ge(stored, DUOS * DMA)

        @block.tensor
        def _(pe):
            pe.wait_ge(consts_in, DMA)

            def turn_tokens(b):
                pe.wait_ge(normed_in[b % 2], (b // 2 + 1) * DMA)
                if b >= 2:
                    pe.wait_ge(normed_t_ready, b - 1)
                for t in range(TILES):
                    mm = pe.transpose(turned_ps[b % 2][:, t, :], normed[b % 2][:, 128 * t:128 * t + 128], ident[0:CH, 0:CH])
                mm.then_inc(normed_turned, 1)

            turn_tokens(0)
            for q in range(QUADS):
                pe.wait_ge(chosen_ready, q + 1)
                if q:
                    pe.wait_ge(chosen_t_ready, q)
                for t in range(TILES):
                    mm = pe.transpose(chosen_ps[:, t, :], chosen[q][:, 128 * t:128 * t + 128], ident[:, :])
                mm.then_inc(chosen_turned, 1)
                for i in range(GROUP):
                    b = q * GROUP + i
                    if b + 1 < BATCH:
                        turn_tokens(b + 1)
                    if i == 0:
                        pe.wait_ge(chosen_t_ready, q + 1)
                    pe.wait_ge(normed_t_ready, b + 1)
                    if b:
                        pe.wait_ge(pooled_ready, b)
                    for t in range(TILES):
                        mm = pe.matmul(pooled_ps[:, 0:EXPERTS], normed_t[b % 2][:, t, :],
                                       chosen_t[:, t, EXPERTS * i:EXPERTS * i + EXPERTS],
                                       start=(t == 0), stop=(t == TILES - 1))
                    mm.then_inc(pooled_summed, 1)
            pe.wait_ge(weights_in, 4 * DMA)
            pe.wait_ge(ones_set, 2)
            pe.wait_ge(pooled_ready, BATCH)
            for e in range(EXPERTS):
                for h in range(2):
                    at = (e % 16 * 2 + h) * BATCH
                    mm = pe.matmul(work_ps[:, e // 16, at:at + BATCH], w1[:, e, 128 * h:128 * h + 128],
                                   pooled[:, :, e], start=True, stop=True)
                if e % 16 == 15:
                    mm.then_inc(hidden_summed, 1)
            for e in range(EXPERTS):
                if e % 16 == 0:
                    pe.wait_ge(hidden_ready, 2)
                out = work_ps[0:BATCH, e // 8, e % 8 * CH:e % 8 * CH + CH]
                for h in range(2):
                    pe.matmul(out, hidden[:, e, h, :], w2[:, h, e, :], start=(h == 0), stop=False)
                mm = pe.matmul(out, ones[:, :], w2_bias[:, e, :], start=False, stop=True)
                if e % 8 == 7:
                    mm.then_inc(results_summed, 1)
            pe.wait_ge(spread_in, GROUP * DMA)
            pe.wait_ge(results_ready, 4)
            for n in range(PIECES):
                j, c = n // CHUNKS, n % CHUNKS
                first = 2 * j % GROUP
                if n >= 4:
                    pe.wait_ge(final_ready, n - 3)
                pe.matmul(work_ps[:, n % 4, :], spread[:, 2 * j // GROUP, first:first + 2, :].rearrange("p i c -> p (i c)"),
                          chosen[2 * j // GROUP][:, BANK * c:BANK * c + BANK], start=True, stop=True).then_inc(scattered, 1)

        @block.scalar
        def _(act):
            def exponential(q):
                act.wait_ge(minus_ready, q + 1)
                if q >= 2:
                    act.wait_ge(chosen_ready, q - 1)
                act.activation(probs[q % 2][:, :], logits[q % 2][:, :], ACT.Exp, bias=minus[:, q:q + 1],
                               accum_out=total[:, q:q + 1]).then_inc(exp_ready, 1)

            for q in range(2):
                exponential(q)
            for q in range(QUADS):
                act.wait_ge(chosen_turned, q + 1)
                if q:
                    act.wait_ge(pooled_summed, GROUP * q)
                act.copy(chosen_t[:, 0:4, :], chosen_ps[:, 0:4, :])
                act.copy(chosen_t[:, 4:8, :], chosen_ps[:, 4:8, :]).then_inc(chosen_t_ready, 1)
                for i in range(GROUP):
                    b = q * GROUP + i
                    act.wait_ge(normed_turned, b + 1)
                    if b >= 2:
                        act.wait_ge(pooled_summed, b - 1)
                    act.copy(normed_t[b % 2][:, :, :], turned_ps[b % 2]).then_inc(normed_t_ready, 1)
                if q + 2 < QUADS:
                    exponential(q + 2)
            for h in range(2):
                act.wait_ge(hidden_summed, h + 1)
                act.activation(hidden[:, 16 * h:16 * h + 16, :, :].rearrange("p e h b -> p (e h b)"),
                               work_ps[:, h, :], ACT.Gelu).then_inc(hidden_ready, 1)

        @block.gpsimd
        def _(pool):
            pool.memset(ones[:, :], 1.0).then_inc(ones_set, 1)
            pool.memset(spread[:, :, :, :], 0.0).then_inc(spread_zeroed, 1)

        @block.vector
        def _(dve):
            def top(q):
                dve.wait_ge(logits_in[q % 2], (q // 2 + 1) * DMA)
                dve.max(tops[:, q, :], logits[q % 2][:, :]).then_inc(top_ready, 1)
                dve.wait_ge(top_ready, q + 1)
                dve.tensor_scalar(minus[:, q:q + 1], tops[:, q, 0:1], -1.0, None, ALU.mult).then_inc(minus_ready, 1)

            def choose(q):
                dve.wait_ge(exp_ready, q + 1)
                dve.reciprocal(share[:, q:q + 1], total[:, q:q + 1]).then_inc(share_ready, 1)
                dve.wait_ge(share_ready, q + 1)
                dve.tensor_scalar(probs[q % 2][:, :], probs[q % 2][:, :], share[:, q:q + 1], None,
                                  ALU.mult).then_inc(probs_ready, 1)
                dve.wait_ge(probs_ready, q + 1)
                dve.max(best[:, q, :], probs[q % 2][:, :]).then_inc(best_ready, 1)
                dve.wait_ge(best_ready, q + 1)
                dve.match_replace(out=marked[q % 2][:, :], in_to_replace=best[:, q, :], in_values=probs[q % 2][:, :],
                                  imm_value=-1.0).then_inc(marked_ready, 1)
                dve.wait_ge(marked_ready, q + 1)
                dve.scalar_tensor_tensor(out=chosen[q][:, :], in0=marked[q % 2][:, :], scalar=-1.0,
                                         in1=probs[q % 2][:, :], op0=ALU.is_equal, op1=ALU.mult
                                         ).then_inc(chosen_ready, 1)

            dve.memset(pooled[CH:ROWS1, :, :], 1.0).then_inc(ones_set, 1)
            top(0)
            top(1)
            choose(0)
            for q in range(QUADS):
                if q + 1 < QUADS:
                    choose(q + 1)
                if q + 2 < QUADS:
                    top(q + 2)
                for i in range(GROUP):
                    b = q * GROUP + i
                    dve.wait_ge(pooled_summed, b + 1)
                    dve.tensor_copy(pooled[0:CH, b, :], pooled_ps[:, 0:EXPERTS]).then_inc(pooled_ready, 1)
            for h in range(4):
                dve.wait_ge(results_summed, h + 1)
                dve.tensor_copy(results[:, 8 * h:8 * h + 8, :].rearrange("p e o -> p (e o)"),
                                work_ps[0:BATCH, h, :]).then_inc(results_ready, 1)
            dve.wait_ge(x2_in, DUOS * DMA)
            for n in range(PIECES):
                piece = x2[n // CHUNKS][:, BANK * (n % CHUNKS):BANK * (n % CHUNKS) + BANK]
                dve.wait_ge(scattered, n + 1)
                dve.tensor_tensor(piece, work_ps[:, n % 4, :], piece, ALU.add).then_inc(final_ready, 1)


def kernel(**inputs):
    import numpy as np
    from ml_dtypes import bfloat16
    import concourse.bacc as bacc
    from concourse.bass_utils import run_bass_kernel_spmd

    x = np.asarray(inputs["x"])
    f32 = np.float32
    arrays = {"x_pad": np.pad(x, ((0, 0), (0, 0), (0, 0), (0, PITCH - SIDE))).reshape(BATCH, CH, IMG)}
    i2s = np.asarray(inputs["L0_conv_w_i2s"])
    skip = np.asarray(inputs["L0_conv_w_skip"])
    for side in ("left", "right"):
        w = np.asarray(inputs[f"L0_conv_w_{side}"])
        arrays[f"w_{side}"] = np.concatenate([w[:, :, 0].T, w[:, :, 1].T, i2s.T], 0)
        arrays[f"bias_{side}"] = np.tile(np.asarray(inputs[f"L0_conv_b_{side}"]).reshape(4, FEAT).T, (GROUP, 1))
        rows = np.zeros((128, CH), f32)
        at = FEAT if side == "left" else 0
        rows[at:at + FEAT] = skip.T
        arrays[f"w_skip_{side}"] = rows
    arrays["b_skip"] = np.asarray(inputs["L0_conv_b_skip"]).reshape(CH, 1)
    for name in ("W_delta", "W_B", "W_C", "W_out"):
        arrays[name] = np.asarray(inputs[f"L1_attn_{name}"])
    w_in = np.asarray(inputs["L1_attn_W_in"])
    arrays["W_in"] = np.stack([np.pad(w_in, ((CH * c, CH * (CHUNKS - 1 - c)), (0, 0))) for c in range(CHUNKS)])
    arrays["A_t"] = np.asarray(inputs["L1_attn_A"]).T
    gate_w = np.asarray(inputs["L1_ffn_gate_w"]).T
    arrays["gate_w"] = np.stack([np.pad(gate_w, ((CH * c, CH * (CHUNKS - 1 - c)), (0, 0))) for c in range(CHUNKS)], 1)
    arrays["gate_b"] = np.tile(np.asarray(inputs["L1_ffn_gate_b"]), CHUNKS).reshape(CHUNKS * EXPERTS, 1)
    arrays["weight1"] = np.asarray(inputs["L1_ffn_weight1"])
    arrays["weight2"] = np.asarray(inputs["L1_ffn_weight2"])
    arrays["mean_w"] = np.kron(np.eye(2, dtype=f32), np.full((CH, CH), 1.0 / CH, f32))
    arrays["identity"] = np.eye(128, dtype=f32)
    arrays["selectors"] = np.pad(
        np.tile(np.eye(WIDTH, dtype=f32)[:, :, None], (SPLITS, 1, STATE)),
        ((0, 128 - SPLITS * WIDTH), (0, 0), (0, 0))).astype(bfloat16)
    arrays = {k: np.ascontiguousarray(v) for k, v in arrays.items()}

    nc = bacc.Bacc("TRN2", target_bir_lowering=False, num_devices=1)
    a = {k: nc.dram_tensor(k, v.shape, mybir.dt.from_np(v.dtype), kind="ExternalInput").ap()
         for k, v in arrays.items()}
    out = nc.dram_tensor("out", (BATCH, CH, LEN), F32, kind="ExternalOutput").ap()

    def scratch(name, shape, dt=F32):
        return nc.dram_tensor(name, shape, dt, kind="Internal").ap()

    x1 = scratch("x1_dram", (BATCH, CH, LEN))
    delta = scratch("delta_dram", (PAIRS, SPLITS, INNER, BANK), BF16)
    entering = scratch("input_dram", (PAIRS, STATE, BANK))
    readout = scratch("readout_dram", (PAIRS, STATE, BANK))
    z = scratch("z_dram", (PAIRS, INNER, BANK))
    y = scratch("y_dram", (PAIRS + 1, 4 * FOLD, WIDTH * INNER))
    x2 = scratch("x2_dram", (BATCH, CH, LEN))
    normed = scratch("normed_dram", (BATCH, CH, LEN))
    logits = scratch("logit_dram", (BATCH, EXPERTS, LEN))
    experts = scratch("expert_dram", (BATCH, EXPERTS, CH))

    conv_phase(nc, a["x_pad"], a["w_left"], a["w_right"], a["bias_left"], a["bias_right"],
               a["w_skip_left"], a["w_skip_right"], a["b_skip"], x1)
    project_phase(nc, x1, a["W_in"], a["W_delta"], a["W_B"], a["W_C"], a["mean_w"], delta, entering, readout, z)
    scan_phase(nc, delta, entering, readout, a["A_t"], a["selectors"], y)
    gate_phase(nc, y, z, x1, a["W_out"], a["mean_w"], a["identity"], a["gate_w"], a["gate_b"], x2, normed, logits)
    expert_phase(nc, logits, normed, x2, a["identity"], a["weight1"], a["weight2"], experts, out)

    r = run_bass_kernel_spmd(nc, [arrays], core_ids=[0])
    return r.results[0]["out"].reshape(BATCH, CH, SIDE, SIDE)
```
